# Optimizing a Trainium2 kernel written in Bass

```python
import numpy as np
import jax
import jax.numpy as jnp

def _softmax(x, axis=-1):
    return jax.nn.softmax(x, axis=axis)

def _gelu(x):
    return jax.nn.gelu(x, approximate=True)

def _silu(x):
    return jax.nn.silu(x)

def _sigmoid(x):
    return jax.nn.sigmoid(x)

def _layernorm(x, axis=-1, eps=1e-05):
    m = jnp.mean(x, axis=axis, keepdims=True)
    v = jnp.var(x, axis=axis, keepdims=True)
    return (x - m) / jnp.sqrt(v + eps)

def _scatter_add(tgt, idx, src, axis=0):
    return tgt.at[idx].add(src)

def _segment_sum(src, seg, n):
    return jax.ops.segment_sum(src, seg, n)
kernel_name = 'mk_gnn_resnorm_d2_gnn_r32_97d25c'

def setup_inputs(seed: int=0):
    np.random.seed(seed)
    _w = jnp.asarray

    def _rec_inputs():
        import jax
        import jax.numpy as jnp
        _gk = jax.random.key(seed)
        x = -0.0002117 + 1 * jax.random.normal(jax.random.fold_in(_gk, 1), (3125, 256), jnp.float32)
        src = jax.random.randint(jax.random.fold_in(_gk, 2), (50000,), 0, 3125, jnp.int32)
        dst = jax.random.randint(jax.random.fold_in(_gk, 3), (50000,), 0, 3125, jnp.int32)
        _o = jnp.argsort(dst, stable=True)
        src = src[_o]
        dst = dst[_o]
        edge_weight = jax.random.uniform(jax.random.fold_in(_gk, 13), (50000,), jnp.float32, 0.0, 1)
        return (x, src, dst, edge_weight)
    x, src, dst, edge_weight = _rec_inputs()

    def _L0_gnn_setup():
        import jax, jax.numpy as jnp
        import numpy as np
        N = 3125
        E = 100000
        F_IN = 256
        F_OUT = 256
        key = jax.random.key(seed)
        k1, k2, k3, k4, k5 = jax.random.split(key, 5)
        x = jax.random.normal(k1, (N, F_IN), dtype=jnp.float32)
        edge_row = jax.random.randint(k2, (E,), 0, N, dtype=jnp.int32)
        edge_col = jax.random.randint(k3, (E,), 0, N, dtype=jnp.int32)
        edge_val = jax.random.uniform(k4, (E,), dtype=jnp.float32)
        W = jax.random.normal(k5, (2 * F_IN, F_OUT), dtype=jnp.float32) * (1.0 / np.sqrt(2 * F_IN))
        b = jnp.zeros((F_OUT,), dtype=jnp.float32)
        return {'x': x, 'edge_row': edge_row, 'edge_col': edge_col, 'edge_val': edge_val, 'W': W, 'b': b}
    _L0_gnn_all = _L0_gnn_setup()
    _L0_gnn_in = {k: v for k, v in _L0_gnn_all.items() if k in ('W', 'b')}
    del _L0_gnn_all

    def _L1_gnn_setup():
        import jax, jax.numpy as jnp
        import numpy as np
        N = 50000
        D = 256
        H = 8
        C = D // H
        E = 12500
        NEG_SLOPE = 0.2

        def _gatv2_layer(x, src, dst, Wl, Wr, att, b):
            n = x.shape[0]
            xl = (x @ Wl).reshape(n, H, C)
            xr = (x @ Wr).reshape(n, H, C)
            e = jax.nn.leaky_relu(xl[src] + xr[dst], NEG_SLOPE)
            score = jnp.einsum('ehc,hc->eh', e, att)
            smax = jax.ops.segment_max(score, dst, num_segments=n)
            ex = jnp.exp(score - smax[dst])
            denom = jax.ops.segment_sum(ex, dst, num_segments=n)
            alpha = ex / jnp.maximum(denom[dst], 1e-16)
            out = jax.ops.segment_sum(alpha[:, :, None] * xl[src], dst, num_segments=n)
            return out.reshape(n, H * C) + b
        key = jax.random.key(seed)
        ks = jax.random.split(key, 12)
        inp = {'edge_index': jax.random.randint(ks[0], (2, E), 0, N, dtype=jnp.int64) if jax.config.jax_enable_x64 else jax.random.randint(ks[0], (2, E), 0, N), 'node_embedding': jax.random.normal(ks[1], (N, D), jnp.float32) * 0.1}
        for i in range(2):
            inp[f'Wl{i}'] = jax.random.normal(ks[2 + 4 * i], (D, D), jnp.float32) / np.sqrt(D).astype(np.float32)
            inp[f'Wr{i}'] = jax.random.normal(ks[3 + 4 * i], (D, D), jnp.float32) / np.sqrt(D).astype(np.float32)
            inp[f'att{i}'] = jax.random.normal(ks[4 + 4 * i], (H, C), jnp.float32) / np.sqrt(C).astype(np.float32)
            inp[f'b{i}'] = jnp.zeros((D,), jnp.float32)
        return inp
    _L1_gnn_all = _L1_gnn_setup()
    _L1_gnn_in = {k: v for k, v in _L1_gnn_all.items() if k in ('Wl0', 'Wr0', 'att0', 'b0', 'Wl1', 'Wr1', 'att1', 'b1')}
    del _L1_gnn_all
    return {'x': x, 'src': src, 'dst': dst, 'edge_weight': edge_weight, 'L0_gnn_W': _L0_gnn_in['W'], 'L0_gnn_b': _L0_gnn_in['b'], 'L1_gnn_Wl0': _L1_gnn_in['Wl0'], 'L1_gnn_Wr0': _L1_gnn_in['Wr0'], 'L1_gnn_att0': _L1_gnn_in['att0'], 'L1_gnn_b0': _L1_gnn_in['b0'], 'L1_gnn_Wl1': _L1_gnn_in['Wl1'], 'L1_gnn_Wr1': _L1_gnn_in['Wr1'], 'L1_gnn_att1': _L1_gnn_in['att1'], 'L1_gnn_b1': _L1_gnn_in['b1']}

def reference(x, src, dst, edge_weight, L0_gnn_W, L0_gnn_b, L1_gnn_Wl0, L1_gnn_Wr0, L1_gnn_att0, L1_gnn_b0, L1_gnn_Wl1, L1_gnn_Wr1, L1_gnn_att1, L1_gnn_b1):
    import jax
    import jax.numpy as jnp

    def _L0_gnn_ref(x, edge_row, edge_col, edge_val, W, b):
        import jax, jax.numpy as jnp
        import numpy as np
        N = 3125
        E = 100000
        F_IN = 256
        F_OUT = 256
        gathered = edge_val[:, None] * x[edge_col]
        support = jax.ops.segment_sum(gathered, edge_row, num_segments=N)
        h = jnp.concatenate([x, support], axis=1)
        out = h @ W + b
        return jax.nn.relu(out)

    def _L1_gnn_ref(edge_index, node_embedding, Wl0, Wr0, att0, b0, Wl1, Wr1, att1, b1):
        import jax, jax.numpy as jnp
        import numpy as np
        N = 50000
        D = 256
        H = 8
        C = D // H
        E = 12500
        NEG_SLOPE = 0.2

        def _gatv2_layer(x, src, dst, Wl, Wr, att, b):
            n = x.shape[0]
            xl = (x @ Wl).reshape(n, H, C)
            xr = (x @ Wr).reshape(n, H, C)
            e = jax.nn.leaky_relu(xl[src] + xr[dst], NEG_SLOPE)
            score = jnp.einsum('ehc,hc->eh', e, att)
            smax = jax.ops.segment_max(score, dst, num_segments=n)
            ex = jnp.exp(score - smax[dst])
            denom = jax.ops.segment_sum(ex, dst, num_segments=n)
            alpha = ex / jnp.maximum(denom[dst], 1e-16)
            out = jax.ops.segment_sum(alpha[:, :, None] * xl[src], dst, num_segments=n)
            return out.reshape(n, H * C) + b
        n = node_embedding.shape[0]
        loops = jnp.arange(n, dtype=edge_index.dtype)
        src = jnp.concatenate([edge_index[0], loops])
        dst = jnp.concatenate([edge_index[1], loops])
        x = node_embedding
        for Wl, Wr, att, b in ((Wl0, Wr0, att0, b0), (Wl1, Wr1, att1, b1)):
            tmp = _gatv2_layer(x, src, dst, Wl, Wr, att, b)
            x = x + jax.nn.gelu(tmp, approximate=False)
        return x
    edge_index = jnp.stack([src, dst])
    x = _layernorm(x + _L0_gnn_ref(x, src, dst, edge_weight, L0_gnn_W, L0_gnn_b), axis=-1)
    x = _layernorm(x + _L1_gnn_ref(edge_index, x, L1_gnn_Wl0, L1_gnn_Wr0, L1_gnn_att0, L1_gnn_b0, L1_gnn_Wl1, L1_gnn_Wr1, L1_gnn_att1, L1_gnn_b1), axis=-1)
    return x

_drawn_inputs = setup_inputs


def setup_inputs(seed=0):
    import zlib

    import numpy as np

    out = dict(_drawn_inputs(seed))
    spreads = {'L0_gnn_b': (0.0, 0.1), 'L1_gnn_b0': (0.0, 0.1), 'L1_gnn_b1': (0.0, 0.304)}
    factors = {}
    for name, (base, spread) in spreads.items():
        noise = np.random.default_rng([zlib.crc32(name.encode()), seed]).standard_normal(out[name].shape)
        drawn = base * np.exp(spread * noise) if base else spread * noise
        out[name] = jnp.asarray(drawn.astype(out[name].dtype))
    for name, factor in factors.items():
        out[name] = (out[name] * factor).astype(out[name].dtype)
    return out
```

```python
import concourse.bass as bass
from concourse import mybir
from contextlib import ExitStack

FP32 = mybir.dt.float32
BF16 = mybir.dt.bfloat16
I32 = mybir.dt.int32
ALU = mybir.AluOpType
ACT = mybir.ActivationFunctionType
AX = mybir.AxisListType.X

P = 128
N, D, H, E = 3125, 256, 8, 50000
C = D // H
NT = -(-N // P)
NP = NT * P
TAIL = N - (NT - 1) * P
NB = -(-E // P)
EB = NB + 1
EP = EB * P
CHUNKS = P // H
NI = -(-(NB + NT - 1) // CHUNKS) * CHUNKS
RUN = NI // CHUNKS
G = 4
NG = NI // G
IR = NI // G
NJ = NT - 1
XW = D + H
RW = D + 2 * H
UW = D + 1
BIG = 1.0e30
NO_EDGE_DST = float(NP + 800)
SKIP = 60000.0
SLOPE = 0.2
EPS = 1e-5
LAST_EDGES = E - (P - 1) * EB


class Chain:

    def __init__(self, eng, sem, base=0):
        self.eng, self.sem, self.n = eng, sem, base

    def __call__(self, ins):
        self.n += 1
        ins.then_inc(self.sem, 1)
        self.eng.wait_ge(self.sem, self.n)


def back(it, par, k, ways):
    return (par - k) % ways, it + (par - k) // ways


def build(nc, x, src, dst, edge_weight, W0, b0, gat, out):
    top = ExitStack()

    def sb(name, shape, dt):
        return top.enter_context(nc.sbuf_tensor(name, shape, dt))

    def dram(name, shape, dt):
        return nc.dram_tensor(name, shape, dt)

    stage_no = [0]

    def stage():
        stage_no[0] += 1
        k = stage_no[0]
        ctx = ExitStack()
        sems = []

        def clear():
            nc.clear_and_free_semaphores(sems)
            nc.all_engine_barrier()

        ctx.callback(clear)

        def sem(name):
            sems.append(nc.alloc_semaphore(name=f"s{k}_{name}"))
            return sems[-1]

        ps = lambda name, shape: ctx.enter_context(nc.psum_tensor(f"p{k}_{name}", shape, FP32))
        return ctx, sem, ps

    with top:
        src_d = dram("src_sorted", [EB, P], FP32)
        dst_d = dram("dst_sorted", [EB, P], FP32)
        prev_d = dram("prev_dst", [EB, P], FP32)
        pos_d = dram("position", [EB, P], FP32)
        w_d = dram("weight", [EB, P], FP32)
        step_d = dram("step_tables", [3, NI], I32)
        loc_d = dram("local_rows", [NI, P], BF16)
        sup_d = dram("rows_by_src", [EP, UW], FP32)
        tab_d = dram("gather_table", [NP, XW], FP32)
        spill_d = dram("gathered", [NG, P, G * XW], FP32)
        sum_d = dram("chunk_summary", [P, 5], FP32)
        carry_d = dram("chunk_carry", [2, P], FP32)

        iota_row = sb("iota_row", [P, P], FP32)
        iota_p = sb("iota_p", [P, 1], FP32)
        ident = sb("ident", [P, P], FP32)
        before = sb("before", [P, P], FP32)
        ones = sb("ones", [P, P], FP32)
        step_no = sb("step_no", [P, G], FP32)
        tile_no = sb("tile_no", [P, NT], FP32)

        X = sb("X", [P, NT * D], FP32)
        Xv = X[:, :].rearrange("p (t d) -> p t d", d=D)
        gath = sb("gath", [P, 4 * G * XW], FP32)
        GATH = gath[:, :].rearrange("p (s g w) -> p s g w", s=4, g=G)
        node = sb("node", [P, 3 * NT * RW // 2], FP32)
        PARTS = node[:, :].bitcast(BF16).rearrange("p (k t w) -> p k t w", k=3, t=NT)
        ACC = node[:, 0:NT * RW].rearrange("p (t w) -> p t w", t=NT)
        SUP = node[:, 0:NT * D].rearrange("p (t d) -> p t d", t=NT)
        LOC = sb("LOC", [P, NI], FP32)
        WGT = sb("WGT", [P, NI], FP32)
        RESET = sb("RESET", [P, NI], FP32)
        MASK = sb("MASK", [P, NI], FP32)
        START = sb("START", [P, NI], FP32)
        SRCI = sb("SRCI", [P, NI], I32)
        POSI = sb("POSI", [P, NI], I32)
        JROW = sb("JROW", [1, 3 * NI], I32)
        TILE0 = sb("TILE0", [P, NI], FP32)
        arena = sb("arena", [P, 5 * NI * H + 8], FP32)
        SC = arena[:, 0:NI * H]
        SELF = arena[:, NI * H:2 * NI * H]
        RST = arena[:, 2 * NI * H:3 * NI * H + 1]
        EX = arena[:, 3 * NI * H + 8:5 * NI * H + 8]
        D1 = EX[:, 0:NI * H]
        FW = EX[:, NI * H:2 * NI * H]
        LBC = sb("LBC", [P, 2, G * P], BF16)
        OHT = sb("OHT", [P, 2, G * P], BF16)
        OH = sb("OH", [P, 2, G, P], FP32)
        work = sb("work", [P, 4 * G * XW], FP32)
        Z = work[:, 0:2 * G * XW].rearrange("p (s w) -> p s w", s=2)
        T = work[:, 2 * G * XW:].rearrange("p (s w) -> p s w", s=2)
        GIDX = sb("GIDX", [P, 4, G], I32)

        ctx, sem, ps = stage()
        with ctx:
            M = node[:, 0:NT * EB]
            CUM = arena[:, 0:NT * EB]
            tmp_w = work
            SIi = tmp_w[:, 0:EB].bitcast(I32)
            DIi = tmp_w[:, EB:2 * EB].bitcast(I32)
            WL = tmp_w[:, 2 * EB:3 * EB]
            SF = tmp_w[:, 3 * EB:4 * EB]
            DF = tmp_w[:, 4 * EB:5 * EB]
            PV = tmp_w[:, 5 * EB:6 * EB]
            BK = tmp_w[:, 6 * EB:7 * EB]
            POS = tmp_w[:, 7 * EB:8 * EB]
            JUNK = tmp_w[:, 8 * EB:9 * EB]
            small = ctx.enter_context(nc.sbuf_tensor("prep_small", [P, 400], FP32))
            PC = small[:, 0:1].bitcast(I32)
            RT = small[:, 8:8 + NT]
            CD = small[:, 40:40 + NT + NJ]
            OFF = small[:, 96:96 + NT]
            BI = small[:, 128:128 + 2 * NJ].bitcast(I32)
            BI2 = small[:, 176:176 + 2 * NJ].bitcast(I32)
            BND = small[:, 224:224 + 2 * NJ]
            JC = small[:, 280:280 + 3 * G]
            JI = small[:, 296:296 + 3 * G].bitcast(I32)
            BIX = small[:, 312:312 + G].bitcast(I32)
            BF = small[:, 320:320 + G]
            J128 = small[:, 328:328 + G]
            rows = arena[:, NT * EB:NT * EB + 10 * G * P].rearrange("p (k g q) -> p k g q", k=10, g=G)
            PS, PD, PP, PW, PV2, VAL, ST, RS, MK, LC = [rows[0:IR, k] for k in range(10)]
            LB16 = ctx.enter_context(nc.sbuf_tensor("loc16", [P, G, P], BF16))
            TI = TILE0[:, :].bitcast(I32)
            psum_off = ps("off", [P, 512])
            psum_bnd = ps("bnd", [P, 512])
            psum_tr = [ps(f"tr{k}", [P, 512]) for k in range(4)]

            pad_set, loaded, x_loaded = sem("pad_set"), sem("loaded"), sem("x_loaded")
            consts, chain = sem("consts"), sem("chain")
            edges_ready, edges_stored = sem("edges_ready"), sem("edges_stored")
            counts_ready, sums_ready = sem("counts_ready"), sem("sums_ready")
            steps_ready, steps_stored, steps_back = sem("steps_ready"), sem("steps_stored"), sem("steps_back")
            rows_in, rows_ready = sem("rows_in"), sem("rows_ready")
            loc_stored, trans, evac = sem("loc_stored"), sem("trans"), sem("evac")
            with nc.Block() as block:

                @block.sync
                def _(sp):
                    sp.wait_ge(pad_set, 1)
                    for tile, flat in ((SIi, src), (DIi, dst), (WL, edge_weight)):
                        sp.dma_start(tile[0:P - 1, :], flat[0:(P - 1) * EB].rearrange("(p c) -> p c", c=EB)).then_inc(loaded, 16)
                        sp.dma_start(tile[P - 1:P, 0:LAST_EDGES],
                                     flat[(P - 1) * EB:E].rearrange("(a c) -> a c", a=1)).then_inc(loaded, 16)
                    sp.dma_start(PC[1:P, :], dst[0:(P - 1) * EB].rearrange("(p c) -> p c", c=EB)[:, EB - 1:EB],
                                 allow_slow_non_contiguous=True).then_inc(loaded, 16)
                    sp.dma_start(Xv[:, 0:NT - 1, :], x[0:(NT - 1) * P, :].rearrange("(t p) d -> p t d", p=P)).then_inc(x_loaded, 16)
                    sp.dma_start(Xv[0:TAIL, NT - 1, :], x[(NT - 1) * P:N, :]).then_inc(x_loaded, 16)
                    sp.wait_ge(edges_ready, 1)
                    for arr, flat in ((SF, src_d), (DF, dst_d), (PV, prev_d), (WL, w_d)):
                        sp.dma_start(flat[:, :].rearrange("b q -> (b q)").rearrange("(p c) -> p c", c=EB), arr).then_inc(edges_stored, 16)
                    sp.dma_start(sup_d[E:E + P, :], arena[:, 0:UW]).then_inc(edges_stored, 16)
                    sp.dma_start(sup_d[E + P:EP, :], arena[0:EP - E - P, 0:UW]).then_inc(edges_stored, 16)
                    sp.wait_ge(edges_ready, 2)
                    sp.dma_start(pos_d[:, :].rearrange("b q -> (b q)").rearrange("(p c) -> p c", c=EB), POS).then_inc(edges_stored, 16)
                    sp.wait_ge(steps_ready, 1)
                    for k in range(3):
                        sp.dma_start(step_d[k, :].rearrange("(g p) -> p g", p=IR), JI[0:IR, k * G:k * G + G],
                                     allow_slow_non_contiguous=True).then_inc(steps_stored, 16)
                    sp.wait_ge(steps_stored, 48)
                    sp.dma_start(JROW[0:1, :], step_d[:, :].rearrange("k i -> (k i)").rearrange("(a i) -> a i", a=1)).then_inc(steps_back, 16)
                    sp.dma_start(TI, step_d[1:2, :].broadcast_to([P, NI])).then_inc(steps_back, 16)
                    sp.wait_ge(rows_ready, 1)
                    sp.dma_start(loc_d[:, :].rearrange("(g p) q -> p g q", p=IR), LB16[0:IR, :, :]).then_inc(loc_stored, 16)
                    sp.wait_ge(loc_stored, 16)
                    sp.wait_ge(steps_back, 32)

                @block.gpsimd
                def _(pool):
                    IMP = dict(allow_small_or_imprecise_dtypes=True)
                    pool.iota(tile_no[:, :], pattern=[[1, NT]], base=0, channel_multiplier=0, **IMP).then_inc(consts, 1)
                    pool.memset(ones[:, :], 1.0).then_inc(consts, 1)
                    pool.memset(ident[:, :], 0.0).then_inc(consts, 1)
                    pool.memset(before[:, :], 0.0).then_inc(consts, 1)
                    pool.iota(iota_row[:, :], pattern=[[1, P]], base=0, channel_multiplier=0, **IMP).then_inc(consts, 1)
                    pool.iota(iota_p[:, :], pattern=[[0, 1]], base=0, channel_multiplier=1, **IMP).then_inc(consts, 1)
                    pool.iota(step_no[:, :], pattern=[[IR, G]], base=0, channel_multiplier=1, **IMP).then_inc(consts, 1)
                    pool.wait_ge(consts, 7)
                    pool.affine_select(out=ident[:, :], in_=ident[:, :], compare_op=ALU.not_equal, fill=1.0, base=0,
                                       pattern=[[-1, P]], channel_multiplier=1).then_inc(consts, 1)
                    pool.affine_select(out=before[:, :], in_=before[:, :], compare_op=ALU.is_ge, fill=1.0, base=0,
                                       pattern=[[-1, P]], channel_multiplier=1).then_inc(consts, 1)
                    pool.wait_ge(edges_stored, 7 * 16)
                    pool.wait_ge(steps_ready, 2)
                    pool.nop(nofuse=True)
                    for row, flat in ((PS, src_d), (PD, dst_d), (PV2, prev_d), (PW, w_d), (PP, pos_d)):
                        for g in range(G):
                            pool.indirect_dma_start(row[:, g, :], None, flat[:, :],
                                                    bass.IndirectOffsetOnAxis(BIX[0:IR, g:g + 1], 0)).then_inc(rows_in, 16)

                @block.vector
                def _(dve):
                    link = Chain(dve, chain)
                    dve.memset(DIi, int(NO_EDGE_DST))
                    dve.memset(SIi, NP)
                    dve.memset(PC, -1)
                    dve.memset(CD, 0.0)
                    dve.memset(arena[:, 0:UW], 0.0)
                    link(dve.memset(WL, 0.0))
                    link(dve.memset(X[:, (NT - 1) * D:], 0.0))
                    dve.memset(RST[:, NI * H:], 0.0).then_inc(pad_set, 1)
                    dve.wait_ge(loaded, 7 * 16)
                    link(dve.tensor_copy(DF, DIi))
                    dve.tensor_copy(PV[:, 0:1], PC)
                    dve.tensor_copy(PV[:, 1:EB], DF[:, 0:EB - 1])
                    link(dve.tensor_copy(SF, SIi))
                    link(dve.tensor_scalar(DIi, SIi, 7, None, ALU.arith_shift_right))
                    dve.tensor_copy(BK, DIi).then_inc(edges_ready, 1)
                    dve.wait_ge(edges_ready, 1)
                    dve.wait_ge(consts, 9)
                    Mv = M.rearrange("p (k c) -> p k c", c=EB)
                    link(dve.tensor_tensor(Mv, BK.unsqueeze(1).broadcast_to([P, NT, EB]),
                                           tile_no[:, :].unsqueeze(2).broadcast_to([P, NT, EB]), ALU.is_equal))
                    dve.wait_ge(edges_stored, 6 * 16)
                    link(dve.tensor_tensor_scan(CUM, ones[:, 0:1].broadcast_to([P, NT * EB]), M, 0.0, ALU.mult, ALU.add))
                    CUMv = CUM.rearrange("p (k c) -> p k c", c=EB)
                    ends = CUMv[:, :, EB - 1]
                    link(dve.tensor_copy(CD[:, 1:NT], ends[:, 0:NT - 1]))
                    link(dve.tensor_tensor(RT, ends, CD[:, 0:NT], ALU.subtract))
                    for j in range(NJ):
                        link(dve.tensor_scalar(JUNK, DF, float(P * (j + 1)), 0.0, ALU.is_lt, ALU.add,
                                               accum_out=CD[:, NT + j:NT + j + 1]))
                    dve.tensor_copy(JUNK[:, 0:1], tile_no[:, 0:1]).then_inc(counts_ready, 1)
                    dve.wait_ge(counts_ready, 1)
                    dve.wait_ge(sums_ready, 1)
                    link(dve.scalar_tensor_tensor(OFF, psum_off[:, 0:NT], -1.0, CD[:, 0:NT], ALU.add, ALU.subtract))
                    for k in range(NT):
                        ins = dve.scalar_tensor_tensor(CUMv[:, k, :], CUMv[:, k, :], OFF[:, k:k + 1], Mv[:, k, :], ALU.add, ALU.mult)
                    link(ins)
                    dve.tensor_reduce(POS, CUM.rearrange("p (k c) -> p c k", c=EB), AX, ALU.add).then_inc(edges_ready, 1)
                    link(dve.tensor_copy(BI, psum_bnd[:, 0:2 * NJ]))
                    link(dve.tensor_scalar(BI2, BI, 7, None, ALU.arith_shift_right))
                    link(dve.tensor_copy(BND, BI2))
                    BNDv = BND.rearrange("p (w j) -> p w j", w=2)
                    link(dve.tensor_tensor(BNDv, BNDv, tile_no[:, 1:NT].unsqueeze(1).broadcast_to([P, 2, NJ]), ALU.add))
                    for w, which in ((0, 1), (1, 0)):
                        for g in range(G):
                            link(dve.tensor_scalar(JUNK[:, 0:NJ], BND[:, which * NJ:which * NJ + NJ], step_no[:, g:g + 1], 0.0,
                                                   ALU.is_le, ALU.add, accum_out=JC[:, w * G + g:w * G + g + 1]))
                    link(dve.tensor_tensor(JC[:, 2 * G:], step_no[:, :], JC[:, G:2 * G], ALU.subtract))
                    link(dve.tensor_copy(JI, JC))
                    dve.tensor_tensor(BF, step_no[:, :], JC[:, 0:G], ALU.subtract).then_inc(steps_ready, 1)
                    dve.wait_ge(steps_ready, 1)
                    dve.tensor_copy(BIX, BF).then_inc(steps_ready, 1)
                    link(dve.tensor_scalar(J128, JC[:, 0:G], float(P), None, ALU.mult))
                    dve.wait_ge(rows_in, 20 * 16)
                    for g in range(G):
                        ins = dve.tensor_scalar(LC[:, g, :], PD[:, g, :], J128[0:IR, g:g + 1], None, ALU.subtract)
                    link(ins)
                    link(dve.tensor_scalar(VAL, LC, 0.0, None, ALU.is_ge))
                    link(dve.scalar_tensor_tensor(VAL, LC, float(P), VAL, ALU.is_lt, ALU.mult))
                    link(dve.tensor_tensor(ST, PD, PV2, ALU.not_equal))
                    link(dve.tensor_tensor(ST, ST, VAL, ALU.mult))
                    dve.tensor_scalar(RS, ST, -BIG, None, ALU.mult)
                    dve.tensor_scalar(MK, VAL, -1.0, BIG, ALU.add, ALU.mult)
                    dve.tensor_scalar(PS, PS, float(NP - 1), None, ALU.min)
                    link(dve.scalar_tensor_tensor(PP, PP, -SKIP, VAL, ALU.add, ALU.mult))
                    link(dve.tensor_scalar(PP, PP, SKIP, None, ALU.add))
                    dve.tensor_copy(LB16[0:IR, :, :], LC).then_inc(rows_ready, 1)
                    dve.wait_ge(rows_ready, 1)
                    for k, col in enumerate((LOC, SRCI, POSI, WGT, RESET, MASK, START)):
                        dve.wait_ge(trans, k + 1)
                        dve.tensor_copy(col[:, :], psum_tr[k % 4][:, 0:NI]).then_inc(evac, 1)

                @block.tensor
                def _(pe):
                    pe.wait_ge(counts_ready, 1)
                    pe.matmul(psum_off[:, 0:NT], before[:, :], RT, start=True, stop=False)
                    pe.matmul(psum_off[:, 0:NT], ones[:, :], CD[:, 0:NT], start=False, stop=True)
                    pe.matmul(psum_bnd[:, 0:2 * NJ], ones[:, :], CD[:, 1:1 + 2 * NJ], start=True, stop=True).then_inc(sums_ready, 1)
                    pe.wait_ge(rows_ready, 1)
                    for k, row in enumerate((LC, PS, PP, PW, RS, MK, ST)):
                        if k >= 4:
                            pe.wait_ge(evac, k - 3)
                        for g in range(G):
                            ins = pe.transpose(psum_tr[k % 4][:, g * IR:(g + 1) * IR], row[:, g, :], ident[0:IR, 0:IR])
                        ins.then_inc(trans, 1)

            with nc.Block() as block:
                scan_tr, scan_ev, ch2 = sem("scan_tr"), sem("scan_ev"), sem("ch2")
                res, parts = sem("res"), sem("parts")
                RX = arena[:, 0:NI * H].rearrange("p (r k h) -> p r k h", r=RUN, k=CHUNKS)
                R1 = EX[:, 0:NT * D]
                R1v = R1.rearrange("p (t d) -> p t d", d=D)

                @block.tensor
                def _(pe):
                    pe.wait_ge(res, 1)
                    for r in range(RUN):
                        b = r // 4
                        if b >= 4 and r % 4 == 0:
                            pe.wait_ge(scan_ev, b - 3)
                        ins = pe.transpose(psum_tr[b % 4][:, (r % 4) * P:(r % 4 + 1) * P],
                                           arena[:, r * P:(r + 1) * P], ident[:, :])
                        if r % 4 == 3 or r == RUN - 1:
                            ins.then_inc(scan_tr, 1)

                @block.vector
                def _(dve):
                    link = Chain(dve, ch2)
                    link(dve.tensor_copy(T[:, 0, 0:NI], TI))
                    link(dve.tensor_scalar(TILE0[:, :], T[:, 0, 0:NI], float(P), None, ALU.mult))
                    dve.tensor_copy(RX, RESET[:, :].rearrange("p (k r) -> p r k", k=CHUNKS).unsqueeze(3).broadcast_to([P, RUN, CHUNKS, H])).then_inc(res, 1)
                    for b in range(-(-RUN // 4)):
                        n = min(4, RUN - 4 * b) * P
                        dve.wait_ge(scan_tr, b + 1)
                        dve.tensor_copy(RST[:, b * 4 * P:b * 4 * P + n], psum_tr[b % 4][:, 0:n]).then_inc(scan_ev, 1)

                @block.gpsimd
                def _(pool):
                    pool.wait_ge(parts, 1)
                    pool.tensor_tensor(R1v, Xv, PARTS[:, 0, :, 0:D], ALU.subtract).then_inc(parts, 1)
                    pool.wait_ge(parts, 3)
                    pool.tensor_tensor(R1v, R1v, PARTS[:, 1, :, 0:D], ALU.subtract).then_inc(parts, 1)

                @block.scalar
                def _(act):
                    act.wait_ge(x_loaded, 32)
                    act.activation(PARTS[:, 0, :, 0:D], Xv, ACT.Copy).then_inc(parts, 1)
                    act.wait_ge(parts, 2)
                    act.activation(PARTS[:, 1, :, 0:D], R1v, ACT.Copy).then_inc(parts, 1)
                    act.wait_ge(parts, 4)
                    act.activation(PARTS[:, 2, :, 0:D], R1v, ACT.Copy)

        ctx, sem, ps = stage()
        with ctx:
            U = gath[:, 0:2 * G * UW].rearrange("p (s g w) -> p s g w", s=2, g=G)
            expd = [ps(f"expd{k}", [P, 2, 512]) for k in range(2)]
            loc_in = [sem(f"loc_in{k}") for k in range(2)]
            hot_ready, exp_ready, u_ready, idx_ready = sem("hot_ready"), sem("exp_ready"), sem("u_ready"), sem("idx_ready")
            src_ready = sem("src_ready")
            scattered = [sem(f"scattered{k}") for k in range(2)]
            turns = NG // 2
            with nc.Block() as block:

                def both(eng, body):
                    body(0)
                    with eng.Fori(1, turns) as it:
                        body(it)

                @block.sync
                def _(sp):
                    def body(it):
                        for s in range(2):
                            q = 2 * it + s
                            if it is not 0:
                                sp.wait_ge(hot_ready, q - 1)
                            sp.dma_start(LBC[:, s, :], loc_d[bass.ds(G * q, G), :].rearrange("g q -> (g q)").rearrange("(a n) -> a n", a=1)
                                         .broadcast_to([P, G * P])).then_inc(loc_in[s], 16)
                    both(sp, body)

                @block.vector
                def _(dve):
                    def body(it):
                        for s in range(2):
                            q = 2 * it + s
                            dve.wait_ge(loc_in[s], 16 * (it + 1))
                            if it is not 0:
                                dve.wait_ge(exp_ready, q - 1)
                            dve.tensor_scalar(OHT[:, s, :], LBC[:, s, :], iota_p[:, 0:1], None, ALU.is_equal).then_inc(hot_ready, 1)
                            if it is not 0:
                                dve.wait_ge(scattered[s], 64 * it)
                            dve.tensor_copy(U[:, s, :, D], SRCI[:, bass.ds(G * q, G)]).then_inc(src_ready, 1)
                    both(dve, body)

                @block.tensor
                def _(pe):
                    def body(it):
                        for s in range(2):
                            q = 2 * it + s
                            pe.wait_ge(hot_ready, q + 1)
                            if it is not 0:
                                pe.wait_ge(u_ready, q - 1)
                            for g in range(G):
                                j = pe.value_load(JROW[0:1, bass.ds(G * q + g, 1)], min_val=0, max_val=NT - 1)
                                for k in range(3):
                                    ins = pe.matmul(expd[s][:, g // 2, (g % 2) * D:(g % 2 + 1) * D], OHT[:, s, g * P:(g + 1) * P],
                                                    PARTS[:, k, bass.ds(j, 1), 0:D], start=(k == 0), stop=(k == 2))
                            ins.then_inc(exp_ready, 1)
                    both(pe, body)

                @block.scalar
                def _(act):
                    def body(it):
                        for s in range(2):
                            q = 2 * it + s
                            act.wait_ge(exp_ready, q + 1)
                            if it is not 0:
                                act.wait_ge(scattered[s], 64 * it)
                            for g in range(G):
                                ins = act.activation(U[:, s, g, 0:D], expd[s][:, g // 2, (g % 2) * D:(g % 2 + 1) * D], ACT.Copy,
                                                     scale=WGT[:, bass.ds(G * q + g, 1)])
                            ins.then_inc(u_ready, 1)
                    both(act, body)

                @block.gpsimd
                def _(pool):
                    def body(it):
                        for s in range(2):
                            q = 2 * it + s
                            if it is not 0:
                                pool.wait_ge(scattered[s], 64 * it)
                            pool.tensor_copy(GIDX[:, s, :], POSI[:, bass.ds(G * q, G)]).then_inc(idx_ready, 1)
                            pool.wait_ge(idx_ready, q + 1)
                            pool.wait_ge(u_ready, q + 1)
                            pool.wait_ge(src_ready, q + 1)
                            pool.nop(nofuse=True)
                            for g in range(G):
                                pool.indirect_dma_start(sup_d[:, :], bass.IndirectOffsetOnAxis(GIDX[:, s, g:g + 1], 0), U[:, s, g, :], None,
                                                        bounds_check=EP - 1, oob_is_err=False).then_inc(scattered[s], 16)
                    both(pool, body)
                    for s in range(2):
                        pool.wait_ge(scattered[s], 64 * turns)

        ctx, sem, ps = stage()
        with ctx:
            U = gath[:, 0:2 * G * UW].rearrange("p (s g w) -> p s g w", s=2, g=G)
            LS = ctx.enter_context(nc.sbuf_tensor("src_local", [P, 2, G], FP32))
            sums = [ps(f"sums{k}", [P, 2, 512]) for k in range(2)]
            rows_in = [sem(f"rows_in{k}") for k in range(2)]
            cleared, loc_ready, hot_ready, sum_ready, added = (sem("cleared"), sem("loc_ready"), sem("hot_ready"),
                                                               sem("sum_ready"), sem("added"))
            turns = NG // 2
            with nc.Block() as block:

                def both(eng, body):
                    body(0)
                    with eng.Fori(1, turns) as it:
                        body(it)

                @block.sync
                def _(sp):
                    def body(it):
                        for s in range(2):
                            q = 2 * it + s
                            for g in range(G):
                                m = sp.value_load(JROW[0:1, bass.ds(2 * NI + G * q + g, 1)], min_val=0, max_val=NB)
                                if it is not 0 and g == 0:
                                    sp.wait_ge(sum_ready, q - 1)
                                    sp.wait_ge(hot_ready, q - 1)
                                sp.dma_start(U[:, s, g, :], sup_d[bass.ds(m * P, P), :]).then_inc(rows_in[s], 16)
                    both(sp, body)

                @block.vector
                def _(dve):
                    dve.memset(SUP, 0.0).then_inc(cleared, 1)
                    dve.wait_ge(cleared, 1)

                    def hots(it, s):
                        q = 2 * it + s
                        dve.wait_ge(rows_in[s], 64 * (it + 1))
                        if it is not 0:
                            dve.wait_ge(sum_ready, q - 1)
                        dve.tensor_tensor(LS[:, s, :], U[:, s, :, D], TILE0[:, bass.ds(G * q, G)], ALU.subtract).then_inc(loc_ready, 1)
                        dve.wait_ge(loc_ready, q + 1)
                        dve.tensor_tensor(OH[:, s], iota_row[:, :].unsqueeze(1).broadcast_to([P, G, P]),
                                          LS[:, s, :].unsqueeze(2).broadcast_to([P, G, P]), ALU.is_equal).then_inc(hot_ready, 1)

                    def add(it, s):
                        q = 2 * it + s
                        for g in range(G):
                            j = dve.value_load(JROW[0:1, bass.ds(NI + G * q + g, 1)], min_val=0, max_val=NT - 1)
                            if g == 0:
                                dve.wait_ge(sum_ready, q + 1)
                            dve.tensor_tensor(SUP[:, bass.ds(j, 1), :], SUP[:, bass.ds(j, 1), :],
                                              sums[s][:, g // 2, (g % 2) * D:(g % 2 + 1) * D].unsqueeze(1), ALU.add).then_inc(added, 1)
                            dve.wait_ge(added, G * q + g + 1)

                    hots(0, 0)
                    hots(0, 1)
                    add(0, 0)
                    with dve.Fori(1, turns) as it:
                        hots(it, 0)
                        add(it - 1, 1)
                        hots(it, 1)
                        add(it, 0)
                    add(turns - 1, 1)

                @block.tensor
                def _(pe):
                    def body(it):
                        for s in range(2):
                            q = 2 * it + s
                            pe.wait_ge(hot_ready, q + 1)
                            if it is not 0:
                                pe.wait_ge(added, G * (q - 1))
                            for g in range(G):
                                ins = pe.matmul(sums[s][:, g // 2, (g % 2) * D:(g % 2 + 1) * D], OH[:, s, g, :], U[:, s, g, 0:D],
                                                start=True, stop=True)
                            ins.then_inc(sum_ready, 1)
                    both(pe, body)

        WB = sb("WB", [P, 4 * D], FP32)
        VEC = sb("VEC", [P, 3, D], FP32)
        STATS = sb("STATS", [P, NT, 8], FP32)
        MOM = sb("MOM", [P, NT, 2], FP32)
        RSTD = sb("RSTD", [P, NT, 2], FP32)
        x1_d = dram("x1", [NP, D], FP32)

        def by_tile(eng, one):
            one(0, 0, 0, True)
            one(1, 1, 0, True)
            with eng.Fori(1, NT // 2) as it:
                one(2 * it, 0, it, False)
                one(2 * it + 1, 1, it, False)
            one(NT - 1, 0, NT // 2, False)

        XS = gath[:, 0:4 * D].rearrange("p (s w) -> p s w", s=2)
        XT = gath[:, 4 * D:8 * D].rearrange("p (s w) -> p s w", s=2)

        def layernorm(dve, moments, rooted, chain, count, normed):
            link = Chain(dve, chain, count)
            for t in range(NT):
                ins = dve.bn_stats(STATS[:, t, 0:6], Xv[:, t, :])
            link(ins)
            for t in range(NT):
                ins = dve.bn_aggr(MOM[:, t, :], STATS[:, t, 0:6])
            link(ins)
            dve.tensor_scalar(MOM[:, :, 1], MOM[:, :, 1], EPS, None, ALU.add).then_inc(moments, 1)
            dve.wait_ge(rooted, 1)
            link(dve.reciprocal(RSTD[:, :, 1], RSTD[:, :, 0]))
            for t in range(NT):
                ins = dve.tensor_scalar(Xv[:, t, :], Xv[:, t, :], MOM[:, t, 0:1], RSTD[:, t, 1:2], ALU.subtract, ALU.mult)
            ins.then_inc(normed, 1)

        ctx, sem, ps = stage()
        with ctx:
            psum_t = [ps(f"t{k}", [P, 512]) for k in range(2)]
            psum_o = [ps(f"o{k}", [P, 512]) for k in range(2)]
            w_in, copied, transposed, evacuated, product, chain, moments, rooted, normed, stored = (
                sem("w_in"), sem("copied"), sem("transposed"), sem("evacuated"), sem("product"), sem("chain"),
                sem("moments"), sem("rooted"), sem("normed"), sem("stored"))
            O = work[:, 0:2 * D].rearrange("p (s d) -> p s d", s=2)
            with nc.Block() as block:

                @block.sync
                def _(sp):
                    sp.dma_start(WB[:, :].rearrange("p (k n) -> p k n", k=4), W0.rearrange("(k p) n -> p k n", p=P)).then_inc(w_in, 16)
                    sp.dma_start(VEC[:, 0, :], b0.rearrange("(a n) -> a n", a=1).broadcast_to([P, D])).then_inc(w_in, 16)
                    sp.wait_ge(normed, 1)
                    sp.dma_start(x1_d[:, :].rearrange("(t p) d -> p t d", p=P), Xv).then_inc(stored, 16)
                    sp.wait_ge(stored, 16)

                @block.scalar
                def _(act):
                    def one(q, s, turn, first):
                        if not first:
                            act.wait_ge(transposed, q - 1)
                        act.activation(XS[:, s, 0:D], Xv[:, bass.ds(q, 1), :], ACT.Copy).then_inc(copied, 1)
                        act.activation(XS[:, s, D:2 * D], SUP[:, bass.ds(q, 1), :], ACT.Copy).then_inc(copied, 1)
                        act.wait_ge(transposed, q + 1)
                        if not first:
                            act.wait_ge(product, q - 1)
                        act.activation(XT[:, s, :], psum_t[s][:, :], ACT.Copy).then_inc(evacuated, 1)
                    by_tile(act, one)
                    act.wait_ge(moments, 1)
                    act.activation(RSTD[:, :, 0], MOM[:, :, 1], ACT.Sqrt).then_inc(rooted, 1)

                @block.tensor
                def _(pe):
                    pe.wait_ge(w_in, 32)

                    def one(q, s, turn, first):
                        pe.wait_ge(copied, 2 * q + 2)
                        if not first:
                            pe.wait_ge(evacuated, q - 1)
                        for k in range(4):
                            ins = pe.transpose(psum_t[s][:, k * P:(k + 1) * P], XS[:, s, k * P:(k + 1) * P], ident[:, :])
                        ins.then_inc(transposed, 1)
                        pe.wait_ge(evacuated, q + 1)
                        if not first:
                            pe.wait_ge(chain, 2 * (q - 1))
                        for k in range(4):
                            ins = pe.matmul(psum_o[s][:, 0:D], XT[:, s, k * P:(k + 1) * P], WB[:, k * D:(k + 1) * D],
                                            start=(k == 0), stop=(k == 3))
                        ins.then_inc(product, 1)
                    by_tile(pe, one)

                @block.vector
                def _(dve):
                    dve.wait_ge(w_in, 32)

                    def one(q, s, turn, first):
                        link = Chain(dve, chain, 2 * q)
                        dve.wait_ge(product, q + 1)
                        link(dve.tensor_tensor(O[:, s, :], psum_o[s][:, 0:D], VEC[:, 0, :], ALU.add))
                        dve.wait_ge(copied, 2 * q + 2)
                        link(dve.scalar_tensor_tensor(Xv[:, bass.ds(q, 1), :], O[:, s, :].unsqueeze(1), 0.0, Xv[:, bass.ds(q, 1), :], ALU.max, ALU.add))
                    by_tile(dve, one)
                    layernorm(dve, moments, rooted, chain, 2 * NT, normed)

        for layer, (Wl, Wr, att, bias) in enumerate(gat):
            ctx, sem, ps = stage()
            with ctx:
                psum_t = [ps(f"t{k}", [P, 512]) for k in range(2)]
                psum_o = [ps(f"o{k}", [P, 512]) for k in range(2)]
                w_in, copied, transposed, evacuated, product, chain, att_ready, rows_copied, stored = (
                    sem("w_in"), sem("copied"), sem("transposed"), sem("evacuated"), sem("product"), sem("chain"),
                    sem("att_ready"), sem("rows_copied"), sem("stored"))
                rows_stored = [sem(f"rows_stored{k}") for k in range(2)]
                parts = sem("parts")
                LR = work[:, 0:4 * RW].rearrange("p (s k w) -> p s k w", s=2, k=2)
                PR = work[:, 4 * RW:4 * RW + 4 * D].rearrange("p (s k w) -> p s k w", s=2, k=2)
                RES = gath[:, 8 * D:8 * D + 2 * RW].rearrange("p (s w) -> p s w", s=2)
                S8 = gath[:, 8 * D + 2 * RW:8 * D + 2 * RW + 2 * H].rearrange("p (s w) -> p s w", s=2)
                STEPS = 7
                with nc.Block() as block:

                    @block.sync
                    def _(sp):
                        WBv = WB[:, :].rearrange("p (k n) -> p k n", k=2)
                        sp.dma_start(WBv[:, :, 0:D], Wl.rearrange("(k p) n -> p k n", p=P)).then_inc(w_in, 16)
                        sp.dma_start(WBv[:, :, D:2 * D], Wr.rearrange("(k p) n -> p k n", p=P)).then_inc(w_in, 16)
                        sp.dma_start(VEC[:, 0, :], bias.rearrange("(a n) -> a n", a=1).broadcast_to([P, D])).then_inc(w_in, 16)
                        sp.dma_start(VEC[:, 2, :], att.rearrange("h c -> (h c)").rearrange("(a n) -> a n", a=1).broadcast_to([P, D])).then_inc(w_in, 16)

                        def one(q, s, turn, first):
                            sp.wait_ge(chain, STEPS * q + 2)
                            sp.dma_start(tab_d[bass.ds(P * q, P), :], LR[:, s, 0, 0:XW]).then_inc(rows_stored[s], 16)
                        by_tile(sp, one)
                        sp.wait_ge(rows_stored[0], 16 * (NT - NT // 2))
                        sp.wait_ge(rows_stored[1], 16 * (NT // 2))

                    @block.scalar
                    def _(act):
                        def one(q, s, turn, first):
                            if not first:
                                act.wait_ge(transposed, q - 1)
                            act.activation(XS[:, s, 0:D], Xv[:, bass.ds(q, 1), :], ACT.Copy).then_inc(copied, 1)
                            act.wait_ge(transposed, q + 1)
                            if not first:
                                act.wait_ge(product, q - 1)
                            act.activation(XT[:, s, 0:D], psum_t[s][:, 0:D], ACT.Copy).then_inc(evacuated, 1)
                            act.wait_ge(product, q + 1)
                            if not first:
                                act.wait_ge(parts, 5 * (q - 1))
                                act.wait_ge(rows_stored[s], 16 * turn)
                            act.activation(LR[:, s, :, 0:D], psum_o[s][:, :].rearrange("p (k d) -> p k d", k=2), ACT.Copy).then_inc(rows_copied, 1)
                            act.wait_ge(chain, STEPS * (q + 1))
                            act.activation(PARTS[:, 0, bass.ds(q, 1), :], LR[:, s, 1, :].unsqueeze(1), ACT.Copy).then_inc(parts, 1)
                            act.wait_ge(parts, 5 * q + 2)
                            act.activation(PARTS[:, 1, bass.ds(q, 1), :], RES[:, s, :].unsqueeze(1), ACT.Copy).then_inc(parts, 1)
                            act.wait_ge(parts, 5 * q + 4)
                            act.activation(PARTS[:, 2, bass.ds(q, 1), :], RES[:, s, :].unsqueeze(1), ACT.Copy).then_inc(parts, 1)
                        by_tile(act, one)

                    @block.gpsimd
                    def _(pool):
                        def one(q, s, turn, first):
                            pool.wait_ge(parts, 5 * q + 1)
                            pool.tensor_tensor(RES[:, s, :].unsqueeze(1), LR[:, s, 1, :].unsqueeze(1), PARTS[:, 0, bass.ds(q, 1), :], ALU.subtract).then_inc(parts, 1)
                            pool.wait_ge(parts, 5 * q + 3)
                            pool.tensor_tensor(RES[:, s, :].unsqueeze(1), RES[:, s, :].unsqueeze(1), PARTS[:, 1, bass.ds(q, 1), :], ALU.subtract).then_inc(parts, 1)
                        by_tile(pool, one)

                    @block.tensor
                    def _(pe):
                        pe.wait_ge(w_in, 64)

                        def one(q, s, turn, first):
                            pe.wait_ge(copied, q + 1)
                            if not first:
                                pe.wait_ge(evacuated, q - 1)
                            for k in range(2):
                                ins = pe.transpose(psum_t[s][:, k * P:(k + 1) * P], XS[:, s, k * P:(k + 1) * P], ident[:, :])
                            ins.then_inc(transposed, 1)
                            pe.wait_ge(evacuated, q + 1)
                            if not first:
                                pe.wait_ge(rows_copied, q - 1)
                            for k in range(2):
                                ins = pe.matmul(psum_o[s][:, :], XT[:, s, k * P:(k + 1) * P], WB[:, 2 * k * D:2 * (k + 1) * D],
                                                start=(k == 0), stop=(k == 1))
                            ins.then_inc(product, 1)
                        by_tile(pe, one)

                    @block.vector
                    def _(dve):
                        dve.wait_ge(w_in, 64)
                        dve.tensor_scalar(VEC[:, 1, :], VEC[:, 2, :], SLOPE, None, ALU.mult).then_inc(att_ready, 1)
                        dve.wait_ge(att_ready, 1)
                        dve.tensor_scalar(VEC[:, 2, :], VEC[:, 2, :], 1.0 - SLOPE, None, ALU.mult).then_inc(att_ready, 1)
                        dve.wait_ge(att_ready, 2)

                        def one(q, s, turn, first):
                            link = Chain(dve, chain, STEPS * q)
                            dve.wait_ge(rows_copied, q + 1)
                            link(dve.tensor_tensor(PR[:, s, :, :], LR[:, s, :, 0:D], VEC[:, 1, :].unsqueeze(1).broadcast_to([P, 2, D]), ALU.mult))
                            link(dve.tensor_reduce(LR[:, s, :, D:D + H], PR[:, s, :, :].rearrange("p k (h c) -> p k h c", c=C), AX, ALU.add))
                            link(dve.tensor_tensor(PR[:, s, 0, :], LR[:, s, 0, 0:D], LR[:, s, 1, 0:D], ALU.add))
                            link(dve.scalar_tensor_tensor(PR[:, s, 1, :], PR[:, s, 0, :], 0.0, VEC[:, 2, :], ALU.max, ALU.mult))
                            link(dve.tensor_reduce(S8[:, s, :], PR[:, s, 1, :].rearrange("p (h c) -> p h c", c=C), AX, ALU.add))
                            link(dve.tensor_tensor(S8[:, s, :], S8[:, s, :], LR[:, s, 0, D:D + H], ALU.add))
                            link(dve.tensor_tensor(LR[:, s, 1, D + H:RW], S8[:, s, :], LR[:, s, 1, D:D + H], ALU.add))
                        by_tile(dve, one)

            ctx, sem, ps = stage()
            with ctx:
                expd = [ps(f"expd{k}", [P, G, 512]) for k in range(2)]
                loc_in = [sem(f"loc_in{k}") for k in range(2)]
                gathered = [sem(f"gathered{k}") for k in range(4)]
                spilled = [sem(f"spilled{k}") for k in range(4)]
                hot_ready, exp_ready, idx_ready, z_ready, self_ready, relu_ready, weighted, scored = (
                    sem("hot_ready"), sem("exp_ready"), sem("idx_ready"), sem("z_ready"), sem("self_ready"),
                    sem("relu_ready"), sem("weighted"), sem("scored"))
                turns = NG // 4
                with nc.Block() as block:

                    def quads(eng, body):
                        body(0)
                        with eng.Fori(1, turns) as it:
                            body(it)

                    @block.gpsimd
                    def _(pool):
                        def body(it):
                            for s in range(4):
                                q = 4 * it + s
                                if it is not 0:
                                    pool.wait_ge(spilled[s], 16 * it)
                                    pool.wait_ge(z_ready, q - 3)
                                pool.tensor_copy(GIDX[:, s, :], SRCI[:, bass.ds(G * q, G)]).then_inc(idx_ready, 1)
                                pool.wait_ge(idx_ready, q + 1)
                                pool.nop(nofuse=True)
                                for g in range(G):
                                    pool.indirect_dma_start(GATH[:, s, g, :], None, tab_d[:, :],
                                                            bass.IndirectOffsetOnAxis(GIDX[:, s, g:g + 1], 0)).then_inc(gathered[s], 16)
                        quads(pool, body)

                    @block.sync
                    def _(sp):
                        def spill(q, s, turn):
                            sp.wait_ge(gathered[s], 64 * (turn + 1))
                            sp.dma_start(spill_d[bass.ds(q, 1), :, :].rearrange("a p w -> (a p) w"), GATH[:, s].rearrange("p g w -> p (g w)")).then_inc(spilled[s], 16)

                        def body(it):
                            for s in range(4):
                                q = 4 * it + s
                                if not (it is 0 and s < 2):
                                    sp.wait_ge(hot_ready, q - 1)
                                sp.dma_start(LBC[:, s % 2, :], loc_d[bass.ds(G * q, G), :].rearrange("g q -> (g q)")
                                             .rearrange("(a n) -> a n", a=1).broadcast_to([P, G * P])).then_inc(loc_in[s % 2], 16)
                                if not (it is 0 and s < 2):
                                    ps_, turn = back(it, s, 2, 4)
                                    spill(q - 2, ps_, turn)
                        quads(sp, body)
                        spill(NG - 2, 2, turns - 1)
                        spill(NG - 1, 3, turns - 1)
                        for s in range(4):
                            sp.wait_ge(spilled[s], 16 * turns)

                    @block.tensor
                    def _(pe):
                        def body(it):
                            for s in range(4):
                                q = 4 * it + s
                                pe.wait_ge(hot_ready, q + 1)
                                if not (it is 0 and s < 2):
                                    pe.wait_ge(z_ready, q - 1)
                                    pe.wait_ge(self_ready, q - 1)
                                for g in range(G):
                                    j = pe.value_load(JROW[0:1, bass.ds(G * q + g, 1)], min_val=0, max_val=NT - 1)
                                    for k in range(3):
                                        ins = pe.matmul(expd[s % 2][:, g, 0:RW], OHT[:, s % 2, g * P:(g + 1) * P],
                                                        PARTS[:, k, bass.ds(j, 1), :], start=(k == 0), stop=(k == 2))
                                ins.then_inc(exp_ready, 1)
                        quads(pe, body)

                    @block.vector
                    def _(dve):
                        Zv = Z.rearrange("p s (g w) -> p s g w", g=G)
                        Tv = T.rearrange("p s (g h c) -> p s g h c", g=G, h=H)

                        def hots(q, s2, turn2, first):
                            dve.wait_ge(loc_in[s2], 16 * (turn2 + 1))
                            if not first:
                                dve.wait_ge(exp_ready, q - 1)
                            dve.tensor_scalar(OHT[:, s2, :], LBC[:, s2, :], iota_p[:, 0:1], None, ALU.is_equal).then_inc(hot_ready, 1)

                        def add(q, s4, turn4, first):
                            dve.wait_ge(gathered[s4], 64 * (turn4 + 1))
                            dve.wait_ge(exp_ready, q + 1)
                            if not first:
                                dve.wait_ge(relu_ready, 2 * (q - 1))
                            dve.tensor_tensor(Zv[:, s4 % 2], expd[s4 % 2][:, :, 0:XW], GATH[:, s4], ALU.add).then_inc(z_ready, 1)

                        def score(q, s2):
                            dve.wait_ge(relu_ready, 2 * q + 2)
                            TR = Tv[:, s2, :, :, 0:C]
                            dve.tensor_tensor(TR, TR, VEC[:, 2, :].rearrange("p (h c) -> p h c", h=H).unsqueeze(1).broadcast_to([P, G, H, C]),
                                              ALU.mult).then_inc(weighted, 1)
                            dve.wait_ge(weighted, q + 1)
                            dve.tensor_reduce(SC[:, bass.ds(G * H * q, G * H)], T[:, s2, :].rearrange("p (g c) -> p g c", c=C + 1),
                                              AX, ALU.add).then_inc(scored, 1)

                        def body(it):
                            for s in range(4):
                                q = 4 * it + s
                                at0 = it is 0
                                hots(q, s % 2, 2 * it + s // 2, at0 and s < 2)
                                if not (at0 and s < 1):
                                    b, turn = back(it, s, 1, 4)
                                    add(q - 1, b, turn, at0 and s < 3)
                                if not (at0 and s < 2):
                                    score(q - 2, s % 2)
                        quads(dve, body)
                        add(NG - 1, 3, turns - 1, False)
                        score(NG - 2, 0)
                        score(NG - 1, 1)

                    @block.scalar
                    def _(act):
                        Zv = Z.rearrange("p s (g w) -> p s g w", g=G)
                        Tv = T.rearrange("p s (g h c) -> p s g h c", g=G, h=H)

                        def body(it):
                            for s in range(4):
                                q = 4 * it + s
                                act.wait_ge(z_ready, q + 1)
                                if not (it is 0 and s < 2):
                                    act.wait_ge(scored, q - 1)
                                act.activation(SELF[:, bass.ds(G * H * q, G * H)].rearrange("p (g h) -> p g h", g=G),
                                               expd[s % 2][:, :, XW:RW], ACT.Copy).then_inc(self_ready, 1)
                                act.activation(Tv[:, s % 2, :, :, 0:C], Zv[:, s % 2, :, 0:D].rearrange("p g (h c) -> p g h c", h=H),
                                               ACT.Relu).then_inc(relu_ready, 1)
                                act.activation(Tv[:, s % 2, :, :, C], Zv[:, s % 2, :, D:XW], ACT.Copy).then_inc(relu_ready, 1)
                        quads(act, body)

            ctx, sem, ps = stage()
            with ctx:
                psum_f = [ps(f"f{k}", [P, 512]) for k in range(4)]
                BANKS = -(-RUN // 4)
                W = NI * H
                SM = ctx.enter_context(nc.sbuf_tensor(f"summary{layer}", [P, 8], FP32))
                CR = ctx.enter_context(nc.sbuf_tensor(f"carries{layer}", [P, 2], FP32))
                KH = ctx.enter_context(nc.sbuf_tensor(f"by_head{layer}", [H, 10, CHUNKS], FP32))
                F2 = gath[:, 0:W]
                masked, to_rows, rows_ev, chain, summary, sum_in, carried, back_ready, to_cols, cols_ev, shifted, exped = (
                    sem("masked"), sem("to_rows"), sem("rows_ev"), sem("chain"), sem("summary"), sem("sum_in"), sem("carried"),
                    sem("back_ready"), sem("to_cols"), sem("cols_ev"), sem("shifted"), sem("exped"))
                carry_s = sem("carry_s")

                def krh(a):
                    return a.rearrange("p (k r h) -> p k r h", k=CHUNKS, r=RUN)

                def rkh(a):
                    return a.rearrange("p (r k h) -> p k r h", k=CHUNKS, r=RUN)

                with nc.Block() as block:

                    @block.vector
                    def _(dve):
                        link = Chain(dve, chain)
                        link(dve.tensor_tensor(SC.rearrange("p (i h) -> p i h", h=H), SC.rearrange("p (i h) -> p i h", h=H),
                                               MASK[:, :].unsqueeze(2).broadcast_to([P, NI, H]), ALU.add))
                        link(dve.tensor_tensor(SELF.rearrange("p (i h) -> p i h", h=H), SELF.rearrange("p (i h) -> p i h", h=H),
                                               MASK[:, :].unsqueeze(2).broadcast_to([P, NI, H]), ALU.add))
                        dve.tensor_tensor(rkh(FW), krh(SC), krh(SELF), ALU.max).then_inc(masked, 1)
                        dve.tensor_copy(SM[:, 4:5], RST[:, 0:1])
                        link(dve.tensor_reduce(SM[:, 1:2], RST[:, 0:W], AX, ALU.min))
                        link(dve.tensor_reduce(SM[:, 3:4], RST[:, 1:W], AX, ALU.min))
                        link(dve.memset(KH[:, :, :], -BIG))
                        dve.wait_ge(rows_ev, BANKS)
                        link(dve.tensor_tensor_scan(FW, RST[:, 0:W], D1, -BIG, ALU.add, ALU.max))
                        link(dve.tensor_copy(SM[:, 0:1], FW[:, W - 1:W]))
                        link(dve.tensor_tensor_scan(F2[:, ::-1], RST[:, 1:W + 1][:, ::-1], FW[:, ::-1], -BIG, ALU.add, ALU.max))
                        dve.tensor_copy(SM[:, 2:3], F2[:, 0:1]).then_inc(summary, 1)
                        dve.wait_ge(sum_in, 5 * 16)
                        last, low, first, low1, reset = [KH[:, k, :] for k in range(5)]
                        run, left, right, t0, t1 = [KH[:, k, :] for k in range(5, 10)]
                        K1 = CHUNKS - 1
                        link(dve.tensor_tensor_scan(run, low, last, -BIG, ALU.add, ALU.max))
                        link(dve.tensor_copy(left[:, 1:], run[:, 0:K1]))
                        link(dve.tensor_tensor(t0[:, 0:K1], low1[:, 0:K1], reset[:, 1:], ALU.add))
                        link(dve.tensor_tensor_scan(t1[:, ::-1], t0[:, ::-1], first[:, ::-1], -BIG, ALU.add, ALU.max))
                        link(dve.tensor_tensor(right[:, 0:K1], t1[:, 1:], reset[:, 1:], ALU.add))
                        dve.tensor_copy(t0, right).then_inc(carried, 1)
                        dve.wait_ge(back_ready, 2 * 16)
                        link(dve.tensor_tensor_scan(F2, RST[:, 0:W], D1, CR[:, 0:1], ALU.add, ALU.max))
                        dve.tensor_tensor_scan(D1[:, ::-1], RST[:, 1:W + 1][:, ::-1], F2[:, ::-1], CR[:, 1:2], ALU.add, ALU.max).then_inc(masked, 1)
                        dve.wait_ge(cols_ev, BANKS)
                        dve.tensor_tensor(krh(SC), krh(SC), rkh(FW), ALU.subtract)
                        dve.tensor_tensor(krh(SELF), krh(SELF), rkh(FW), ALU.subtract).then_inc(shifted, 1)
                        dve.wait_ge(exped, 2)
                        EXs = EX.rearrange("p (i w) -> p i w", w=2 * H)[:, :, H:2 * H]
                        dve.tensor_tensor(EXs, EXs, START[:, :].unsqueeze(2).broadcast_to([P, NI, H]), ALU.mult)

                    @block.tensor
                    def _(pe):
                        pe.wait_ge(masked, 1)
                        for r in range(RUN):
                            b = r // 4
                            if b >= 4 and r % 4 == 0:
                                pe.wait_ge(rows_ev, b - 3)
                            ins = pe.transpose(psum_f[b % 4][:, (r % 4) * P:(r % 4 + 1) * P], FW[:, r * P:(r + 1) * P], ident[:, :])
                            if r % 4 == 3 or r == RUN - 1:
                                ins.then_inc(to_rows, 1)
                        pe.wait_ge(masked, 2)
                        pe.wait_ge(rows_ev, BANKS)
                        for r in range(RUN):
                            b = r // 4
                            if b >= 4 and r % 4 == 0:
                                pe.wait_ge(cols_ev, b - 3)
                            ins = pe.transpose(psum_f[b % 4][:, (r % 4) * P:(r % 4 + 1) * P], D1[:, r * P:(r + 1) * P], ident[:, :])
                            if r % 4 == 3 or r == RUN - 1:
                                ins.then_inc(to_cols, 1)

                    @block.scalar
                    def _(act):
                        for dst_buf, full, done in ((D1, to_rows, rows_ev), (FW, to_cols, cols_ev)):
                            for b in range(BANKS):
                                n = min(4, RUN - 4 * b) * P
                                act.wait_ge(full, b + 1)
                                act.activation(dst_buf[:, b * 4 * P:b * 4 * P + n], psum_f[b % 4][:, 0:n], ACT.Copy).then_inc(done, 1)
                        EXv = EX.rearrange("p (i w) -> p i w", w=2 * H)
                        act.wait_ge(shifted, 1)
                        act.activation(EXv[:, :, 0:H], SC.rearrange("p (i h) -> p i h", h=H), ACT.Exp).then_inc(exped, 1)
                        act.activation(EXv[:, :, H:2 * H], SELF.rearrange("p (i h) -> p i h", h=H), ACT.Exp).then_inc(exped, 1)

                    @block.sync
                    def _(sp):
                        SLOW = dict(allow_slow_non_contiguous=True)
                        sp.wait_ge(summary, 1)
                        sp.dma_start(sum_d[:, :], SM[:, 0:5]).then_inc(carry_s, 16)
                        sp.wait_ge(carry_s, 16)
                        for k in range(5):
                            sp.dma_start(KH[:, k, :], sum_d[:, k].rearrange("(k h) -> h k", h=H), **SLOW).then_inc(sum_in, 16)
                        sp.wait_ge(carried, 1)
                        for k in range(2):
                            sp.dma_start(carry_d[k, :].rearrange("(k h) -> h k", h=H), KH[:, 6 + k, :], **SLOW).then_inc(carry_s, 16)
                        sp.wait_ge(carry_s, 48)
                        for k in range(2):
                            sp.dma_start(CR[:, k:k + 1], carry_d[k, :].rearrange("(p a) -> p a", a=1), **SLOW).then_inc(back_ready, 16)
                        sp.wait_ge(back_ready, 32)

            ctx, sem, ps = stage()
            with ctx:
                sums = [ps(f"sums{k}", [P, G, 512]) for k in range(2)]
                rows_in = [sem(f"rows_in{k}") for k in range(4)]
                cleared, hot_ready, sum_ready, added, weighted = (sem("cleared"), sem("hot_ready"), sem("sum_ready"),
                                                                  sem("added"), sem("weighted"))
                turns = NG // 4
                EXv = EX.rearrange("p (i w) -> p i w", w=2 * H)
                with nc.Block() as block:

                    def quads(eng, body):
                        body(0)
                        with eng.Fori(1, turns) as it:
                            body(it)

                    @block.sync
                    def _(sp):
                        def body(it):
                            for s in range(4):
                                q = 4 * it + s
                                if it is not 0:
                                    sp.wait_ge(sum_ready, q - 3)
                                sp.dma_start(GATH[:, s].rearrange("p g w -> p (g w)"), spill_d[bass.ds(q, 1), :, :].rearrange("a p w -> (a p) w")).then_inc(rows_in[s], 16)
                        quads(sp, body)

                    @block.gpsimd
                    def _(pool):
                        def body(it):
                            for s in range(4):
                                q = 4 * it + s
                                pool.wait_ge(rows_in[s], 16 * (it + 1))
                                V = GATH[:, s, :, 0:D].rearrange("p g (h c) -> p g h c", h=H)
                                pool.tensor_tensor(V, V, EXv[:, bass.ds(G * q, G), 0:H].unsqueeze(3).broadcast_to([P, G, H, C]), ALU.mult).then_inc(weighted, 1)
                        quads(pool, body)

                    @block.tensor
                    def _(pe):
                        def body(it):
                            for s in range(4):
                                q = 4 * it + s
                                pe.wait_ge(hot_ready, q + 1)
                                pe.wait_ge(weighted, q + 1)
                                if not (it is 0 and s < 2):
                                    pe.wait_ge(added, G * (q - 1))
                                for g in range(G):
                                    pe.matmul(sums[s % 2][:, g, 0:D], OH[:, s % 2, g, :], GATH[:, s, g, 0:D], start=True, stop=True)
                                    ins = pe.matmul(sums[s % 2][:, g, D:RW], OH[:, s % 2, g, :], EXv[:, bass.ds(G * q + g, 1), :], start=True, stop=True)
                                ins.then_inc(sum_ready, 1)
                        quads(pe, body)

                    @block.vector
                    def _(dve):
                        dve.memset(ACC, 0.0).then_inc(cleared, 1)
                        dve.wait_ge(cleared, 1)

                        def hots(q, s2, first):
                            if not first:
                                dve.wait_ge(sum_ready, q - 1)
                            dve.tensor_tensor(OH[:, s2], iota_row[:, :].unsqueeze(1).broadcast_to([P, G, P]),
                                              LOC[:, bass.ds(G * q, G)].unsqueeze(2).broadcast_to([P, G, P]), ALU.is_equal).then_inc(hot_ready, 1)

                        def add(q, s2):
                            for g in range(G):
                                j = dve.value_load(JROW[0:1, bass.ds(G * q + g, 1)], min_val=0, max_val=NT - 1)
                                if g == 0:
                                    dve.wait_ge(sum_ready, q + 1)
                                dve.tensor_tensor(ACC[:, bass.ds(j, 1), :], ACC[:, bass.ds(j, 1), :], sums[s2][:, g, 0:RW].unsqueeze(1), ALU.add).then_inc(added, 1)
                                dve.wait_ge(added, G * q + g + 1)

                        def body(it):
                            for s in range(4):
                                q = 4 * it + s
                                hots(q, s % 2, it is 0 and s < 2)
                                if not (it is 0 and s < 1):
                                    add(q - 1, (s - 1) % 2)
                        quads(dve, body)
                        add(NG - 1, 1)

            ctx, sem, ps = stage()
            with ctx:
                TB = gath[:, 0:2 * D].rearrange("p (s d) -> p s d", s=2)
                TO = gath[:, 2 * D:4 * D].rearrange("p (s d) -> p s d", s=2)
                TG = gath[:, 4 * D:6 * D].rearrange("p (s d) -> p s d", s=2)
                SW = work[:, 0:NT * H].rearrange("p (t h) -> p t h", h=H)
                DN = work[:, NT * H:2 * NT * H].rearrange("p (t h) -> p t h", h=H)
                rows_in = [sem(f"rows_in{k}") for k in range(2)]
                chain, gelu_ready, summed = sem("chain"), sem("gelu_ready"), sem("summed")
                heads = lambda a: a.rearrange("p (h c) -> p h c", h=H)
                with nc.Block() as block:

                    @block.sync
                    def _(sp):
                        def one(q, s, turn, first):
                            if not first:
                                sp.wait_ge(chain, 5 + 4 * (q - 1))
                            sp.dma_start(TB[:, s, :], tab_d[bass.ds(P * q, P), 0:D]).then_inc(rows_in[s], 16)
                        by_tile(sp, one)

                    @block.vector
                    def _(dve):
                        link = Chain(dve, chain)
                        link(dve.tensor_scalar(DN, ACC[:, :, D:D + H], 0.0, None, ALU.is_equal))
                        link(dve.tensor_tensor(SW, ACC[:, :, D + H:RW], DN, ALU.max))
                        link(dve.tensor_tensor(DN, ACC[:, :, D:D + H], SW, ALU.add))
                        link(dve.tensor_scalar(DN, DN, 1e-16, None, ALU.max))
                        link(dve.reciprocal(DN, DN))

                        def one(q, s, turn, first):
                            link = Chain(dve, chain, 5 + 4 * q)
                            dve.wait_ge(rows_in[s], 16 * (turn + 1))
                            link(dve.tensor_tensor(heads(TB[:, s, :]), heads(TB[:, s, :]),
                                                   SW[:, bass.ds(q, 1), :].rearrange("p a h -> p (a h)").unsqueeze(2).broadcast_to([P, H, C]), ALU.mult))
                            if not first:
                                dve.wait_ge(gelu_ready, q - 1)
                            link(dve.tensor_tensor(TO[:, s, :].unsqueeze(1), TB[:, s, :].unsqueeze(1), ACC[:, bass.ds(q, 1), 0:D], ALU.add))
                            link(dve.tensor_tensor(heads(TO[:, s, :]), heads(TO[:, s, :]),
                                                   DN[:, bass.ds(q, 1), :].rearrange("p a h -> p (a h)").unsqueeze(2).broadcast_to([P, H, C]), ALU.mult))
                            link(dve.tensor_tensor(TO[:, s, :], TO[:, s, :], VEC[:, 0, :], ALU.add))
                        by_tile(dve, one)

                    @block.scalar
                    def _(act):
                        def one(q, s, turn, first):
                            act.wait_ge(chain, 5 + 4 * (q + 1))
                            if not first:
                                act.wait_ge(summed, q - 1)
                            act.activation(TG[:, s, :], TO[:, s, :], ACT.Gelu).then_inc(gelu_ready, 1)
                        by_tile(act, one)

                    @block.gpsimd
                    def _(pool):
                        def one(q, s, turn, first):
                            pool.wait_ge(gelu_ready, q + 1)
                            pool.tensor_tensor(Xv[:, bass.ds(q, 1), :], Xv[:, bass.ds(q, 1), :], TG[:, s, :].unsqueeze(1), ALU.add).then_inc(summed, 1)
                        by_tile(pool, one)

        ctx, sem, ps = stage()
        with ctx:
            O = gath[:, 0:2 * D].rearrange("p (s d) -> p s d", s=2)
            rows_in = [sem(f"rows_in{k}") for k in range(2)]
            chain, moments, rooted, normed, stored = (sem("chain"), sem("moments"), sem("rooted"), sem("normed"), sem("stored"))
            with nc.Block() as block:

                @block.sync
                def _(sp):
                    def one(q, s, turn, first):
                        if not first:
                            sp.wait_ge(chain, q - 1)
                        sp.dma_start(O[:, s, :], x1_d[bass.ds(P * q, P), :]).then_inc(rows_in[s], 16)
                    by_tile(sp, one)
                    sp.wait_ge(normed, 1)
                    sp.dma_start(out[0:(NT - 1) * P, :].rearrange("(t p) d -> p t d", p=P), Xv[:, 0:NT - 1, :]).then_inc(stored, 16)
                    sp.dma_start(out[(NT - 1) * P:N, :], Xv[0:TAIL, NT - 1, :]).then_inc(stored, 16)
                    sp.wait_ge(stored, 32)

                @block.vector
                def _(dve):
                    def one(q, s, turn, first):
                        link = Chain(dve, chain, q)
                        dve.wait_ge(rows_in[s], 16 * (turn + 1))
                        link(dve.tensor_tensor(Xv[:, bass.ds(q, 1), :], Xv[:, bass.ds(q, 1), :], O[:, s, :].unsqueeze(1), ALU.add))
                    by_tile(dve, one)
                    layernorm(dve, moments, rooted, chain, NT, normed)

                @block.scalar
                def _(act):
                    act.wait_ge(moments, 1)
                    act.activation(RSTD[:, :, 0], MOM[:, :, 1], ACT.Sqrt).then_inc(rooted, 1)


_INS = ['x', 'src', 'dst', 'edge_weight', 'L0_gnn_W', 'L0_gnn_b', 'L1_gnn_Wl0', 'L1_gnn_Wr0', 'L1_gnn_att0', 'L1_gnn_b0',
        'L1_gnn_Wl1', 'L1_gnn_Wr1', 'L1_gnn_att1', 'L1_gnn_b1']


def kernel(**inputs):
    import numpy as np
    import concourse.bacc as bacc
    from concourse.bass_utils import run_bass_kernel_spmd as run

    nc = bacc.Bacc("TRN2", target_bir_lowering=False, num_devices=1)
    arrays, ins = {}, []
    for name in _INS:
        a = np.ascontiguousarray(inputs[name])
        arrays[f"in_{name}"] = a
        ins.append(nc.dram_tensor(f"in_{name}", a.shape, mybir.dt.from_np(a.dtype), kind="ExternalInput").ap())
    out = nc.dram_tensor("out_0", (N, D), FP32, kind="ExternalOutput").ap()
    gat = [ins[6:10], ins[10:14]]
    build(nc, *ins[:6], gat, out)
    r = run(nc, [arrays], core_ids=[0])
    return r.results[0]["out_0"]
```

```python
import concourse.bass as bass
from concourse import mybir
from contextlib import ExitStack

FP32 = mybir.dt.float32
BF16 = mybir.dt.bfloat16
I32 = mybir.dt.int32
ALU = mybir.AluOpType
ACT = mybir.ActivationFunctionType
AX = mybir.AxisListType.X

P = 128
N, D, H, E = 3125, 256, 8, 50000
C = D // H
NT = -(-N // P)
NP = NT * P
TAIL = N - (NT - 1) * P
NB = -(-E // P)
EB = NB + 1
EP = EB * P
CHUNKS = P // H
NI = -(-(NB + NT - 1) // CHUNKS) * CHUNKS
RUN = NI // CHUNKS
G = 4
NG = NI // G
IR = NI // G
NJ = NT - 1
VS = EB // G + NJ
VD = NG + NJ
XW = D + H
RW = D + 2 * H
UW = D + 1
BIG = 1.0e30
NO_EDGE_DST = float(NP + 800)
NOWHERE = -5000.0
SKIP = 60000.0
SLOPE = 0.2
EPS = 1e-5
LAST_EDGES = E - (P - 1) * EB


class Chain:

    def __init__(self, eng, sem, base=0):
        self.eng, self.sem, self.n = eng, sem, base

    def __call__(self, ins):
        self.n += 1
        ins.then_inc(self.sem, 1)
        self.eng.wait_ge(self.sem, self.n)


def back(it, par, k, ways):
    return (par - k) % ways, it + (par - k) // ways


def build(nc, x, src, dst, edge_weight, W0, b0, gat, out):
    top = ExitStack()

    def sb(name, shape, dt):
        return top.enter_context(nc.sbuf_tensor(name, shape, dt))

    def dram(name, shape, dt):
        return nc.dram_tensor(name, shape, dt)

    def group_of(value, most):
        return nc.s_assert_within(value, 0, most, skip_runtime_bounds_check_because="visit v is at tile j(v) <= v, and groups + tiles - 1 visits leave v - j(v) < groups")

    stage_no = [0]

    def stage():
        stage_no[0] += 1
        k = stage_no[0]
        ctx = ExitStack()
        sems = []

        def clear():
            nc.clear_and_free_semaphores(sems)
            nc.all_engine_barrier()

        ctx.callback(clear)

        def sem(name):
            sems.append(nc.alloc_semaphore(name=f"s{k}_{name}"))
            return sems[-1]

        ps = lambda name, shape: ctx.enter_context(nc.psum_tensor(f"p{k}_{name}", shape, FP32))
        return ctx, sem, ps

    with top:
        src_d = dram("src_sorted", [EB, P], FP32)
        dst_d = dram("dst_sorted", [EB, P], FP32)
        prev_d = dram("prev_dst", [EB, P], FP32)
        pos_d = dram("position", [EB, P], FP32)
        w_d = dram("weight", [EB, P], FP32)
        step_d = dram("step_tables", [1, NI + 2 * P], I32)
        loc_d = dram("local_rows", [NI, P], BF16)
        sup_d = dram("rows_by_src", [EP, UW], FP32)
        tab_d = dram("gather_table", [NP, XW], FP32)
        spill_d = dram("gathered", [NG, P, G * RW], FP32)
        sum_d = dram("chunk_summary", [P, 5], FP32)
        carry_d = dram("chunk_carry", [2, P], FP32)

        iota_row = sb("iota_row", [P, P], FP32)
        iota_p = sb("iota_p", [P, 1], FP32)
        ident = sb("ident", [P, P], FP32)
        before = sb("before", [P, P], FP32)
        ones = sb("ones", [P, P], FP32)
        step_no = sb("step_no", [P, G], FP32)
        tile_no = sb("tile_no", [P, NT], FP32)

        X = sb("X", [P, NT * D], FP32)
        Xv = X[:, :].rearrange("p (t d) -> p t d", d=D)
        gath = sb("gath", [P, 4 * G * RW], FP32)
        GATH = gath[:, :].rearrange("p (s g w) -> p s g w", s=4, g=G)
        node = sb("node", [P, 3 * NT * RW // 2], FP32)
        PARTS = node[:, :].bitcast(BF16).rearrange("p (k t w) -> p k t w", k=3, t=NT)
        ACC = node[:, 0:NT * RW].rearrange("p (t w) -> p t w", t=NT)
        SUP = node[:, 0:NT * D].rearrange("p (t d) -> p t d", t=NT)
        DSTM = sb("DSTM", [P, NI], FP32)
        WGT = sb("WGT", [P, NI], FP32)
        RESET = sb("RESET", [P, NI], FP32)
        MASK = sb("MASK", [P, NI], FP32)
        START = sb("START", [P, NI], FP32)
        SRCI = sb("SRCI", [P, NI], I32)
        POSI = sb("POSI", [P, NI], I32)
        JROW = sb("JROW", [1, NI + 2 * P], I32)
        FIRST = sb("FIRST", [P, 2, P], FP32)
        arena = sb("arena", [P, 5 * NI * H + 8], FP32)
        SC = arena[:, 0:NI * H]
        SELF = arena[:, NI * H:2 * NI * H]
        RST = arena[:, 2 * NI * H:3 * NI * H + 1]
        EX = arena[:, 3 * NI * H + 8:5 * NI * H + 8]
        D1 = EX[:, 0:NI * H]
        FW = EX[:, NI * H:2 * NI * H]
        LBC = sb("LBC", [P, 2, G * P], BF16)
        OHT = sb("OHT", [P, 2, G * P], BF16)
        OH = sb("OH", [P, 2, G, P], FP32)
        work = sb("work", [P, 4 * G * XW], FP32)
        Z = work[:, 0:2 * G * XW].rearrange("p (s w) -> p s w", s=2)
        T = work[:, 2 * G * XW:].rearrange("p (s w) -> p s w", s=2)
        GIDX = sb("GIDX", [P, 4, G], I32)

        ctx, sem, ps = stage()
        with ctx:
            M = node[:, 0:NT * EB]
            CUM = arena[:, 0:NT * EB]
            tmp_w = work
            SIi = tmp_w[:, 0:EB].bitcast(I32)
            DIi = tmp_w[:, EB:2 * EB].bitcast(I32)
            WL = tmp_w[:, 2 * EB:3 * EB]
            SF = tmp_w[:, 3 * EB:4 * EB]
            DF = tmp_w[:, 4 * EB:5 * EB]
            PV = tmp_w[:, 5 * EB:6 * EB]
            BK = tmp_w[:, 6 * EB:7 * EB]
            POS = tmp_w[:, 7 * EB:8 * EB]
            JUNK = tmp_w[:, 8 * EB:9 * EB]
            small = ctx.enter_context(nc.sbuf_tensor("prep_small", [P, 400], FP32))
            PC = small[:, 0:1].bitcast(I32)
            RT = small[:, 8:8 + NT]
            CD = small[:, 40:40 + NT + NJ]
            OFF = small[:, 96:96 + NT]
            BI = small[:, 128:128 + 2 * NJ].bitcast(I32)
            BI2 = small[:, 176:176 + 2 * NJ].bitcast(I32)
            BND = small[:, 224:224 + 2 * NJ]
            VB = small[:, 344:344 + 2 * NJ]
            VBI = small[:, 176:176 + 2 * NJ].bitcast(I32)
            VBJ = small[:, 128:128 + 2 * NJ].bitcast(I32)
            JC = small[:, 280:280 + G + 2]
            JI = small[:, 296:296 + G + 2].bitcast(I32)
            BIX = small[:, 312:312 + G].bitcast(I32)
            BF = small[:, 320:320 + G]
            J128 = small[:, 328:328 + G]
            rows = arena[:, NT * EB:NT * EB + 10 * G * P].rearrange("p (k g q) -> p k g q", k=10, g=G)
            PS, PD, PP, PW, PV2, VAL, ST, RS, MK, LC = [rows[0:IR, k] for k in range(10)]
            LB16 = ctx.enter_context(nc.sbuf_tensor("loc16", [P, G, P], BF16))
            TI = FIRST[:, :, :].rearrange("p k v -> p (k v)").bitcast(I32)
            psum_off = ps("off", [P, 512])
            psum_bnd = ps("bnd", [P, 512])
            psum_tr = [ps(f"tr{k}", [P, 512]) for k in range(4)]

            pad_set, loaded, x_loaded = sem("pad_set"), sem("loaded"), sem("x_loaded")
            consts, chain = sem("consts"), sem("chain")
            edges_ready, edges_stored = sem("edges_ready"), sem("edges_stored")
            counts_ready, sums_ready = sem("counts_ready"), sem("sums_ready")
            steps_ready, steps_stored, steps_back = sem("steps_ready"), sem("steps_stored"), sem("steps_back")
            rows_in, rows_ready = sem("rows_in"), sem("rows_ready")
            loc_stored, trans, evac = sem("loc_stored"), sem("trans"), sem("evac")
            with nc.Block() as block:

                @block.sync
                def _(sp):
                    sp.wait_ge(pad_set, 1)
                    for tile, flat in ((SIi, src), (DIi, dst), (WL, edge_weight)):
                        sp.dma_start(tile[0:P - 1, :], flat[0:(P - 1) * EB].rearrange("(p c) -> p c", c=EB)).then_inc(loaded, 16)
                        sp.dma_start(tile[P - 1:P, 0:LAST_EDGES],
                                     flat[(P - 1) * EB:E].rearrange("(a c) -> a c", a=1)).then_inc(loaded, 16)
                    sp.dma_start(PC[1:P, :], dst[0:(P - 1) * EB].rearrange("(p c) -> p c", c=EB)[:, EB - 1:EB],
                                 allow_slow_non_contiguous=True).then_inc(loaded, 16)
                    sp.dma_start(Xv[:, 0:NT - 1, :], x[0:(NT - 1) * P, :].rearrange("(t p) d -> p t d", p=P)).then_inc(x_loaded, 16)
                    sp.dma_start(Xv[0:TAIL, NT - 1, :], x[(NT - 1) * P:N, :]).then_inc(x_loaded, 16)
                    sp.wait_ge(edges_ready, 1)
                    for arr, flat in ((SF, src_d), (DF, dst_d), (PV, prev_d), (WL, w_d)):
                        sp.dma_start(flat[:, :].rearrange("b q -> (b q)").rearrange("(p c) -> p c", c=EB), arr).then_inc(edges_stored, 16)
                    sp.dma_start(sup_d[E:E + P, :], arena[:, 0:UW]).then_inc(edges_stored, 16)
                    sp.dma_start(sup_d[E + P:EP, :], arena[0:EP - E - P, 0:UW]).then_inc(edges_stored, 16)
                    sp.wait_ge(edges_ready, 2)
                    sp.dma_start(pos_d[:, :].rearrange("b q -> (b q)").rearrange("(p c) -> p c", c=EB), POS).then_inc(edges_stored, 16)
                    sp.wait_ge(steps_ready, 3)
                    sp.dma_start(step_d[0, 0:NI].rearrange("(g p) -> p g", p=IR), JI[0:IR, 0:G],
                                 allow_slow_non_contiguous=True).then_inc(steps_stored, 16)
                    sp.dma_start(step_d[0, NI:].rearrange("(k p) -> p k", p=P), JI[:, G:G + 2],
                                 allow_slow_non_contiguous=True).then_inc(steps_stored, 16)
                    sp.wait_ge(steps_stored, 32)
                    sp.dma_start(JROW[0:1, :], step_d[:, :]).then_inc(steps_back, 16)
                    sp.dma_start(TI, step_d[:, NI:].broadcast_to([P, 2 * P])).then_inc(steps_back, 16)
                    sp.wait_ge(rows_ready, 1)
                    sp.dma_start(loc_d[:, :].rearrange("(g p) q -> p g q", p=IR), LB16[0:IR, :, :]).then_inc(loc_stored, 16)
                    sp.wait_ge(loc_stored, 16)
                    sp.wait_ge(steps_back, 32)

                @block.gpsimd
                def _(pool):
                    IMP = dict(allow_small_or_imprecise_dtypes=True)
                    pool.iota(tile_no[:, :], pattern=[[1, NT]], base=0, channel_multiplier=0, **IMP).then_inc(consts, 1)
                    pool.memset(ones[:, :], 1.0).then_inc(consts, 1)
                    pool.memset(ident[:, :], 0.0).then_inc(consts, 1)
                    pool.memset(before[:, :], 0.0).then_inc(consts, 1)
                    pool.iota(iota_row[:, :], pattern=[[1, P]], base=0, channel_multiplier=0, **IMP).then_inc(consts, 1)
                    pool.iota(iota_p[:, :], pattern=[[0, 1]], base=0, channel_multiplier=1, **IMP).then_inc(consts, 1)
                    pool.iota(step_no[:, :], pattern=[[IR, G]], base=0, channel_multiplier=1, **IMP).then_inc(consts, 1)
                    pool.wait_ge(consts, 7)
                    pool.affine_select(out=ident[:, :], in_=ident[:, :], compare_op=ALU.not_equal, fill=1.0, base=0,
                                       pattern=[[-1, P]], channel_multiplier=1).then_inc(consts, 1)
                    pool.affine_select(out=before[:, :], in_=before[:, :], compare_op=ALU.is_ge, fill=1.0, base=0,
                                       pattern=[[-1, P]], channel_multiplier=1).then_inc(consts, 1)
                    pool.wait_ge(edges_stored, 7 * 16)
                    pool.wait_ge(steps_ready, 2)
                    pool.nop(nofuse=True)
                    for row, flat in ((PS, src_d), (PD, dst_d), (PV2, prev_d), (PW, w_d), (PP, pos_d)):
                        for g in range(G):
                            pool.indirect_dma_start(row[:, g, :], None, flat[:, :],
                                                    bass.IndirectOffsetOnAxis(BIX[0:IR, g:g + 1], 0)).then_inc(rows_in, 16)

                @block.vector
                def _(dve):
                    link = Chain(dve, chain)
                    dve.memset(DIi, int(NO_EDGE_DST))
                    dve.memset(SIi, NP)
                    dve.memset(PC, -1)
                    dve.memset(CD, 0.0)
                    dve.memset(arena[:, 0:UW], 0.0)
                    link(dve.memset(WL, 0.0))
                    dve.memset(X[:, (NT - 1) * D:], 0.0).then_inc(pad_set, 1)
                    dve.wait_ge(loaded, 7 * 16)
                    link(dve.tensor_copy(DF, DIi))
                    dve.tensor_copy(PV[:, 0:1], PC)
                    dve.tensor_copy(PV[:, 1:EB], DF[:, 0:EB - 1])
                    link(dve.tensor_copy(SF, SIi))
                    link(dve.tensor_scalar(DIi, SIi, 7, None, ALU.arith_shift_right))
                    dve.tensor_copy(BK, DIi).then_inc(edges_ready, 1)
                    dve.wait_ge(edges_ready, 1)
                    dve.wait_ge(consts, 9)
                    Mv = M.rearrange("p (k c) -> p k c", c=EB)
                    link(dve.tensor_tensor(Mv, BK.unsqueeze(1).broadcast_to([P, NT, EB]),
                                           tile_no[:, :].unsqueeze(2).broadcast_to([P, NT, EB]), ALU.is_equal))
                    dve.wait_ge(edges_stored, 6 * 16)
                    link(dve.tensor_tensor_scan(CUM, ones[:, 0:1].broadcast_to([P, NT * EB]), M, 0.0, ALU.mult, ALU.add))
                    CUMv = CUM.rearrange("p (k c) -> p k c", c=EB)
                    ends = CUMv[:, :, EB - 1]
                    link(dve.tensor_copy(CD[:, 1:NT], ends[:, 0:NT - 1]))
                    link(dve.tensor_tensor(RT, ends, CD[:, 0:NT], ALU.subtract))
                    for j in range(NJ):
                        link(dve.tensor_scalar(JUNK, DF, float(P * (j + 1)), 0.0, ALU.is_lt, ALU.add,
                                               accum_out=CD[:, NT + j:NT + j + 1]))
                    dve.tensor_copy(JUNK[:, 0:1], tile_no[:, 0:1]).then_inc(counts_ready, 1)
                    dve.wait_ge(counts_ready, 1)
                    dve.wait_ge(sums_ready, 1)
                    link(dve.scalar_tensor_tensor(OFF, psum_off[:, 0:NT], -1.0, CD[:, 0:NT], ALU.add, ALU.subtract))
                    for k in range(NT):
                        ins = dve.scalar_tensor_tensor(CUMv[:, k, :], CUMv[:, k, :], OFF[:, k:k + 1], Mv[:, k, :], ALU.add, ALU.mult)
                    link(ins)
                    dve.tensor_reduce(POS, CUM.rearrange("p (k c) -> p c k", c=EB), AX, ALU.add).then_inc(edges_ready, 1)
                    link(dve.tensor_copy(BI, psum_bnd[:, 0:2 * NJ]))
                    link(dve.tensor_scalar(BI2, BI, 7, None, ALU.arith_shift_right))
                    link(dve.tensor_copy(BND, BI2))
                    BNDv = BND.rearrange("p (w j) -> p w j", w=2)
                    link(dve.tensor_tensor(BNDv, BNDv, tile_no[:, 1:NT].unsqueeze(1).broadcast_to([P, 2, NJ]), ALU.add))
                    for g in range(G):
                        link(dve.tensor_scalar(JUNK[:, 0:NJ], BND[:, NJ:2 * NJ], step_no[:, g:g + 1], 0.0,
                                               ALU.is_le, ALU.add, accum_out=JC[:, g:g + 1]))
                    dve.tensor_tensor(BF, step_no[:, :], JC[:, 0:G], ALU.subtract).then_inc(steps_ready, 1)
                    dve.wait_ge(steps_ready, 1)
                    dve.tensor_copy(BIX, BF).then_inc(steps_ready, 1)
                    link(dve.tensor_copy(VBI[:, NJ:], BND[:, NJ:]))
                    link(dve.tensor_scalar(VBJ[:, NJ:], VBI[:, NJ:], 2, None, ALU.arith_shift_right))
                    link(dve.tensor_copy(VBI[:, 0:NJ], psum_bnd[:, 0:NJ]))
                    link(dve.tensor_scalar(VBJ[:, 0:NJ], VBI[:, 0:NJ], 9, None, ALU.arith_shift_right))
                    link(dve.tensor_copy(VB, VBJ))
                    VBv = VB.rearrange("p (w j) -> p w j", w=2)
                    link(dve.tensor_tensor(VBv, VBv, tile_no[:, 1:NT].unsqueeze(1).broadcast_to([P, 2, NJ]), ALU.add))
                    for w in range(2):
                        link(dve.tensor_scalar(JUNK[:, 0:NJ], VB[:, w * NJ:(w + 1) * NJ], iota_p[:, 0:1], 0.0,
                                               ALU.is_le, ALU.add, accum_out=JC[:, G + w:G + w + 1]))
                    dve.tensor_copy(JI, JC).then_inc(steps_ready, 1)
                    link(dve.tensor_scalar(J128, JC[:, 0:G], float(P), None, ALU.mult))
                    dve.wait_ge(rows_in, 20 * 16)
                    for g in range(G):
                        ins = dve.tensor_scalar(LC[:, g, :], PD[:, g, :], J128[0:IR, g:g + 1], None, ALU.subtract)
                    link(ins)
                    link(dve.tensor_scalar(VAL, LC, 0.0, None, ALU.is_ge))
                    link(dve.scalar_tensor_tensor(VAL, LC, float(P), VAL, ALU.is_lt, ALU.mult))
                    link(dve.tensor_tensor(ST, PD, PV2, ALU.not_equal))
                    link(dve.tensor_tensor(ST, ST, VAL, ALU.mult))
                    dve.tensor_scalar(RS, ST, -BIG, None, ALU.mult)
                    dve.tensor_scalar(MK, VAL, -1.0, BIG, ALU.add, ALU.mult)
                    dve.scalar_tensor_tensor(PV2, PD, -NOWHERE, VAL, ALU.add, ALU.mult)
                    dve.tensor_scalar(PS, PS, float(NP - 1), None, ALU.min)
                    link(dve.scalar_tensor_tensor(PP, PP, -SKIP, VAL, ALU.add, ALU.mult))
                    dve.tensor_scalar(PP, PP, SKIP, None, ALU.add)
                    link(dve.tensor_scalar(PV2, PV2, NOWHERE, None, ALU.add))
                    dve.tensor_copy(LB16[0:IR, :, :], LC).then_inc(rows_ready, 1)
                    dve.wait_ge(rows_ready, 1)
                    for k, col in enumerate((DSTM, SRCI, POSI, WGT, RESET, MASK, START)):
                        dve.wait_ge(trans, k + 1)
                        dve.tensor_copy(col[:, :], psum_tr[k % 4][:, 0:NI]).then_inc(evac, 1)

                @block.tensor
                def _(pe):
                    pe.wait_ge(counts_ready, 1)
                    pe.matmul(psum_off[:, 0:NT], before[:, :], RT, start=True, stop=False)
                    pe.matmul(psum_off[:, 0:NT], ones[:, :], CD[:, 0:NT], start=False, stop=True)
                    pe.matmul(psum_bnd[:, 0:2 * NJ], ones[:, :], CD[:, 1:1 + 2 * NJ], start=True, stop=True).then_inc(sums_ready, 1)
                    pe.wait_ge(rows_ready, 1)
                    for k, row in enumerate((PV2, PS, PP, PW, RS, MK, ST)):
                        if k >= 4:
                            pe.wait_ge(evac, k - 3)
                        for g in range(G):
                            ins = pe.transpose(psum_tr[k % 4][:, g * IR:(g + 1) * IR], row[:, g, :], ident[0:IR, 0:IR])
                        ins.then_inc(trans, 1)

            with nc.Block() as block:
                scan_tr, scan_ev, ch2 = sem("scan_tr"), sem("scan_ev"), sem("ch2")
                res, parts = sem("res"), sem("parts")
                RX = arena[:, 0:NI * H].rearrange("p (r k h) -> p r k h", r=RUN, k=CHUNKS)
                R1 = EX[:, 0:NT * D]
                R1v = R1.rearrange("p (t d) -> p t d", d=D)

                @block.tensor
                def _(pe):
                    pe.wait_ge(res, 1)
                    for r in range(RUN):
                        b = r // 4
                        if b >= 4 and r % 4 == 0:
                            pe.wait_ge(scan_ev, b - 3)
                        ins = pe.transpose(psum_tr[b % 4][:, (r % 4) * P:(r % 4 + 1) * P],
                                           arena[:, r * P:(r + 1) * P], ident[:, :])
                        if r % 4 == 3 or r == RUN - 1:
                            ins.then_inc(scan_tr, 1)

                @block.vector
                def _(dve):
                    link = Chain(dve, ch2)
                    dve.memset(RST[:, NI * H:], 0.0)
                    link(dve.tensor_copy(T[:, 0, 0:2 * P], TI))
                    link(dve.tensor_scalar(FIRST[:, :, :].rearrange("p k v -> p (k v)"), T[:, 0, 0:2 * P], float(P), None, ALU.mult))
                    dve.tensor_copy(RX, RESET[:, :].rearrange("p (k r) -> p r k", k=CHUNKS).unsqueeze(3).broadcast_to([P, RUN, CHUNKS, H])).then_inc(res, 1)
                    for b in range(-(-RUN // 4)):
                        n = min(4, RUN - 4 * b) * P
                        dve.wait_ge(scan_tr, b + 1)
                        dve.tensor_copy(RST[:, b * 4 * P:b * 4 * P + n], psum_tr[b % 4][:, 0:n]).then_inc(scan_ev, 1)

                @block.gpsimd
                def _(pool):
                    pool.wait_ge(parts, 1)
                    pool.tensor_tensor(R1v, Xv, PARTS[:, 0, :, 0:D], ALU.subtract).then_inc(parts, 1)
                    pool.wait_ge(parts, 3)
                    pool.tensor_tensor(R1v, R1v, PARTS[:, 1, :, 0:D], ALU.subtract).then_inc(parts, 1)

                @block.scalar
                def _(act):
                    act.wait_ge(x_loaded, 32)
                    act.activation(PARTS[:, 0, :, 0:D], Xv, ACT.Copy).then_inc(parts, 1)
                    act.wait_ge(parts, 2)
                    act.activation(PARTS[:, 1, :, 0:D], R1v, ACT.Copy).then_inc(parts, 1)
                    act.wait_ge(parts, 4)
                    act.activation(PARTS[:, 2, :, 0:D], R1v, ACT.Copy)

        ctx, sem, ps = stage()
        with ctx:
            U = gath[:, 0:4 * G * UW].rearrange("p (s g w) -> p s g w", s=4, g=G)
            expd = [ps(f"expd{k}", [P, 2, 512]) for k in range(2)]
            loc_in = [sem(f"loc_in{k}") for k in range(2)]
            hot_ready, exp_ready, u_ready, idx_ready = sem("hot_ready"), sem("exp_ready"), sem("u_ready"), sem("idx_ready")
            src_ready = sem("src_ready")
            scattered = [sem(f"scattered{k}") for k in range(4)]
            turns = NG // 4
            with nc.Block() as block:

                def quads(eng, body):
                    body(0)
                    with eng.Fori(1, turns) as it:
                        body(it)

                @block.sync
                def _(sp):
                    def body(it):
                        for s in range(4):
                            q = 4 * it + s
                            if it is not 0 or s > 1:
                                sp.wait_ge(hot_ready, q - 1)
                            sp.dma_start(LBC[:, s % 2, :], loc_d[bass.ds(G * q, G), :].rearrange("g q -> (g q)").rearrange("(a n) -> a n", a=1)
                                         .broadcast_to([P, G * P])).then_inc(loc_in[s % 2], 16)
                    quads(sp, body)

                @block.vector
                def _(dve):
                    def body(it):
                        for s in range(4):
                            q = 4 * it + s
                            dve.wait_ge(loc_in[s % 2], 16 * (2 * it + s // 2 + 1))
                            if it is not 0 or s > 1:
                                dve.wait_ge(exp_ready, q - 1)
                            dve.tensor_scalar(OHT[:, s % 2, :], LBC[:, s % 2, :], iota_p[:, 0:1], None, ALU.is_equal).then_inc(hot_ready, 1)
                            if it is not 0:
                                dve.wait_ge(scattered[s], 64 * it)
                            dve.tensor_copy(U[:, s, :, D], SRCI[:, bass.ds(G * q, G)]).then_inc(src_ready, 1)
                            dve.tensor_copy(GIDX[:, s, :], POSI[:, bass.ds(G * q, G)]).then_inc(idx_ready, 1)
                    quads(dve, body)

                @block.tensor
                def _(pe):
                    def body(it):
                        for s in range(4):
                            q = 4 * it + s
                            pe.wait_ge(hot_ready, q + 1)
                            if it is not 0 or s > 1:
                                pe.wait_ge(u_ready, q - 1)
                            for g in range(G):
                                j = pe.value_load(JROW[0:1, bass.ds(G * q + g, 1)], min_val=0, max_val=NT - 1)
                                for k in range(3):
                                    ins = pe.matmul(expd[s % 2][:, g // 2, (g % 2) * D:(g % 2 + 1) * D], OHT[:, s % 2, g * P:(g + 1) * P],
                                                    PARTS[:, k, bass.ds(j, 1), 0:D], start=(k == 0), stop=(k == 2))
                            ins.then_inc(exp_ready, 1)
                    quads(pe, body)

                @block.scalar
                def _(act):
                    def body(it):
                        for s in range(4):
                            q = 4 * it + s
                            act.wait_ge(exp_ready, q + 1)
                            if it is not 0:
                                act.wait_ge(scattered[s], 64 * it)
                            for g in range(G):
                                ins = act.activation(U[:, s, g, 0:D], expd[s % 2][:, g // 2, (g % 2) * D:(g % 2 + 1) * D], ACT.Copy,
                                                     scale=WGT[:, bass.ds(G * q + g, 1)])
                            ins.then_inc(u_ready, 1)
                    quads(act, body)

                @block.gpsimd
                def _(pool):
                    def body(it):
                        for s in range(4):
                            q = 4 * it + s
                            pool.wait_ge(idx_ready, q + 1)
                            pool.wait_ge(u_ready, q + 1)
                            pool.wait_ge(src_ready, q + 1)
                            pool.nop(nofuse=True)
                            for g in range(G):
                                pool.indirect_dma_start(sup_d[:, :], bass.IndirectOffsetOnAxis(GIDX[:, s, g:g + 1], 0), U[:, s, g, :], None,
                                                        bounds_check=EP - 1, oob_is_err=False).then_inc(scattered[s], 16)
                    quads(pool, body)
                    for s in range(4):
                        pool.wait_ge(scattered[s], 64 * turns)

        ctx, sem, ps = stage()
        with ctx:
            U = gath[:, 0:4 * G * UW].rearrange("p (s g w) -> p s g w", s=4, g=G)
            LS = ctx.enter_context(nc.sbuf_tensor("src_local", [P, 2, G], FP32))
            sums = [ps(f"sums{k}", [P, 512]) for k in range(4)]
            rows_in = [sem(f"rows_in{k}") for k in range(4)]
            cleared, loc_ready, hot_ready, sum_ready, added = (sem("cleared"), sem("loc_ready"), sem("hot_ready"),
                                                               sem("sum_ready"), sem("added"))
            turns = VS // 4
            sup_rows = sup_d[:, :].rearrange("(m g p) w -> m p g w", g=G, p=P)
            with nc.Block() as block:

                def visits(eng, one):
                    for s in range(4):
                        one(s, s, 0, s)
                    with eng.Fori(1, turns) as it:
                        for s in range(4):
                            one(4 * it + s, s, it, 4)
                    for v in range(4 * turns, VS):
                        one(v, v % 4, turns, 4)

                @block.sync
                def _(sp):
                    def one(v, s, turn, past):
                        j = sp.value_load(JROW[0:1, bass.ds(NI + v, 1)], min_val=0, max_val=NJ)
                        m = group_of(v - j, EB // G - 1)
                        if past == 4:
                            sp.wait_ge(sum_ready, v - 3)
                        sp.dma_start(U[:, s], sup_rows[bass.ds(m, 1)].rearrange("a p g w -> (a p) g w")).then_inc(rows_in[s], 16)
                    visits(sp, one)

                @block.vector
                def _(dve):
                    dve.memset(SUP, 0.0).then_inc(cleared, 1)
                    dve.wait_ge(cleared, 1)

                    def hots(v, s, turn, past):
                        dve.wait_ge(rows_in[s], 16 * (turn + 1))
                        if past >= 2:
                            dve.wait_ge(sum_ready, v - 1)
                        dve.tensor_tensor(LS[:, s % 2, :], U[:, s, :, D], FIRST[:, 0, bass.ds(v, 1)].broadcast_to([P, G]), ALU.subtract).then_inc(loc_ready, 1)
                        dve.wait_ge(loc_ready, v + 1)
                        dve.tensor_tensor(OH[:, s % 2], iota_row[:, :].unsqueeze(1).broadcast_to([P, G, P]),
                                          LS[:, s % 2, :].unsqueeze(2).broadcast_to([P, G, P]), ALU.is_equal).then_inc(hot_ready, 1)

                    def add(v, s, past):
                        j = dve.value_load(JROW[0:1, bass.ds(NI + v, 1)], min_val=0, max_val=NJ)
                        dve.wait_ge(sum_ready, v + 1)
                        if past:
                            dve.wait_ge(added, v)
                        dve.tensor_tensor(SUP[:, bass.ds(j, 1), :], SUP[:, bass.ds(j, 1), :], sums[s][:, 0:D].unsqueeze(1), ALU.add).then_inc(added, 1)

                    def one(v, s, turn, past):
                        hots(v, s, turn, past)
                        if past:
                            add(v - 1, (s - 1) % 4, past - 1)
                    visits(dve, one)
                    add(VS - 1, (VS - 1) % 4, 3)

                @block.tensor
                def _(pe):
                    def one(v, s, turn, past):
                        pe.wait_ge(hot_ready, v + 1)
                        if past == 4:
                            pe.wait_ge(added, v - 3)
                        for g in range(G):
                            ins = pe.matmul(sums[s][:, 0:D], OH[:, s % 2, g, :], U[:, s, g, 0:D], start=(g == 0), stop=(g == G - 1))
                        ins.then_inc(sum_ready, 1)
                    visits(pe, one)

        WB = sb("WB", [P, 4 * D], FP32)
        VEC = sb("VEC", [P, 3, D], FP32)
        STATS = sb("STATS", [P, NT, 8], FP32)
        MOM = sb("MOM", [P, NT, 2], FP32)
        RSTD = sb("RSTD", [P, NT, 2], FP32)
        x1_d = dram("x1", [NP, D], FP32)

        def by_tile(eng, one):
            one(0, 0, 0, True)
            one(1, 1, 0, True)
            with eng.Fori(1, NT // 2) as it:
                one(2 * it, 0, it, False)
                one(2 * it + 1, 1, it, False)
            one(NT - 1, 0, NT // 2, False)

        XS = gath[:, 0:4 * D].rearrange("p (s w) -> p s w", s=2)
        XT = gath[:, 4 * D:8 * D].rearrange("p (s w) -> p s w", s=2)

        def layernorm(dve, moments, rooted, chain, count, normed):
            link = Chain(dve, chain, count)
            for t in range(NT):
                ins = dve.bn_stats(STATS[:, t, 0:6], Xv[:, t, :])
            link(ins)
            for t in range(NT):
                ins = dve.bn_aggr(MOM[:, t, :], STATS[:, t, 0:6])
            link(ins)
            dve.tensor_scalar(MOM[:, :, 1], MOM[:, :, 1], EPS, None, ALU.add).then_inc(moments, 1)
            dve.wait_ge(rooted, 1)
            link(dve.reciprocal(RSTD[:, :, 1], RSTD[:, :, 0]))
            for t in range(NT):
                ins = dve.tensor_scalar(Xv[:, t, :], Xv[:, t, :], MOM[:, t, 0:1], RSTD[:, t, 1:2], ALU.subtract, ALU.mult)
            ins.then_inc(normed, 1)

        ctx, sem, ps = stage()
        with ctx:
            psum_t = [ps(f"t{k}", [P, 512]) for k in range(2)]
            psum_o = [ps(f"o{k}", [P, 512]) for k in range(2)]
            w_in, copied, transposed, evacuated, product, chain, moments, rooted, normed, stored = (
                sem("w_in"), sem("copied"), sem("transposed"), sem("evacuated"), sem("product"), sem("chain"),
                sem("moments"), sem("rooted"), sem("normed"), sem("stored"))
            O = work[:, 0:2 * D].rearrange("p (s d) -> p s d", s=2)
            with nc.Block() as block:

                @block.sync
                def _(sp):
                    sp.dma_start(WB[:, :].rearrange("p (k n) -> p k n", k=4), W0.rearrange("(k p) n -> p k n", p=P)).then_inc(w_in, 16)
                    sp.dma_start(VEC[:, 0, :], b0.rearrange("(a n) -> a n", a=1).broadcast_to([P, D])).then_inc(w_in, 16)
                    sp.wait_ge(normed, 1)
                    sp.dma_start(x1_d[:, :].rearrange("(t p) d -> p t d", p=P), Xv).then_inc(stored, 16)
                    sp.wait_ge(stored, 16)

                @block.scalar
                def _(act):
                    def one(q, s, turn, first):
                        if not first:
                            act.wait_ge(transposed, q - 1)
                        act.activation(XS[:, s, 0:D], Xv[:, bass.ds(q, 1), :], ACT.Copy).then_inc(copied, 1)
                        act.activation(XS[:, s, D:2 * D], SUP[:, bass.ds(q, 1), :], ACT.Copy).then_inc(copied, 1)
                        act.wait_ge(transposed, q + 1)
                        if not first:
                            act.wait_ge(product, q - 1)
                        act.activation(XT[:, s, :], psum_t[s][:, :], ACT.Copy).then_inc(evacuated, 1)
                    by_tile(act, one)
                    act.wait_ge(moments, 1)
                    act.activation(RSTD[:, :, 0], MOM[:, :, 1], ACT.Sqrt).then_inc(rooted, 1)

                @block.gpsimd
                def _(pool):
                    pool.memset(gath[:, 8 * D:], 0.0)

                @block.tensor
                def _(pe):
                    pe.wait_ge(w_in, 32)

                    def one(q, s, turn, first):
                        pe.wait_ge(copied, 2 * q + 2)
                        if not first:
                            pe.wait_ge(evacuated, q - 1)
                        for k in range(4):
                            ins = pe.transpose(psum_t[s][:, k * P:(k + 1) * P], XS[:, s, k * P:(k + 1) * P], ident[:, :])
                        ins.then_inc(transposed, 1)
                        pe.wait_ge(evacuated, q + 1)
                        if not first:
                            pe.wait_ge(chain, 2 * (q - 1))
                        for k in range(4):
                            ins = pe.matmul(psum_o[s][:, 0:D], XT[:, s, k * P:(k + 1) * P], WB[:, k * D:(k + 1) * D],
                                            start=(k == 0), stop=(k == 3))
                        ins.then_inc(product, 1)
                    by_tile(pe, one)

                @block.vector
                def _(dve):
                    dve.wait_ge(w_in, 32)

                    def one(q, s, turn, first):
                        link = Chain(dve, chain, 2 * q)
                        dve.wait_ge(product, q + 1)
                        link(dve.tensor_tensor(O[:, s, :], psum_o[s][:, 0:D], VEC[:, 0, :], ALU.add))
                        dve.wait_ge(copied, 2 * q + 2)
                        link(dve.scalar_tensor_tensor(Xv[:, bass.ds(q, 1), :], O[:, s, :].unsqueeze(1), 0.0, Xv[:, bass.ds(q, 1), :], ALU.max, ALU.add))
                    by_tile(dve, one)
                    layernorm(dve, moments, rooted, chain, 2 * NT, normed)

        for layer, (Wl, Wr, att, bias) in enumerate(gat):
            ctx, sem, ps = stage()
            with ctx:
                psum_t = [ps(f"t{k}", [P, 512]) for k in range(2)]
                psum_o = [ps(f"o{k}", [P, 512]) for k in range(2)]
                w_in, copied, transposed, evacuated, product, chain, att_ready, rows_copied, stored = (
                    sem("w_in"), sem("copied"), sem("transposed"), sem("evacuated"), sem("product"), sem("chain"),
                    sem("att_ready"), sem("rows_copied"), sem("stored"))
                rows_stored = [sem(f"rows_stored{k}") for k in range(2)]
                parts = sem("parts")
                LR = work[:, 0:4 * RW].rearrange("p (s k w) -> p s k w", s=2, k=2)
                PR = work[:, 4 * RW:4 * RW + 4 * D].rearrange("p (s k w) -> p s k w", s=2, k=2)
                RES = gath[:, 8 * D:8 * D + 2 * RW].rearrange("p (s w) -> p s w", s=2)
                S8 = gath[:, 8 * D + 2 * RW:8 * D + 2 * RW + 2 * H].rearrange("p (s w) -> p s w", s=2)
                STEPS = 7
                with nc.Block() as block:

                    @block.sync
                    def _(sp):
                        WBv = WB[:, :].rearrange("p (k n) -> p k n", k=2)
                        sp.dma_start(WBv[:, :, 0:D], Wl.rearrange("(k p) n -> p k n", p=P)).then_inc(w_in, 16)
                        sp.dma_start(WBv[:, :, D:2 * D], Wr.rearrange("(k p) n -> p k n", p=P)).then_inc(w_in, 16)
                        sp.dma_start(VEC[:, 0, :], bias.rearrange("(a n) -> a n", a=1).broadcast_to([P, D])).then_inc(w_in, 16)
                        sp.dma_start(VEC[:, 2, :], att.rearrange("h c -> (h c)").rearrange("(a n) -> a n", a=1).broadcast_to([P, D])).then_inc(w_in, 16)

                        def one(q, s, turn, first):
                            sp.wait_ge(chain, STEPS * q + 2)
                            sp.dma_start(tab_d[bass.ds(P * q, P), :], LR[:, s, 0, 0:XW]).then_inc(rows_stored[s], 16)
                        by_tile(sp, one)
                        sp.wait_ge(rows_stored[0], 16 * (NT - NT // 2))
                        sp.wait_ge(rows_stored[1], 16 * (NT // 2))

                    @block.scalar
                    def _(act):
                        def one(q, s, turn, first):
                            if not first:
                                act.wait_ge(transposed, q - 1)
                            act.activation(XS[:, s, 0:D], Xv[:, bass.ds(q, 1), :], ACT.Copy).then_inc(copied, 1)
                            act.wait_ge(transposed, q + 1)
                            if not first:
                                act.wait_ge(product, q - 1)
                            act.activation(XT[:, s, 0:D], psum_t[s][:, 0:D], ACT.Copy).then_inc(evacuated, 1)
                            act.wait_ge(product, q + 1)
                            if not first:
                                act.wait_ge(parts, 5 * (q - 1))
                                act.wait_ge(rows_stored[s], 16 * turn)
                            act.activation(LR[:, s, :, 0:D], psum_o[s][:, :].rearrange("p (k d) -> p k d", k=2), ACT.Copy).then_inc(rows_copied, 1)
                            act.wait_ge(chain, STEPS * (q + 1))
                            act.activation(PARTS[:, 0, bass.ds(q, 1), :], LR[:, s, 1, :].unsqueeze(1), ACT.Copy).then_inc(parts, 1)
                            act.wait_ge(parts, 5 * q + 2)
                            act.activation(PARTS[:, 1, bass.ds(q, 1), :], RES[:, s, :].unsqueeze(1), ACT.Copy).then_inc(parts, 1)
                            act.wait_ge(parts, 5 * q + 4)
                            act.activation(PARTS[:, 2, bass.ds(q, 1), :], RES[:, s, :].unsqueeze(1), ACT.Copy).then_inc(parts, 1)
                        by_tile(act, one)

                    @block.gpsimd
                    def _(pool):
                        def one(q, s, turn, first):
                            pool.wait_ge(parts, 5 * q + 1)
                            pool.tensor_tensor(RES[:, s, :].unsqueeze(1), LR[:, s, 1, :].unsqueeze(1), PARTS[:, 0, bass.ds(q, 1), :], ALU.subtract).then_inc(parts, 1)
                            pool.wait_ge(parts, 5 * q + 3)
                            pool.tensor_tensor(RES[:, s, :].unsqueeze(1), RES[:, s, :].unsqueeze(1), PARTS[:, 1, bass.ds(q, 1), :], ALU.subtract).then_inc(parts, 1)
                        by_tile(pool, one)

                    @block.tensor
                    def _(pe):
                        pe.wait_ge(w_in, 64)

                        def one(q, s, turn, first):
                            pe.wait_ge(copied, q + 1)
                            if not first:
                                pe.wait_ge(evacuated, q - 1)
                            for k in range(2):
                                ins = pe.transpose(psum_t[s][:, k * P:(k + 1) * P], XS[:, s, k * P:(k + 1) * P], ident[:, :])
                            ins.then_inc(transposed, 1)
                            pe.wait_ge(evacuated, q + 1)
                            if not first:
                                pe.wait_ge(rows_copied, q - 1)
                            for k in range(2):
                                ins = pe.matmul(psum_o[s][:, :], XT[:, s, k * P:(k + 1) * P], WB[:, 2 * k * D:2 * (k + 1) * D],
                                                start=(k == 0), stop=(k == 1))
                            ins.then_inc(product, 1)
                        by_tile(pe, one)

                    @block.vector
                    def _(dve):
                        dve.wait_ge(w_in, 64)
                        dve.tensor_scalar(VEC[:, 1, :], VEC[:, 2, :], SLOPE, None, ALU.mult).then_inc(att_ready, 1)
                        dve.wait_ge(att_ready, 1)
                        dve.tensor_scalar(VEC[:, 2, :], VEC[:, 2, :], 1.0 - SLOPE, None, ALU.mult).then_inc(att_ready, 1)
                        dve.wait_ge(att_ready, 2)

                        def one(q, s, turn, first):
                            link = Chain(dve, chain, STEPS * q)
                            dve.wait_ge(rows_copied, q + 1)
                            link(dve.tensor_tensor(PR[:, s, :, :], LR[:, s, :, 0:D], VEC[:, 1, :].unsqueeze(1).broadcast_to([P, 2, D]), ALU.mult))
                            link(dve.tensor_reduce(LR[:, s, :, D:D + H], PR[:, s, :, :].rearrange("p k (h c) -> p k h c", c=C), AX, ALU.add))
                            link(dve.tensor_tensor(PR[:, s, 0, :], LR[:, s, 0, 0:D], LR[:, s, 1, 0:D], ALU.add))
                            link(dve.scalar_tensor_tensor(PR[:, s, 1, :], PR[:, s, 0, :], 0.0, VEC[:, 2, :], ALU.max, ALU.mult))
                            link(dve.tensor_reduce(S8[:, s, :], PR[:, s, 1, :].rearrange("p (h c) -> p h c", c=C), AX, ALU.add))
                            link(dve.tensor_tensor(S8[:, s, :], S8[:, s, :], LR[:, s, 0, D:D + H], ALU.add))
                            link(dve.tensor_tensor(LR[:, s, 1, D + H:RW], S8[:, s, :], LR[:, s, 1, D:D + H], ALU.add))
                        by_tile(dve, one)

            ctx, sem, ps = stage()
            with ctx:
                expd = [ps(f"expd{k}", [P, G, 512]) for k in range(2)]
                loc_in = [sem(f"loc_in{k}") for k in range(2)]
                gathered = [sem(f"gathered{k}") for k in range(4)]
                spilled = [sem(f"spilled{k}") for k in range(4)]
                hot_ready, exp_ready, idx_ready, z_ready, self_ready, relu_ready, weighted, scored = (
                    sem("hot_ready"), sem("exp_ready"), sem("idx_ready"), sem("z_ready"), sem("self_ready"),
                    sem("relu_ready"), sem("weighted"), sem("scored"))
                turns = NG // 4
                with nc.Block() as block:

                    def quads(eng, body):
                        body(0)
                        with eng.Fori(1, turns) as it:
                            body(it)

                    @block.gpsimd
                    def _(pool):
                        def body(it):
                            for s in range(4):
                                q = 4 * it + s
                                if it is not 0:
                                    pool.wait_ge(spilled[s], 16 * it)
                                    pool.wait_ge(z_ready, q - 3)
                                pool.wait_ge(idx_ready, q + 1)
                                pool.nop(nofuse=True)
                                for g in range(G):
                                    pool.indirect_dma_start(GATH[:, s, g, 0:XW], None, tab_d[:, :],
                                                            bass.IndirectOffsetOnAxis(GIDX[:, s, g:g + 1], 0)).then_inc(gathered[s], 16)
                        quads(pool, body)

                    @block.sync
                    def _(sp):
                        def spill(q, s, turn):
                            sp.wait_ge(gathered[s], 64 * (turn + 1))
                            sp.dma_start(spill_d[bass.ds(q, 1), :, :].rearrange("a p w -> (a p) w"), GATH[:, s].rearrange("p g w -> p (g w)")).then_inc(spilled[s], 16)

                        def body(it):
                            for s in range(4):
                                q = 4 * it + s
                                if not (it is 0 and s < 2):
                                    sp.wait_ge(hot_ready, q - 1)
                                sp.dma_start(LBC[:, s % 2, :], loc_d[bass.ds(G * q, G), :].rearrange("g q -> (g q)")
                                             .rearrange("(a n) -> a n", a=1).broadcast_to([P, G * P])).then_inc(loc_in[s % 2], 16)
                                if not (it is 0 and s < 2):
                                    ps_, turn = back(it, s, 2, 4)
                                    spill(q - 2, ps_, turn)
                        quads(sp, body)
                        spill(NG - 2, 2, turns - 1)
                        spill(NG - 1, 3, turns - 1)
                        for s in range(4):
                            sp.wait_ge(spilled[s], 16 * turns)

                    @block.tensor
                    def _(pe):
                        def body(it):
                            for s in range(4):
                                q = 4 * it + s
                                pe.wait_ge(hot_ready, q + 1)
                                if not (it is 0 and s < 2):
                                    pe.wait_ge(z_ready, q - 1)
                                    pe.wait_ge(self_ready, q - 1)
                                for g in range(G):
                                    j = pe.value_load(JROW[0:1, bass.ds(G * q + g, 1)], min_val=0, max_val=NT - 1)
                                    for k in range(3):
                                        ins = pe.matmul(expd[s % 2][:, g, 0:RW], OHT[:, s % 2, g * P:(g + 1) * P],
                                                        PARTS[:, k, bass.ds(j, 1), :], start=(k == 0), stop=(k == 2))
                                ins.then_inc(exp_ready, 1)
                        quads(pe, body)

                    @block.vector
                    def _(dve):
                        Zv = Z.rearrange("p s (g w) -> p s g w", g=G)
                        Tv = T.rearrange("p s (g h c) -> p s g h c", g=G, h=H)

                        def hots(q, s2, turn2, first):
                            dve.wait_ge(loc_in[s2], 16 * (turn2 + 1))
                            if not first:
                                dve.wait_ge(exp_ready, q - 1)
                            dve.tensor_scalar(OHT[:, s2, :], LBC[:, s2, :], iota_p[:, 0:1], None, ALU.is_equal).then_inc(hot_ready, 1)

                        def add(q, s4, turn4, first):
                            dve.wait_ge(gathered[s4], 64 * (turn4 + 1))
                            dve.wait_ge(exp_ready, q + 1)
                            if not first:
                                dve.wait_ge(relu_ready, 2 * (q - 1))
                            dve.tensor_tensor(Zv[:, s4 % 2], expd[s4 % 2][:, :, 0:XW], GATH[:, s4, :, 0:XW], ALU.add).then_inc(z_ready, 1)

                        def score(q, s2):
                            dve.wait_ge(relu_ready, 2 * q + 2)
                            TR = Tv[:, s2, :, :, 0:C]
                            dve.tensor_tensor(TR, TR, VEC[:, 2, :].rearrange("p (h c) -> p h c", h=H).unsqueeze(1).broadcast_to([P, G, H, C]),
                                              ALU.mult).then_inc(weighted, 1)
                            dve.wait_ge(weighted, q + 1)
                            dve.tensor_reduce(SC[:, bass.ds(G * H * q, G * H)], T[:, s2, :].rearrange("p (g c) -> p g c", c=C + 1),
                                              AX, ALU.add).then_inc(scored, 1)

                        def body(it):
                            for s in range(4):
                                q = 4 * it + s
                                at0 = it is 0
                                hots(q, s % 2, 2 * it + s // 2, at0 and s < 2)
                                if not (at0 and s < 1):
                                    b, turn = back(it, s, 1, 4)
                                    add(q - 1, b, turn, at0 and s < 3)
                                if not (at0 and s < 2):
                                    score(q - 2, s % 2)
                        quads(dve, body)
                        add(NG - 1, 3, turns - 1, False)
                        score(NG - 2, 0)
                        score(NG - 1, 1)

                    @block.scalar
                    def _(act):
                        Zv = Z.rearrange("p s (g w) -> p s g w", g=G)
                        Tv = T.rearrange("p s (g h c) -> p s g h c", g=G, h=H)

                        def body(it, ahead=True):
                            for s in range(4):
                                q = 4 * it + s
                                if ahead:
                                    act.wait_ge(gathered[s], 64 * (it + 1))
                                    act.activation(GIDX[:, s, :], SRCI[:, bass.ds(G * (q + 4), G)], ACT.Copy).then_inc(idx_ready, 1)
                                act.wait_ge(z_ready, q + 1)
                                if not (it is 0 and s < 2):
                                    act.wait_ge(scored, q - 1)
                                act.activation(SELF[:, bass.ds(G * H * q, G * H)].rearrange("p (g h) -> p g h", g=G),
                                               expd[s % 2][:, :, XW:RW], ACT.Copy).then_inc(self_ready, 1)
                                act.activation(Tv[:, s % 2, :, :, 0:C], Zv[:, s % 2, :, 0:D].rearrange("p g (h c) -> p g h c", h=H),
                                               ACT.Relu).then_inc(relu_ready, 1)
                                act.activation(Tv[:, s % 2, :, :, C], Zv[:, s % 2, :, D:XW], ACT.Copy).then_inc(relu_ready, 1)
                        for s in range(4):
                            act.activation(GIDX[:, s, :], SRCI[:, G * s:G * (s + 1)], ACT.Copy).then_inc(idx_ready, 1)
                        body(0)
                        with act.Fori(1, turns - 1) as it:
                            body(it)
                        body(turns - 1, ahead=False)

            ctx, sem, ps = stage()
            with ctx:
                psum_f = [ps(f"f{k}", [P, 512]) for k in range(4)]
                BANKS = -(-RUN // 4)
                W = NI * H
                SM = ctx.enter_context(nc.sbuf_tensor(f"summary{layer}", [P, 8], FP32))
                CR = ctx.enter_context(nc.sbuf_tensor(f"carries{layer}", [P, 2], FP32))
                KH = ctx.enter_context(nc.sbuf_tensor(f"by_head{layer}", [H, 10, CHUNKS], FP32))
                F2 = gath[:, 0:W]
                masked, to_rows, rows_ev, chain, summary, sum_in, carried, back_ready, to_cols, cols_ev, shifted, exped = (
                    sem("masked"), sem("to_rows"), sem("rows_ev"), sem("chain"), sem("summary"), sem("sum_in"), sem("carried"),
                    sem("back_ready"), sem("to_cols"), sem("cols_ev"), sem("shifted"), sem("exped"))
                carry_s = sem("carry_s")

                def krh(a):
                    return a.rearrange("p (k r h) -> p k r h", k=CHUNKS, r=RUN)

                def rkh(a):
                    return a.rearrange("p (r k h) -> p k r h", k=CHUNKS, r=RUN)

                with nc.Block() as block:

                    @block.vector
                    def _(dve):
                        link = Chain(dve, chain)
                        link(dve.tensor_tensor(SC.rearrange("p (i h) -> p i h", h=H), SC.rearrange("p (i h) -> p i h", h=H),
                                               MASK[:, :].unsqueeze(2).broadcast_to([P, NI, H]), ALU.add))
                        link(dve.tensor_tensor(SELF.rearrange("p (i h) -> p i h", h=H), SELF.rearrange("p (i h) -> p i h", h=H),
                                               MASK[:, :].unsqueeze(2).broadcast_to([P, NI, H]), ALU.add))
                        dve.tensor_tensor(rkh(FW), krh(SC), krh(SELF), ALU.max).then_inc(masked, 1)
                        dve.tensor_copy(SM[:, 4:5], RST[:, 0:1])
                        link(dve.tensor_reduce(SM[:, 1:2], RST[:, 0:W], AX, ALU.min))
                        link(dve.tensor_reduce(SM[:, 3:4], RST[:, 1:W], AX, ALU.min))
                        link(dve.memset(KH[:, :, :], -BIG))
                        dve.wait_ge(rows_ev, BANKS)
                        link(dve.tensor_tensor_scan(FW, RST[:, 0:W], D1, -BIG, ALU.add, ALU.max))
                        link(dve.tensor_copy(SM[:, 0:1], FW[:, W - 1:W]))
                        link(dve.tensor_tensor_scan(F2[:, ::-1], RST[:, 1:W + 1][:, ::-1], FW[:, ::-1], -BIG, ALU.add, ALU.max))
                        dve.tensor_copy(SM[:, 2:3], F2[:, 0:1]).then_inc(summary, 1)
                        dve.wait_ge(sum_in, 5 * 16)
                        last, low, first, low1, reset = [KH[:, k, :] for k in range(5)]
                        run, left, right, t0, t1 = [KH[:, k, :] for k in range(5, 10)]
                        K1 = CHUNKS - 1
                        link(dve.tensor_tensor_scan(run, low, last, -BIG, ALU.add, ALU.max))
                        link(dve.tensor_copy(left[:, 1:], run[:, 0:K1]))
                        link(dve.tensor_tensor(t0[:, 0:K1], low1[:, 0:K1], reset[:, 1:], ALU.add))
                        link(dve.tensor_tensor_scan(t1[:, ::-1], t0[:, ::-1], first[:, ::-1], -BIG, ALU.add, ALU.max))
                        link(dve.tensor_tensor(right[:, 0:K1], t1[:, 1:], reset[:, 1:], ALU.add))
                        dve.tensor_copy(t0, right).then_inc(carried, 1)
                        dve.wait_ge(back_ready, 2 * 16)
                        link(dve.tensor_tensor_scan(F2, RST[:, 0:W], D1, CR[:, 0:1], ALU.add, ALU.max))
                        dve.tensor_tensor_scan(D1[:, ::-1], RST[:, 1:W + 1][:, ::-1], F2[:, ::-1], CR[:, 1:2], ALU.add, ALU.max).then_inc(masked, 1)
                        dve.wait_ge(cols_ev, BANKS)
                        dve.tensor_tensor(krh(SC), krh(SC), rkh(FW), ALU.subtract)
                        dve.tensor_tensor(krh(SELF), krh(SELF), rkh(FW), ALU.subtract).then_inc(shifted, 1)
                        dve.wait_ge(exped, 2)
                        EXs = EX.rearrange("p (i w) -> p i w", w=2 * H)[:, :, H:2 * H]
                        dve.tensor_tensor(EXs, EXs, START[:, :].unsqueeze(2).broadcast_to([P, NI, H]), ALU.mult)

                    @block.tensor
                    def _(pe):
                        pe.wait_ge(masked, 1)
                        for r in range(RUN):
                            b = r // 4
                            if b >= 4 and r % 4 == 0:
                                pe.wait_ge(rows_ev, b - 3)
                            ins = pe.transpose(psum_f[b % 4][:, (r % 4) * P:(r % 4 + 1) * P], FW[:, r * P:(r + 1) * P], ident[:, :])
                            if r % 4 == 3 or r == RUN - 1:
                                ins.then_inc(to_rows, 1)
                        pe.wait_ge(masked, 2)
                        pe.wait_ge(rows_ev, BANKS)
                        for r in range(RUN):
                            b = r // 4
                            if b >= 4 and r % 4 == 0:
                                pe.wait_ge(cols_ev, b - 3)
                            ins = pe.transpose(psum_f[b % 4][:, (r % 4) * P:(r % 4 + 1) * P], D1[:, r * P:(r + 1) * P], ident[:, :])
                            if r % 4 == 3 or r == RUN - 1:
                                ins.then_inc(to_cols, 1)

                    @block.scalar
                    def _(act):
                        for dst_buf, full, done in ((D1, to_rows, rows_ev), (FW, to_cols, cols_ev)):
                            for b in range(BANKS):
                                n = min(4, RUN - 4 * b) * P
                                act.wait_ge(full, b + 1)
                                act.activation(dst_buf[:, b * 4 * P:b * 4 * P + n], psum_f[b % 4][:, 0:n], ACT.Copy).then_inc(done, 1)
                        EXv = EX.rearrange("p (i w) -> p i w", w=2 * H)
                        act.wait_ge(shifted, 1)
                        act.activation(EXv[:, :, 0:H], SC.rearrange("p (i h) -> p i h", h=H), ACT.Exp).then_inc(exped, 1)
                        act.activation(EXv[:, :, H:2 * H], SELF.rearrange("p (i h) -> p i h", h=H), ACT.Exp).then_inc(exped, 1)

                    @block.sync
                    def _(sp):
                        SLOW = dict(allow_slow_non_contiguous=True)
                        sp.wait_ge(summary, 1)
                        sp.dma_start(sum_d[:, :], SM[:, 0:5]).then_inc(carry_s, 16)
                        sp.wait_ge(carry_s, 16)
                        for k in range(5):
                            sp.dma_start(KH[:, k, :], sum_d[:, k].rearrange("(k h) -> h k", h=H), **SLOW).then_inc(sum_in, 16)
                        sp.wait_ge(carried, 1)
                        for k in range(2):
                            sp.dma_start(carry_d[k, :].rearrange("(k h) -> h k", h=H), KH[:, 6 + k, :], **SLOW).then_inc(carry_s, 16)
                        sp.wait_ge(carry_s, 48)
                        for k in range(2):
                            sp.dma_start(CR[:, k:k + 1], carry_d[k, :].rearrange("(p a) -> p a", a=1), **SLOW).then_inc(back_ready, 16)
                        sp.wait_ge(back_ready, 32)

            ctx, sem, ps = stage()
            with ctx:
                sums = [ps(f"sums{k}", [P, 512]) for k in range(4)]
                rows_in = [sem(f"rows_in{k}") for k in range(4)]
                LS = ctx.enter_context(nc.sbuf_tensor(f"dst_local{layer}", [P, 2, G], FP32))
                LD = ctx.enter_context(nc.sbuf_tensor(f"dst_visit{layer}", [P, 4, G], FP32))
                dst_ready = sem("dst_ready")
                cleared, loc_ready, hot_ready, sum_ready, added, weighted, weighted2, appended = (
                    sem("cleared"), sem("loc_ready"), sem("hot_ready"), sem("sum_ready"), sem("added"), sem("weighted"),
                    sem("weighted2"), sem("appended"))
                turns = VD // 4
                PG = 3
                EXv = EX.rearrange("p (i w) -> p i w", w=2 * H)
                with nc.Block() as block:

                    def quads(eng, body):
                        body(0)
                        with eng.Fori(1, turns) as it:
                            body(it)

                    def visit(eng, v):
                        j = eng.value_load(JROW[0:1, bass.ds(NI + P + v, 1)], min_val=0, max_val=NJ)
                        return j, group_of(v - j, NG - 1)

                    def weigh(eng, s, g0, g1):
                        V = GATH[:, s, g0:g1, 0:D].rearrange("p g (h c) -> p g h c", h=H)
                        return eng.tensor_tensor(V, V, GATH[:, s, g0:g1, D:D + H].unsqueeze(3).broadcast_to([P, g1 - g0, H, C]), ALU.mult)

                    @block.sync
                    def _(sp):
                        def body(it):
                            for s in range(4):
                                v = 4 * it + s
                                j, q = visit(sp, v)
                                if it is not 0:
                                    sp.wait_ge(sum_ready, v - 3)
                                sp.dma_start(GATH[:, s].rearrange("p g w -> p (g w)"), spill_d[bass.ds(q, 1), :, :].rearrange("a p w -> (a p) w")).then_inc(rows_in[s], 16)
                        quads(sp, body)

                    @block.gpsimd
                    def _(pool):
                        def body(it):
                            for s in range(4):
                                pool.wait_ge(appended, 4 * it + s + 1)
                                weigh(pool, s, 0, PG).then_inc(weighted, 1)
                        quads(pool, body)

                    @block.scalar
                    def _(act):
                        def body(it):
                            for s in range(4):
                                v = 4 * it + s
                                j, q = visit(act, v)
                                if it is not 0:
                                    act.wait_ge(loc_ready, v - 3)
                                act.activation(LD[:, s, :], DSTM[:, bass.ds(G * q, G)], ACT.Copy).then_inc(dst_ready, 1)
                                act.wait_ge(rows_in[s], 16 * (it + 1))
                                act.activation(GATH[:, s, :, D:RW], EXv[:, bass.ds(G * q, G), :], ACT.Copy).then_inc(appended, 1)
                        quads(act, body)

                    @block.tensor
                    def _(pe):
                        def body(it):
                            for s in range(4):
                                v = 4 * it + s
                                pe.wait_ge(hot_ready, v + 1)
                                pe.wait_ge(weighted, v + 1)
                                pe.wait_ge(appended, v + 1)
                                if it is not 0:
                                    pe.wait_ge(added, v - 3)
                                for g in range(G):
                                    ins = pe.matmul(sums[s][:, 0:RW], OH[:, s % 2, g, :], GATH[:, s, g, :], start=(g == 0), stop=(g == G - 1))
                                ins.then_inc(sum_ready, 1)
                        quads(pe, body)

                    @block.vector
                    def _(dve):
                        dve.memset(ACC, 0.0).then_inc(cleared, 1)
                        dve.wait_ge(cleared, 1)

                        def hots(v, s, it, first):
                            dve.wait_ge(dst_ready, v + 1)
                            if not first:
                                dve.wait_ge(sum_ready, v - 1)
                            dve.tensor_tensor(LS[:, s % 2, :], LD[:, s, :], FIRST[:, 1, bass.ds(v, 1)].broadcast_to([P, G]),
                                              ALU.subtract).then_inc(loc_ready, 1)
                            dve.wait_ge(appended, v + 1)
                            weigh(dve, s, PG, G).then_inc(weighted2, 1)
                            dve.wait_ge(loc_ready, v + 1)
                            dve.tensor_tensor(OH[:, s % 2], iota_row[:, :].unsqueeze(1).broadcast_to([P, G, P]),
                                              LS[:, s % 2, :].unsqueeze(2).broadcast_to([P, G, P]), ALU.is_equal).then_inc(hot_ready, 1)

                        def add(v, s, first):
                            j = dve.value_load(JROW[0:1, bass.ds(NI + P + v, 1)], min_val=0, max_val=NJ)
                            dve.wait_ge(sum_ready, v + 1)
                            if not first:
                                dve.wait_ge(added, v)
                            dve.tensor_tensor(ACC[:, bass.ds(j, 1), :], ACC[:, bass.ds(j, 1), :], sums[s][:, 0:RW].unsqueeze(1), ALU.add).then_inc(added, 1)

                        def body(it):
                            for s in range(4):
                                v = 4 * it + s
                                hots(v, s, it, it is 0 and s < 2)
                                if not (it is 0 and s < 1):
                                    add(v - 1, (s - 1) % 4, it is 0 and s < 2)
                        quads(dve, body)
                        add(VD - 1, 3, False)

            ctx, sem, ps = stage()
            with ctx:
                TB = gath[:, 0:2 * D].rearrange("p (s d) -> p s d", s=2)
                TO = gath[:, 2 * D:4 * D].rearrange("p (s d) -> p s d", s=2)
                TG = gath[:, 4 * D:6 * D].rearrange("p (s d) -> p s d", s=2)
                SW = work[:, 0:NT * H].rearrange("p (t h) -> p t h", h=H)
                DN = work[:, NT * H:2 * NT * H].rearrange("p (t h) -> p t h", h=H)
                rows_in = [sem(f"rows_in{k}") for k in range(2)]
                chain, gelu_ready, summed = sem("chain"), sem("gelu_ready"), sem("summed")
                heads = lambda a: a.rearrange("p (h c) -> p h c", h=H)
                with nc.Block() as block:

                    @block.sync
                    def _(sp):
                        def one(q, s, turn, first):
                            if not first:
                                sp.wait_ge(chain, 5 + 4 * (q - 1))
                            sp.dma_start(TB[:, s, :], tab_d[bass.ds(P * q, P), 0:D]).then_inc(rows_in[s], 16)
                        by_tile(sp, one)

                    @block.vector
                    def _(dve):
                        link = Chain(dve, chain)
                        link(dve.tensor_scalar(DN, ACC[:, :, D:D + H], 0.0, None, ALU.is_equal))
                        link(dve.tensor_tensor(SW, ACC[:, :, D + H:RW], DN, ALU.max))
                        link(dve.tensor_tensor(DN, ACC[:, :, D:D + H], SW, ALU.add))
                        link(dve.tensor_scalar(DN, DN, 1e-16, None, ALU.max))
                        link(dve.reciprocal(DN, DN))

                        def one(q, s, turn, first):
                            link = Chain(dve, chain, 5 + 4 * q)
                            dve.wait_ge(rows_in[s], 16 * (turn + 1))
                            link(dve.tensor_tensor(heads(TB[:, s, :]), heads(TB[:, s, :]),
                                                   SW[:, bass.ds(q, 1), :].rearrange("p a h -> p (a h)").unsqueeze(2).broadcast_to([P, H, C]), ALU.mult))
                            if not first:
                                dve.wait_ge(gelu_ready, q - 1)
                            link(dve.tensor_tensor(TO[:, s, :].unsqueeze(1), TB[:, s, :].unsqueeze(1), ACC[:, bass.ds(q, 1), 0:D], ALU.add))
                            link(dve.tensor_tensor(heads(TO[:, s, :]), heads(TO[:, s, :]),
                                                   DN[:, bass.ds(q, 1), :].rearrange("p a h -> p (a h)").unsqueeze(2).broadcast_to([P, H, C]), ALU.mult))
                            link(dve.tensor_tensor(TO[:, s, :], TO[:, s, :], VEC[:, 0, :], ALU.add))
                        by_tile(dve, one)

                    @block.scalar
                    def _(act):
                        def one(q, s, turn, first):
                            act.wait_ge(chain, 5 + 4 * (q + 1))
                            if not first:
                                act.wait_ge(summed, q - 1)
                            act.activation(TG[:, s, :], TO[:, s, :], ACT.Gelu).then_inc(gelu_ready, 1)
                        by_tile(act, one)

                    @block.gpsimd
                    def _(pool):
                        def one(q, s, turn, first):
                            pool.wait_ge(gelu_ready, q + 1)
                            pool.tensor_tensor(Xv[:, bass.ds(q, 1), :], Xv[:, bass.ds(q, 1), :], TG[:, s, :].unsqueeze(1), ALU.add).then_inc(summed, 1)
                        by_tile(pool, one)

        ctx, sem, ps = stage()
        with ctx:
            O = gath[:, 0:2 * D].rearrange("p (s d) -> p s d", s=2)
            rows_in = [sem(f"rows_in{k}") for k in range(2)]
            chain, moments, rooted, normed, stored = (sem("chain"), sem("moments"), sem("rooted"), sem("normed"), sem("stored"))
            with nc.Block() as block:

                @block.sync
                def _(sp):
                    def one(q, s, turn, first):
                        if not first:
                            sp.wait_ge(chain, q - 1)
                        sp.dma_start(O[:, s, :], x1_d[bass.ds(P * q, P), :]).then_inc(rows_in[s], 16)
                    by_tile(sp, one)
                    sp.wait_ge(normed, 1)
                    sp.dma_start(out[0:(NT - 1) * P, :].rearrange("(t p) d -> p t d", p=P), Xv[:, 0:NT - 1, :]).then_inc(stored, 16)
                    sp.dma_start(out[(NT - 1) * P:N, :], Xv[0:TAIL, NT - 1, :]).then_inc(stored, 16)
                    sp.wait_ge(stored, 32)

                @block.vector
                def _(dve):
                    def one(q, s, turn, first):
                        link = Chain(dve, chain, q)
                        dve.wait_ge(rows_in[s], 16 * (turn + 1))
                        link(dve.tensor_tensor(Xv[:, bass.ds(q, 1), :], Xv[:, bass.ds(q, 1), :], O[:, s, :].unsqueeze(1), ALU.add))
                    by_tile(dve, one)
                    layernorm(dve, moments, rooted, chain, NT, normed)

                @block.scalar
                def _(act):
                    act.wait_ge(moments, 1)
                    act.activation(RSTD[:, :, 0], MOM[:, :, 1], ACT.Sqrt).then_inc(rooted, 1)


_INS = ['x', 'src', 'dst', 'edge_weight', 'L0_gnn_W', 'L0_gnn_b', 'L1_gnn_Wl0', 'L1_gnn_Wr0', 'L1_gnn_att0', 'L1_gnn_b0',
        'L1_gnn_Wl1', 'L1_gnn_Wr1', 'L1_gnn_att1', 'L1_gnn_b1']


def kernel(**inputs):
    import numpy as np
    import concourse.bacc as bacc
    from concourse.bass_utils import run_bass_kernel_spmd as run

    nc = bacc.Bacc("TRN2", target_bir_lowering=False, num_devices=1)
    arrays, ins = {}, []
    for name in _INS:
        a = np.ascontiguousarray(inputs[name])
        arrays[f"in_{name}"] = a
        ins.append(nc.dram_tensor(f"in_{name}", a.shape, mybir.dt.from_np(a.dtype), kind="ExternalInput").ap())
    out = nc.dram_tensor("out_0", (N, D), FP32, kind="ExternalOutput").ap()
    gat = [ins[6:10], ins[10:14]]
    build(nc, *ins[:6], gat, out)
    r = run(nc, [arrays], core_ids=[0])
    return r.results[0]["out_0"]
```

```python
import concourse.bass as bass
from concourse import mybir
from contextlib import ExitStack

FP32 = mybir.dt.float32
BF16 = mybir.dt.bfloat16
I32 = mybir.dt.int32
ALU = mybir.AluOpType
ACT = mybir.ActivationFunctionType
AX = mybir.AxisListType.X

P = 128
N, D, H, E = 3125, 256, 8, 50000
C = D // H
NT = -(-N // P)
NP = NT * P
TAIL = N - (NT - 1) * P
NB = -(-E // P)
EB = NB + 1
EP = EB * P
CHUNKS = P // H
NI = -(-(NB + NT - 1) // CHUNKS) * CHUNKS
RUN = NI // CHUNKS
G = 4
NG = NI // G
IR = NI // G
NJ = NT - 1
VS = EB // G + NJ
VD = NG + NJ
XW = D + H
RW = D + 2 * H
UW = D + 1
BIG = 1.0e30
NO_EDGE_DST = float(NP + 800)
NOWHERE = -5000.0
SKIP = 60000.0
PIECES = 5
SLOPE = 0.2
EPS = 1e-5
LAST_EDGES = E - (P - 1) * EB


class Chain:

    def __init__(self, eng, sem, base=0):
        self.eng, self.sem, self.n = eng, sem, base

    def __call__(self, ins):
        self.n += 1
        ins.then_inc(self.sem, 1)
        self.eng.wait_ge(self.sem, self.n)


def back(it, par, k, ways):
    return (par - k) % ways, it + (par - k) // ways


def build(nc, x, src, dst, edge_weight, W0, b0, gat, out):
    top = ExitStack()

    def sb(name, shape, dt):
        return top.enter_context(nc.sbuf_tensor(name, shape, dt))

    def dram(name, shape, dt):
        return nc.dram_tensor(name, shape, dt)

    def group_of(value, most):
        return nc.s_assert_within(value, 0, most, skip_runtime_bounds_check_because="visit v is at tile j(v) <= v, and groups + tiles - 1 visits leave v - j(v) < groups")

    def piece(k):
        return slice(k * (NT // PIECES), (k + 1) * (NT // PIECES))

    def tiles_at(eng, at, count, most):
        return nc.values_load_multi_w_load_instructions(JROW[0:1, bass.ds(at, count)], (eng.engine,), min_val=0, max_val=most,
                                                        skip_runtime_bounds_check_because="a count of tile boundaries, of which there are most")[1]

    stage_no = [0]

    def stage():
        stage_no[0] += 1
        k = stage_no[0]
        ctx = ExitStack()
        sems = []

        def clear():
            nc.clear_and_free_semaphores(sems)
            nc.all_engine_barrier()

        ctx.callback(clear)

        def sem(name):
            sems.append(nc.alloc_semaphore(name=f"s{k}_{name}"))
            return sems[-1]

        ps = lambda name, shape: ctx.enter_context(nc.psum_tensor(f"p{k}_{name}", shape, FP32))
        return ctx, sem, ps

    with top:
        src_d = dram("src_sorted", [EB, P], FP32)
        dst_d = dram("dst_sorted", [EB, P], FP32)
        prev_d = dram("prev_dst", [EB, P], FP32)
        pos_d = dram("position", [EB, P], FP32)
        w_d = dram("weight", [EB, P], FP32)
        step_d = dram("step_tables", [1, NI + 2 * P], I32)
        loc_d = dram("local_rows", [NI, P], BF16)
        sup_d = dram("rows_by_src", [EP, UW], FP32)
        tab_d = dram("gather_table", [NP, XW], FP32)
        spill_d = dram("gathered", [NG, P, G * RW], FP32)
        sum_d = dram("chunk_summary", [P, 5], FP32)
        carry_d = dram("chunk_carry", [2, P], FP32)

        iota_row = sb("iota_row", [P, P], FP32)
        iota_p = sb("iota_p", [P, 1], FP32)
        ident = sb("ident", [P, P], FP32)
        before = sb("before", [P, P], FP32)
        ones = sb("ones", [P, P], FP32)
        step_no = sb("step_no", [P, G], FP32)
        tile_no = sb("tile_no", [P, NT], FP32)

        X = sb("X", [P, NT * D], FP32)
        Xv = X[:, :].rearrange("p (t d) -> p t d", d=D)
        gath = sb("gath", [P, 4 * G * RW], FP32)
        GATH = gath[:, :].rearrange("p (s g w) -> p s g w", s=4, g=G)
        node = sb("node", [P, 3 * NT * RW // 2], FP32)
        PARTS = node[:, :].bitcast(BF16).rearrange("p (k t w) -> p k t w", k=3, t=NT)
        ACC = node[:, 0:NT * RW].rearrange("p (t w) -> p t w", t=NT)
        SUP = node[:, 0:NT * D].rearrange("p (t d) -> p t d", t=NT)
        DSTM = sb("DSTM", [P, NI], FP32)
        WGT = sb("WGT", [P, NI], FP32)
        RESET = sb("RESET", [P, NI], FP32)
        MASK = sb("MASK", [P, NI], FP32)
        START = sb("START", [P, NI], FP32)
        SRCI = sb("SRCI", [P, NI], I32)
        POSI = sb("POSI", [P, NI], I32)
        JROW = sb("JROW", [1, NI + 2 * P], I32)
        FIRST = sb("FIRST", [P, 2, P], FP32)
        arena = sb("arena", [P, 5 * NI * H + 8], FP32)
        SC = arena[:, 0:NI * H]
        SELF = arena[:, NI * H:2 * NI * H]
        EX = arena[:, 2 * NI * H:4 * NI * H]
        RST = arena[:, 4 * NI * H:5 * NI * H + 1]
        D1 = EX[:, 0:NI * H]
        FW = EX[:, NI * H:2 * NI * H]
        LBC = sb("LBC", [P, 2, G * P], BF16)
        OHT = sb("OHT", [P, 2, G * P], BF16)
        OH = sb("OH", [P, 2, G, P], FP32)
        work = sb("work", [P, 4 * G * XW], FP32)
        Z = work[:, 0:2 * G * XW].rearrange("p (s w) -> p s w", s=2)
        T = work[:, 2 * G * XW:].rearrange("p (s w) -> p s w", s=2)
        GIDX = sb("GIDX", [P, 4, G], I32)

        ctx, sem, ps = stage()
        with ctx:
            M = node[:, 0:NT * EB]
            CUM = arena[:, 0:NT * EB]
            tmp_w = work
            SIi = tmp_w[:, 0:EB].bitcast(I32)
            DIi = tmp_w[:, EB:2 * EB].bitcast(I32)
            WL = tmp_w[:, 2 * EB:3 * EB]
            SF = tmp_w[:, 3 * EB:4 * EB]
            DF = tmp_w[:, 4 * EB:5 * EB]
            PV = tmp_w[:, 5 * EB:6 * EB]
            BK = tmp_w[:, 6 * EB:7 * EB]
            POS = tmp_w[:, 7 * EB:8 * EB]
            JUNK = tmp_w[:, 8 * EB:9 * EB]
            small = ctx.enter_context(nc.sbuf_tensor("prep_small", [P, 400], FP32))
            PC = small[:, 0:1].bitcast(I32)
            RT = small[:, 8:8 + NT]
            CD = small[:, 40:40 + NT + NJ]
            OFF = small[:, 96:96 + NT]
            BI = small[:, 128:128 + 2 * NJ].bitcast(I32)
            BI2 = small[:, 176:176 + 2 * NJ].bitcast(I32)
            BND = small[:, 224:224 + 2 * NJ]
            VB = small[:, 344:344 + 2 * NJ]
            VBI = small[:, 176:176 + 2 * NJ].bitcast(I32)
            VBJ = small[:, 128:128 + 2 * NJ].bitcast(I32)
            JC = small[:, 280:280 + G + 2]
            JI = small[:, 296:296 + G + 2].bitcast(I32)
            BIX = small[:, 312:312 + G].bitcast(I32)
            BF = small[:, 320:320 + G]
            J128 = small[:, 328:328 + G]
            rows = arena[:, NT * EB:NT * EB + 11 * G * P].rearrange("p (k g q) -> p k g q", k=11, g=G)
            PS, PD, PP, PW, PV2, VAL, ST, RS, MK, LC, NS = [rows[0:IR, k] for k in range(11)]
            LB16 = ctx.enter_context(nc.sbuf_tensor("loc16", [P, G, P], BF16))
            TI = FIRST[:, :, :].rearrange("p k v -> p (k v)").bitcast(I32)
            psum_off = ps("off", [P, 512])
            psum_bnd = ps("bnd", [P, 512])
            psum_tr = [ps(f"tr{k}", [P, 512]) for k in range(4)]

            pad_set, loaded, x_loaded = sem("pad_set"), sem("loaded"), sem("x_loaded")
            consts, chain = sem("consts"), sem("chain")
            edges_ready, edges_stored = sem("edges_ready"), sem("edges_stored")
            counts_ready, sums_ready = sem("counts_ready"), sem("sums_ready")
            steps_ready, steps_stored, steps_back = sem("steps_ready"), sem("steps_stored"), sem("steps_back")
            rows_in, rows_ready = sem("rows_in"), sem("rows_ready")
            loc_stored, trans, evac = sem("loc_stored"), sem("trans"), sem("evac")
            with nc.Block() as block:

                @block.sync
                def _(sp):
                    sp.wait_ge(pad_set, 1)
                    for tile, flat in ((SIi, src), (DIi, dst), (WL, edge_weight)):
                        sp.dma_start(tile[0:P - 1, :], flat[0:(P - 1) * EB].rearrange("(p c) -> p c", c=EB)).then_inc(loaded, 16)
                        sp.dma_start(tile[P - 1:P, 0:LAST_EDGES],
                                     flat[(P - 1) * EB:E].rearrange("(a c) -> a c", a=1)).then_inc(loaded, 16)
                    sp.dma_start(PC[1:P, :], dst[0:(P - 1) * EB].rearrange("(p c) -> p c", c=EB)[:, EB - 1:EB],
                                 allow_slow_non_contiguous=True).then_inc(loaded, 16)
                    sp.dma_start(Xv[:, 0:NT - 1, :], x[0:(NT - 1) * P, :].rearrange("(t p) d -> p t d", p=P)).then_inc(x_loaded, 16)
                    sp.dma_start(Xv[0:TAIL, NT - 1, :], x[(NT - 1) * P:N, :]).then_inc(x_loaded, 16)
                    sp.wait_ge(edges_ready, 1)
                    for arr, flat in ((SF, src_d), (DF, dst_d), (PV, prev_d), (WL, w_d)):
                        sp.dma_start(flat[:, :].rearrange("b q -> (b q)").rearrange("(p c) -> p c", c=EB), arr).then_inc(edges_stored, 16)
                    sp.dma_start(sup_d[E:E + P, :], arena[:, 0:UW]).then_inc(edges_stored, 16)
                    sp.dma_start(sup_d[E + P:EP, :], arena[0:EP - E - P, 0:UW]).then_inc(edges_stored, 16)
                    sp.wait_ge(edges_ready, 2)
                    sp.dma_start(pos_d[:, :].rearrange("b q -> (b q)").rearrange("(p c) -> p c", c=EB), POS).then_inc(edges_stored, 16)
                    sp.wait_ge(steps_ready, 3)
                    sp.dma_start(step_d[0, 0:NI].rearrange("(g p) -> p g", p=IR), JI[0:IR, 0:G],
                                 allow_slow_non_contiguous=True).then_inc(steps_stored, 16)
                    sp.dma_start(step_d[0, NI:].rearrange("(k p) -> p k", p=P), JI[:, G:G + 2],
                                 allow_slow_non_contiguous=True).then_inc(steps_stored, 16)
                    sp.wait_ge(steps_stored, 32)
                    sp.dma_start(JROW[0:1, :], step_d[:, :]).then_inc(steps_back, 16)
                    sp.dma_start(TI, step_d[:, NI:].broadcast_to([P, 2 * P])).then_inc(steps_back, 16)
                    sp.wait_ge(rows_ready, 1)
                    sp.dma_start(loc_d[:, :].rearrange("(g p) q -> p g q", p=IR), LB16[0:IR, :, :]).then_inc(loc_stored, 16)
                    sp.wait_ge(loc_stored, 16)
                    sp.wait_ge(steps_back, 32)

                @block.gpsimd
                def _(pool):
                    IMP = dict(allow_small_or_imprecise_dtypes=True)
                    pool.iota(tile_no[:, :], pattern=[[1, NT]], base=0, channel_multiplier=0, **IMP).then_inc(consts, 1)
                    pool.memset(ones[:, :], 1.0).then_inc(consts, 1)
                    pool.memset(ident[:, :], 0.0).then_inc(consts, 1)
                    pool.memset(before[:, :], 0.0).then_inc(consts, 1)
                    pool.iota(iota_row[:, :], pattern=[[1, P]], base=0, channel_multiplier=0, **IMP).then_inc(consts, 1)
                    pool.iota(iota_p[:, :], pattern=[[0, 1]], base=0, channel_multiplier=1, **IMP).then_inc(consts, 1)
                    pool.iota(step_no[:, :], pattern=[[IR, G]], base=0, channel_multiplier=1, **IMP).then_inc(consts, 1)
                    pool.wait_ge(consts, 7)
                    pool.affine_select(out=ident[:, :], in_=ident[:, :], compare_op=ALU.not_equal, fill=1.0, base=0,
                                       pattern=[[-1, P]], channel_multiplier=1).then_inc(consts, 1)
                    pool.affine_select(out=before[:, :], in_=before[:, :], compare_op=ALU.is_ge, fill=1.0, base=0,
                                       pattern=[[-1, P]], channel_multiplier=1).then_inc(consts, 1)
                    pool.wait_ge(edges_stored, 7 * 16)
                    pool.wait_ge(steps_ready, 2)
                    pool.nop(nofuse=True)
                    for row, flat in ((PS, src_d), (PD, dst_d), (PV2, prev_d), (PW, w_d), (PP, pos_d)):
                        for g in range(G):
                            pool.indirect_dma_start(row[:, g, :], None, flat[:, :],
                                                    bass.IndirectOffsetOnAxis(BIX[0:IR, g:g + 1], 0)).then_inc(rows_in, 16)

                @block.vector
                def _(dve):
                    link = Chain(dve, chain)
                    dve.memset(DIi, int(NO_EDGE_DST))
                    dve.memset(SIi, NP)
                    dve.memset(PC, -1)
                    dve.memset(CD, 0.0)
                    dve.memset(arena[:, 0:UW], 0.0)
                    link(dve.memset(WL, 0.0))
                    dve.memset(X[:, (NT - 1) * D:], 0.0).then_inc(pad_set, 1)
                    dve.wait_ge(loaded, 7 * 16)
                    link(dve.tensor_copy(DF, DIi))
                    dve.tensor_copy(PV[:, 0:1], PC)
                    dve.tensor_copy(PV[:, 1:EB], DF[:, 0:EB - 1])
                    link(dve.tensor_copy(SF, SIi))
                    link(dve.tensor_scalar(DIi, SIi, 7, None, ALU.arith_shift_right))
                    dve.tensor_copy(BK, DIi).then_inc(edges_ready, 1)
                    dve.wait_ge(edges_ready, 1)
                    dve.wait_ge(consts, 9)
                    Mv = M.rearrange("p (k c) -> p k c", c=EB)
                    link(dve.tensor_tensor(Mv, BK.unsqueeze(1).broadcast_to([P, NT, EB]),
                                           tile_no[:, :].unsqueeze(2).broadcast_to([P, NT, EB]), ALU.is_equal))
                    dve.wait_ge(edges_stored, 6 * 16)
                    link(dve.tensor_tensor_scan(CUM, ones[:, 0:1].broadcast_to([P, NT * EB]), M, 0.0, ALU.mult, ALU.add))
                    CUMv = CUM.rearrange("p (k c) -> p k c", c=EB)
                    ends = CUMv[:, :, EB - 1]
                    link(dve.tensor_copy(CD[:, 1:NT], ends[:, 0:NT - 1]))
                    link(dve.tensor_tensor(RT, ends, CD[:, 0:NT], ALU.subtract))
                    for j in range(NJ):
                        link(dve.tensor_scalar(JUNK, DF, float(P * (j + 1)), 0.0, ALU.is_lt, ALU.add,
                                               accum_out=CD[:, NT + j:NT + j + 1]))
                    dve.tensor_copy(JUNK[:, 0:1], tile_no[:, 0:1]).then_inc(counts_ready, 1)
                    dve.wait_ge(counts_ready, 1)
                    dve.wait_ge(sums_ready, 1)
                    link(dve.scalar_tensor_tensor(OFF, psum_off[:, 0:NT], -1.0, CD[:, 0:NT], ALU.add, ALU.subtract))
                    for k in range(NT):
                        ins = dve.scalar_tensor_tensor(CUMv[:, k, :], CUMv[:, k, :], OFF[:, k:k + 1], Mv[:, k, :], ALU.add, ALU.mult)
                    link(ins)
                    dve.tensor_reduce(POS, CUM.rearrange("p (k c) -> p c k", c=EB), AX, ALU.add).then_inc(edges_ready, 1)
                    link(dve.tensor_copy(BI, psum_bnd[:, 0:2 * NJ]))
                    link(dve.tensor_scalar(BI2, BI, 7, None, ALU.arith_shift_right))
                    link(dve.tensor_copy(BND, BI2))
                    BNDv = BND.rearrange("p (w j) -> p w j", w=2)
                    link(dve.tensor_tensor(BNDv, BNDv, tile_no[:, 1:NT].unsqueeze(1).broadcast_to([P, 2, NJ]), ALU.add))
                    for g in range(G):
                        link(dve.tensor_scalar(JUNK[:, 0:NJ], BND[:, NJ:2 * NJ], step_no[:, g:g + 1], 0.0,
                                               ALU.is_le, ALU.add, accum_out=JC[:, g:g + 1]))
                    dve.tensor_tensor(BF, step_no[:, :], JC[:, 0:G], ALU.subtract).then_inc(steps_ready, 1)
                    dve.wait_ge(steps_ready, 1)
                    dve.tensor_copy(BIX, BF).then_inc(steps_ready, 1)
                    link(dve.tensor_copy(VBI[:, NJ:], BND[:, NJ:]))
                    link(dve.tensor_scalar(VBJ[:, NJ:], VBI[:, NJ:], 2, None, ALU.arith_shift_right))
                    link(dve.tensor_copy(VBI[:, 0:NJ], psum_bnd[:, 0:NJ]))
                    link(dve.tensor_scalar(VBJ[:, 0:NJ], VBI[:, 0:NJ], 9, None, ALU.arith_shift_right))
                    link(dve.tensor_copy(VB, VBJ))
                    VBv = VB.rearrange("p (w j) -> p w j", w=2)
                    link(dve.tensor_tensor(VBv, VBv, tile_no[:, 1:NT].unsqueeze(1).broadcast_to([P, 2, NJ]), ALU.add))
                    for w in range(2):
                        link(dve.tensor_scalar(JUNK[:, 0:NJ], VB[:, w * NJ:(w + 1) * NJ], iota_p[:, 0:1], 0.0,
                                               ALU.is_le, ALU.add, accum_out=JC[:, G + w:G + w + 1]))
                    dve.tensor_copy(JI, JC).then_inc(steps_ready, 1)
                    link(dve.tensor_scalar(J128, JC[:, 0:G], float(P), None, ALU.mult))
                    dve.wait_ge(rows_in, 20 * 16)
                    for g in range(G):
                        ins = dve.tensor_scalar(LC[:, g, :], PD[:, g, :], J128[0:IR, g:g + 1], None, ALU.subtract)
                    link(ins)
                    link(dve.tensor_scalar(VAL, LC, 0.0, None, ALU.is_ge))
                    link(dve.scalar_tensor_tensor(VAL, LC, float(P), VAL, ALU.is_lt, ALU.mult))
                    link(dve.tensor_tensor(ST, PD, PV2, ALU.not_equal))
                    link(dve.tensor_tensor(ST, ST, VAL, ALU.mult))
                    dve.tensor_scalar(RS, ST, -BIG, None, ALU.mult)
                    dve.tensor_scalar(NS, ST, -1.0, BIG, ALU.add, ALU.mult)
                    dve.tensor_scalar(MK, VAL, -1.0, BIG, ALU.add, ALU.mult)
                    dve.scalar_tensor_tensor(PV2, PD, -NOWHERE, VAL, ALU.add, ALU.mult)
                    dve.tensor_scalar(PS, PS, float(NP - 1), None, ALU.min)
                    link(dve.scalar_tensor_tensor(PP, PP, -SKIP, VAL, ALU.add, ALU.mult))
                    dve.tensor_scalar(PP, PP, SKIP, None, ALU.add)
                    link(dve.tensor_scalar(PV2, PV2, NOWHERE, None, ALU.add))
                    dve.tensor_copy(LB16[0:IR, :, :], LC).then_inc(rows_ready, 1)
                    dve.wait_ge(rows_ready, 1)
                    for k, col in enumerate((DSTM, SRCI, POSI, WGT, RESET, MASK, START)):
                        dve.wait_ge(trans, k + 1)
                        dve.tensor_copy(col[:, :], psum_tr[k % 4][:, 0:NI]).then_inc(evac, 1)

                @block.tensor
                def _(pe):
                    pe.wait_ge(counts_ready, 1)
                    pe.matmul(psum_off[:, 0:NT], before[:, :], RT, start=True, stop=False)
                    pe.matmul(psum_off[:, 0:NT], ones[:, :], CD[:, 0:NT], start=False, stop=True)
                    pe.matmul(psum_bnd[:, 0:2 * NJ], ones[:, :], CD[:, 1:1 + 2 * NJ], start=True, stop=True).then_inc(sums_ready, 1)
                    pe.wait_ge(rows_ready, 1)
                    for k, row in enumerate((PV2, PS, PP, PW, RS, MK, NS)):
                        if k >= 4:
                            pe.wait_ge(evac, k - 3)
                        for g in range(G):
                            ins = pe.transpose(psum_tr[k % 4][:, g * IR:(g + 1) * IR], row[:, g, :], ident[0:IR, 0:IR])
                        ins.then_inc(trans, 1)

            with nc.Block() as block:
                scan_tr, scan_ev, ch2 = sem("scan_tr"), sem("scan_ev"), sem("ch2")
                res, high, rest, middle, rest2 = sem("res"), sem("high"), sem("rest"), sem("middle"), sem("rest2")
                RX = arena[:, 0:NI * H].rearrange("p (r k h) -> p r k h", r=RUN, k=CHUNKS)
                R1 = EX[:, 0:NT * D]
                R1v = R1.rearrange("p (t d) -> p t d", d=D)

                @block.tensor
                def _(pe):
                    pe.wait_ge(res, 1)
                    for r in range(RUN):
                        b = r // 4
                        if b >= 4 and r % 4 == 0:
                            pe.wait_ge(scan_ev, b - 3)
                        ins = pe.transpose(psum_tr[b % 4][:, (r % 4) * P:(r % 4 + 1) * P],
                                           arena[:, r * P:(r + 1) * P], ident[:, :])
                        if r % 4 == 3 or r == RUN - 1:
                            ins.then_inc(scan_tr, 1)

                @block.vector
                def _(dve):
                    link = Chain(dve, ch2)
                    dve.memset(RST[:, NI * H:], 0.0)
                    link(dve.tensor_copy(T[:, 0, 0:2 * P], TI))
                    link(dve.tensor_scalar(FIRST[:, :, :].rearrange("p k v -> p (k v)"), T[:, 0, 0:2 * P], float(P), None, ALU.mult))
                    dve.tensor_copy(RX, RESET[:, :].rearrange("p (k r) -> p r k", k=CHUNKS).unsqueeze(3).broadcast_to([P, RUN, CHUNKS, H])).then_inc(res, 1)
                    for k in range(PIECES):
                        dve.wait_ge(high, k + 1)
                        dve.tensor_tensor(R1v[:, piece(k)], Xv[:, piece(k)], PARTS[:, 0, piece(k), 0:D], ALU.subtract).then_inc(rest, 1)
                    for b in range(-(-RUN // 4)):
                        n = min(4, RUN - 4 * b) * P
                        dve.wait_ge(scan_tr, b + 1)
                        dve.tensor_copy(RST[:, b * 4 * P:b * 4 * P + n], psum_tr[b % 4][:, 0:n]).then_inc(scan_ev, 1)

                @block.gpsimd
                def _(pool):
                    for k in range(PIECES):
                        pool.wait_ge(middle, k + 1)
                        pool.tensor_tensor(R1v[:, piece(k)], R1v[:, piece(k)], PARTS[:, 1, piece(k), 0:D], ALU.subtract).then_inc(rest2, 1)

                @block.scalar
                def _(act):
                    act.wait_ge(x_loaded, 32)
                    for k in range(PIECES + 2):
                        if k < PIECES:
                            act.activation(PARTS[:, 0, piece(k), 0:D], Xv[:, piece(k)], ACT.Copy).then_inc(high, 1)
                        if 1 <= k <= PIECES:
                            act.wait_ge(rest, k)
                            act.activation(PARTS[:, 1, piece(k - 1), 0:D], R1v[:, piece(k - 1)], ACT.Copy).then_inc(middle, 1)
                        if k >= 2:
                            act.wait_ge(rest2, k - 1)
                            act.activation(PARTS[:, 2, piece(k - 2), 0:D], R1v[:, piece(k - 2)], ACT.Copy)

        ctx, sem, ps = stage()
        with ctx:
            U = gath[:, 0:4 * G * UW].rearrange("p (s g w) -> p s g w", s=4, g=G)
            expd = [ps(f"expd{k}", [P, 2, 512]) for k in range(2)]
            loc_in = [sem(f"loc_in{k}") for k in range(2)]
            hot_ready, exp_ready, u_ready, idx_ready = sem("hot_ready"), sem("exp_ready"), sem("u_ready"), sem("idx_ready")
            scattered = [sem(f"scattered{k}") for k in range(4)]
            turns = NG // 4
            with nc.Block() as block:

                def quads(eng, body):
                    body(0)
                    with eng.Fori(1, turns) as it:
                        body(it)

                @block.sync
                def _(sp):
                    def body(it):
                        for s in range(4):
                            q = 4 * it + s
                            if it is not 0 or s > 1:
                                sp.wait_ge(hot_ready, q - 1)
                            sp.dma_start(LBC[:, s % 2, :], loc_d[bass.ds(G * q, G), :].rearrange("g q -> (g q)").rearrange("(a n) -> a n", a=1)
                                         .broadcast_to([P, G * P])).then_inc(loc_in[s % 2], 16)
                    quads(sp, body)

                @block.vector
                def _(dve):
                    def body(it):
                        for s in range(4):
                            q = 4 * it + s
                            dve.wait_ge(loc_in[s % 2], 16 * (2 * it + s // 2 + 1))
                            if it is not 0 or s > 1:
                                dve.wait_ge(exp_ready, q - 1)
                            dve.tensor_scalar(OHT[:, s % 2, :], LBC[:, s % 2, :], iota_p[:, 0:1], None, ALU.is_equal).then_inc(hot_ready, 1)
                            if it is not 0:
                                dve.wait_ge(scattered[s], 64 * it)
                            dve.tensor_copy(U[:, s, :, D], SRCI[:, bass.ds(G * q, G)])
                            dve.tensor_copy(GIDX[:, s, :], POSI[:, bass.ds(G * q, G)]).then_inc(idx_ready, 1)
                    quads(dve, body)

                @block.tensor
                def _(pe):
                    def body(it):
                        for s in range(4):
                            q = 4 * it + s
                            pe.wait_ge(hot_ready, q + 1)
                            if it is not 0 or s > 1:
                                pe.wait_ge(u_ready, q - 1)
                            for g, j in enumerate(tiles_at(pe, G * q, G, NT - 1)):
                                for k in range(3):
                                    ins = pe.matmul(expd[s % 2][:, g // 2, (g % 2) * D:(g % 2 + 1) * D], OHT[:, s % 2, g * P:(g + 1) * P],
                                                    PARTS[:, k, bass.ds(j, 1), 0:D], start=(k == 0), stop=(k == 2))
                            ins.then_inc(exp_ready, 1)
                    quads(pe, body)

                @block.scalar
                def _(act):
                    def body(it):
                        for s in range(4):
                            q = 4 * it + s
                            act.wait_ge(exp_ready, q + 1)
                            if it is not 0:
                                act.wait_ge(scattered[s], 64 * it)
                            act.wait_ge(idx_ready, q + 1)
                            for g in range(G):
                                ins = act.activation(U[:, s, g, 0:D], expd[s % 2][:, g // 2, (g % 2) * D:(g % 2 + 1) * D], ACT.Copy,
                                                     scale=WGT[:, bass.ds(G * q + g, 1)])
                            ins.then_inc(u_ready, 1)
                    quads(act, body)

                @block.gpsimd
                def _(pool):
                    def body(it):
                        for s in range(4):
                            q = 4 * it + s
                            pool.wait_ge(u_ready, q + 1)
                            pool.nop(nofuse=True)
                            for g in range(G):
                                pool.indirect_dma_start(sup_d[:, :], bass.IndirectOffsetOnAxis(GIDX[:, s, g:g + 1], 0), U[:, s, g, :], None,
                                                        bounds_check=EP - 1, oob_is_err=False).then_inc(scattered[s], 16)
                    quads(pool, body)
                    for s in range(4):
                        pool.wait_ge(scattered[s], 64 * turns)

        ctx, sem, ps = stage()
        with ctx:
            U = gath[:, 0:4 * G * UW].rearrange("p (s g w) -> p s g w", s=4, g=G)
            LS = ctx.enter_context(nc.sbuf_tensor("src_local", [P, 2, G], FP32))
            sums = [ps(f"sums{k}", [P, 512]) for k in range(4)]
            rows_in = [sem(f"rows_in{k}") for k in range(4)]
            cleared, loc_ready, hot_ready, sum_ready, added = (sem("cleared"), sem("loc_ready"), sem("hot_ready"),
                                                               sem("sum_ready"), sem("added"))
            turns = VS // 4
            sup_rows = sup_d[:, :].rearrange("(m g p) w -> m p g w", g=G, p=P)
            with nc.Block() as block:

                def visits(eng, one):
                    for s in range(4):
                        one(s, s, 0, s)
                    with eng.Fori(1, turns) as it:
                        for s in range(4):
                            one(4 * it + s, s, it, 4)
                    for v in range(4 * turns, VS):
                        one(v, v % 4, turns, 4)

                @block.sync
                def _(sp):
                    def one(v, s, turn, past):
                        j = sp.value_load(JROW[0:1, bass.ds(NI + v, 1)], min_val=0, max_val=NJ)
                        m = group_of(v - j, EB // G - 1)
                        if past == 4:
                            sp.wait_ge(sum_ready, v - 3)
                        sp.dma_start(U[:, s], sup_rows[bass.ds(m, 1)].rearrange("a p g w -> (a p) g w")).then_inc(rows_in[s], 16)
                    visits(sp, one)

                @block.gpsimd
                def _(pool):
                    pool.memset(SUP, 0.0).then_inc(cleared, 1)

                @block.vector
                def _(dve):
                    def hots(v, s, turn, past):
                        dve.wait_ge(rows_in[s], 16 * (turn + 1))
                        if past >= 2:
                            dve.wait_ge(sum_ready, v - 1)
                        dve.tensor_tensor(LS[:, s % 2, :], U[:, s, :, D], FIRST[:, 0, bass.ds(v, 1)].broadcast_to([P, G]), ALU.subtract).then_inc(loc_ready, 1)
                        dve.wait_ge(loc_ready, v + 1)
                        dve.tensor_tensor(OH[:, s % 2], iota_row[:, :].unsqueeze(1).broadcast_to([P, G, P]),
                                          LS[:, s % 2, :].unsqueeze(2).broadcast_to([P, G, P]), ALU.is_equal).then_inc(hot_ready, 1)

                    def add(v, s, past):
                        j = dve.value_load(JROW[0:1, bass.ds(NI + v, 1)], min_val=0, max_val=NJ)
                        dve.wait_ge(sum_ready, v + 1)
                        if past:
                            dve.wait_ge(added, v)
                        dve.tensor_tensor(SUP[:, bass.ds(j, 1), :], SUP[:, bass.ds(j, 1), :], sums[s][:, 0:D].unsqueeze(1), ALU.add).then_inc(added, 1)

                    def one(v, s, turn, past):
                        hots(v, s, turn, past)
                        if past == 2:
                            dve.wait_ge(cleared, 1)
                        if past >= 2:
                            add(v - 2, (s - 2) % 4, past - 2)
                    visits(dve, one)
                    for v in (VS - 2, VS - 1):
                        add(v, v % 4, 3)

                @block.tensor
                def _(pe):
                    def one(v, s, turn, past):
                        pe.wait_ge(hot_ready, v + 1)
                        if past == 4:
                            pe.wait_ge(added, v - 3)
                        for g in range(G):
                            ins = pe.matmul(sums[s][:, 0:D], OH[:, s % 2, g, :], U[:, s, g, 0:D], start=(g == 0), stop=(g == G - 1))
                        ins.then_inc(sum_ready, 1)
                    visits(pe, one)

        WB = sb("WB", [P, 4 * D], FP32)
        VEC = sb("VEC", [P, 3, D], FP32)
        STATS = sb("STATS", [P, NT, 8], FP32)
        MOM = sb("MOM", [P, NT, 2], FP32)
        RSTD = sb("RSTD", [P, NT, 2], FP32)
        x1_d = dram("x1", [NP, D], FP32)
        X1 = arena[:, 0:NT * D].rearrange("p (t d) -> p t d", d=D)

        def lagged(eng, one, drain):
            for t in range(4):
                one(t, t, 0)
            with eng.Fori(1, NT // 4 - 1) as it:
                for s in range(4):
                    one(4 * it + s, s, it)
            for t in range((NT // 4 - 1) * 4, NT + drain):
                one(t, t % 4, t // 4)

        def exists(t, k=0):
            return not isinstance(t, int) or 0 <= t + k < NT

        def past(t, k):
            return not isinstance(t, int) or t >= k

        XS = gath[:, 0:8 * D].rearrange("p (s w) -> p s w", s=4)
        XT = gath[:, 8 * D:12 * D].rearrange("p (s w) -> p s w", s=2)

        def layernorm(dve, moments, rooted, chain, count, normed, summed=None):
            link = Chain(dve, chain, count)
            for t in range(NT):
                if summed is not None and t % (NT // PIECES) == 0:
                    dve.wait_ge(summed, t // (NT // PIECES) + 1)
                ins = dve.bn_stats(STATS[:, t, 0:6], Xv[:, t, :])
            link(ins)
            for t in range(NT):
                ins = dve.bn_aggr(MOM[:, t, :], STATS[:, t, 0:6])
            link(ins)
            dve.tensor_scalar(MOM[:, :, 1], MOM[:, :, 1], EPS, None, ALU.add).then_inc(moments, 1)
            dve.wait_ge(rooted, 1)
            link(dve.reciprocal(RSTD[:, :, 1], RSTD[:, :, 0]))
            for t in range(NT):
                ins = dve.tensor_scalar(Xv[:, t, :], Xv[:, t, :], MOM[:, t, 0:1], RSTD[:, t, 1:2], ALU.subtract, ALU.mult)
                if (t + 1) % (NT // PIECES) == 0:
                    ins.then_inc(normed, 1)

        ctx, sem, ps = stage()
        with ctx:
            psum_t = [ps(f"t{k}", [P, 512]) for k in range(2)]
            psum_o = [ps(f"o{k}", [P, 512]) for k in range(2)]
            w_in, copied, transposed, evacuated, product, chain, moments, rooted, normed, stored = (
                sem("w_in"), sem("copied"), sem("transposed"), sem("evacuated"), sem("product"), sem("chain"),
                sem("moments"), sem("rooted"), sem("normed"), sem("stored"))
            O = work[:, 0:2 * D].rearrange("p (s d) -> p s d", s=2)
            with nc.Block() as block:

                @block.sync
                def _(sp):
                    sp.dma_start(WB[:, :].rearrange("p (k n) -> p k n", k=4), W0.rearrange("(k p) n -> p k n", p=P)).then_inc(w_in, 16)
                    sp.dma_start(VEC[:, 0, :], b0.rearrange("(a n) -> a n", a=1).broadcast_to([P, D])).then_inc(w_in, 16)
                    for k in range(PIECES):
                        sp.wait_ge(normed, k + 1)
                        sp.dma_start(x1_d[:, :].rearrange("(t p) d -> p t d", p=P)[:, piece(k)], Xv[:, piece(k)]).then_inc(stored, 16)
                    sp.wait_ge(stored, 16 * PIECES)

                @block.gpsimd
                def _(pool):
                    pool.memset(gath[:, 12 * D:], 0.0)

                    def one(t, s, turn):
                        if past(t, 4):
                            pool.wait_ge(transposed, t - 3)
                        pool.tensor_copy(XS[:, s, 0:D].unsqueeze(1), Xv[:, bass.ds(t, 1), :])
                        pool.tensor_copy(XS[:, s, D:2 * D].unsqueeze(1), SUP[:, bass.ds(t, 1), :]).then_inc(copied, 1)
                    lagged(pool, one, 0)

                @block.scalar
                def _(act):
                    def one(t, s, turn):
                        act.wait_ge(transposed, t + 1)
                        if past(t, 2):
                            act.wait_ge(product, t - 1)
                        act.activation(XT[:, s % 2, :], psum_t[s % 2][:, :], ACT.Copy).then_inc(evacuated, 1)
                    lagged(act, one, 0)
                    act.wait_ge(moments, 1)
                    act.activation(RSTD[:, :, 0], MOM[:, :, 1], ACT.Sqrt).then_inc(rooted, 1)

                @block.tensor
                def _(pe):
                    def transpose(t, s):
                        pe.wait_ge(copied, t + 1)
                        if past(t, 2):
                            pe.wait_ge(evacuated, t - 1)
                        for k in range(4):
                            ins = pe.transpose(psum_t[s % 2][:, k * P:(k + 1) * P], XS[:, s, k * P:(k + 1) * P], ident[:, :])
                        ins.then_inc(transposed, 1)

                    def one(t, s, turn):
                        if exists(t, 1):
                            transpose(t + 1, (s + 1) % 4)
                        pe.wait_ge(evacuated, t + 1)
                        if past(t, 2):
                            pe.wait_ge(chain, 2 * (t - 1))
                        for k in range(4):
                            ins = pe.matmul(psum_o[s % 2][:, 0:D], XT[:, s % 2, k * P:(k + 1) * P], WB[:, k * D:(k + 1) * D],
                                            start=(k == 0), stop=(k == 3))
                        ins.then_inc(product, 1)
                    transpose(0, 0)
                    pe.wait_ge(w_in, 32)
                    lagged(pe, one, 0)

                @block.vector
                def _(dve):
                    dve.wait_ge(w_in, 32)

                    def one(q, s, turn):
                        s = s % 2
                        link = Chain(dve, chain, 2 * q)
                        dve.wait_ge(product, q + 1)
                        link(dve.tensor_tensor(O[:, s, :], psum_o[s][:, 0:D], VEC[:, 0, :], ALU.add))
                        dve.wait_ge(transposed, q + 1)
                        link(dve.scalar_tensor_tensor(Xv[:, bass.ds(q, 1), :], O[:, s, :].unsqueeze(1), 0.0, Xv[:, bass.ds(q, 1), :], ALU.max, ALU.add))
                    lagged(dve, one, 0)
                    layernorm(dve, moments, rooted, chain, 2 * NT, normed)

        for layer, (Wl, Wr, att, bias) in enumerate(gat):
            ctx, sem, ps = stage()
            with ctx:
                psum_t = [ps(f"t{k}", [P, 512]) for k in range(2)]
                psum_o = [ps(f"o{k}", [P, 512]) for k in range(2)]
                w_in, copied, transposed, evacuated, product, att_ready, rows_copied = (
                    sem("w_in"), sem("copied"), sem("transposed"), sem("evacuated"), sem("product"), sem("att_ready"), sem("rows_copied"))
                lin_ready, z_ready, sums_ready, linear, relu_ready, self_ready = (
                    sem("lin_ready"), sem("z_ready"), sem("sums_ready"), sem("linear"), sem("relu_ready"), sem("self_ready"))
                rows_stored = [sem(f"rows_stored{k}") for k in range(4)]
                high, rest, middle, rest2 = sem("high"), sem("rest"), sem("middle"), sem("rest2")

                def part(at, n):
                    return arena[:, at:at + n]
                LR = part(0, 8 * RW).rearrange("p (s k w) -> p s k w", s=4, k=2)
                RES = part(8 * RW, 4 * RW).rearrange("p (s w) -> p s w", s=4)
                LIN = part(12 * RW, 2 * D).rearrange("p (k w) -> p k w", k=2)
                ZR = part(12 * RW + 2 * D, 2 * D).rearrange("p (s w) -> p s w", s=2)
                S8 = part(12 * RW + 4 * D, 2 * H).rearrange("p (k w) -> p k w", k=2)
                with nc.Block() as block:

                    @block.sync
                    def _(sp):
                        WBv = WB[:, :].rearrange("p (k n) -> p k n", k=2)
                        sp.dma_start(WBv[:, :, 0:D], Wl.rearrange("(k p) n -> p k n", p=P)).then_inc(w_in, 16)
                        sp.dma_start(WBv[:, :, D:2 * D], Wr.rearrange("(k p) n -> p k n", p=P)).then_inc(w_in, 16)
                        sp.dma_start(VEC[:, 0, :], bias.rearrange("(a n) -> a n", a=1).broadcast_to([P, D])).then_inc(w_in, 16)
                        sp.dma_start(VEC[:, 2, :], att.rearrange("h c -> (h c)").rearrange("(a n) -> a n", a=1).broadcast_to([P, D])).then_inc(w_in, 16)

                        def one(t, s, turn):
                            sp.wait_ge(linear, t + 1)
                            sp.dma_start(tab_d[bass.ds(P * t, P), :], LR[:, s, 0, 0:XW]).then_inc(rows_stored[s], 16)
                        lagged(sp, one, 0)
                        for s in range(4):
                            sp.wait_ge(rows_stored[s], 16 * len(range(s, NT, 4)))

                    @block.gpsimd
                    def _(pool):
                        def copy(t, s):
                            if past(t, 4):
                                pool.wait_ge(transposed, t - 3)
                            pool.tensor_copy(XS[:, s, 0:D].unsqueeze(1), Xv[:, bass.ds(t, 1), :]).then_inc(copied, 1)

                        def one(t, s, turn):
                            if exists(t, 3):
                                copy(t + 3, (s + 3) % 4)
                            if exists(t, -3):
                                s3 = (s - 3) % 4
                                pool.wait_ge(middle, t - 2)
                                pool.tensor_tensor(RES[:, s3, :].unsqueeze(1), RES[:, s3, :].unsqueeze(1), PARTS[:, 1, bass.ds(t - 3, 1), :],
                                                   ALU.subtract).then_inc(rest2, 1)
                            if exists(t, -2):
                                s2 = (s - 2) % 4
                                pool.wait_ge(high, t - 1)
                                pool.tensor_tensor(RES[:, s2, :].unsqueeze(1), LR[:, s2, 1, :].unsqueeze(1), PARTS[:, 0, bass.ds(t - 2, 1), :],
                                                   ALU.subtract).then_inc(rest, 1)
                        for t in range(3):
                            copy(t, t)
                        lagged(pool, one, 3)

                    @block.scalar
                    def _(act):
                        def evacuate(t, s):
                            act.wait_ge(transposed, t + 1)
                            if past(t, 2):
                                act.wait_ge(product, t - 1)
                            act.activation(XT[:, s % 2, 0:D], psum_t[s % 2][:, 0:D], ACT.Copy).then_inc(evacuated, 1)

                        def one(t, s, turn):
                            if exists(t, 1):
                                evacuate(t + 1, (s + 1) % 4)
                            if exists(t):
                                act.wait_ge(product, t + 1)
                                if past(t, 4):
                                    act.wait_ge(rest, t - 3)
                                    act.wait_ge(rows_stored[s], 16 * turn)
                                act.activation(LR[:, s, :, 0:D], psum_o[s % 2][:, :].rearrange("p (k d) -> p k d", k=2), ACT.Copy).then_inc(rows_copied, 1)
                            if exists(t, -4):
                                act.wait_ge(rest2, t - 3)
                                act.activation(PARTS[:, 2, bass.ds(t - 4, 1), :], RES[:, s, :].unsqueeze(1), ACT.Copy)
                            if exists(t, -3):
                                act.wait_ge(rest, t - 2)
                                act.activation(PARTS[:, 1, bass.ds(t - 3, 1), :], RES[:, (s - 3) % 4, :].unsqueeze(1), ACT.Copy).then_inc(middle, 1)
                            if exists(t, -2):
                                act.wait_ge(self_ready, t - 1)
                                act.activation(PARTS[:, 0, bass.ds(t - 2, 1), :], LR[:, (s - 2) % 4, 1, :].unsqueeze(1), ACT.Copy).then_inc(high, 1)
                        evacuate(0, 0)
                        lagged(act, one, 4)

                    @block.tensor
                    def _(pe):
                        def transpose(t, s):
                            pe.wait_ge(copied, t + 1)
                            if past(t, 2):
                                pe.wait_ge(evacuated, t - 1)
                            for k in range(2):
                                ins = pe.transpose(psum_t[s % 2][:, k * P:(k + 1) * P], XS[:, s, k * P:(k + 1) * P], ident[:, :])
                            ins.then_inc(transposed, 1)

                        def one(t, s, turn):
                            if exists(t, 1):
                                transpose(t + 1, (s + 1) % 4)
                            pe.wait_ge(evacuated, t + 1)
                            if past(t, 2):
                                pe.wait_ge(rows_copied, t - 1)
                            for k in range(2):
                                ins = pe.matmul(psum_o[s % 2][:, :], XT[:, s % 2, k * P:(k + 1) * P], WB[:, 2 * k * D:2 * (k + 1) * D],
                                                start=(k == 0), stop=(k == 1))
                            ins.then_inc(product, 1)
                        transpose(0, 0)
                        pe.wait_ge(w_in, 64)
                        lagged(pe, one, 0)

                    @block.vector
                    def _(dve):
                        dve.wait_ge(w_in, 64)
                        dve.tensor_scalar(VEC[:, 1, :], VEC[:, 2, :], SLOPE, None, ALU.mult).then_inc(att_ready, 1)
                        dve.wait_ge(att_ready, 1)
                        dve.tensor_scalar(VEC[:, 2, :], VEC[:, 2, :], 1.0 - SLOPE, None, ALU.mult).then_inc(att_ready, 1)
                        dve.wait_ge(att_ready, 2)

                        def one(t, s, turn):
                            now, prev = exists(t), past(t, 1)
                            o = (s - 1) % 4
                            if now:
                                dve.wait_ge(rows_copied, t + 1)
                                if prev:
                                    dve.wait_ge(relu_ready, t)
                                dve.tensor_tensor(LIN, LR[:, s, :, 0:D], VEC[:, 1, :].unsqueeze(1).broadcast_to([P, 2, D]),
                                                  ALU.mult).then_inc(lin_ready, 1)
                                if past(t, 2):
                                    dve.wait_ge(sums_ready, t - 1)
                                dve.tensor_tensor(ZR[:, s % 2, :], LR[:, s, 0, 0:D], LR[:, s, 1, 0:D], ALU.add).then_inc(z_ready, 1)
                            if prev:
                                if past(t, 2):
                                    dve.wait_ge(self_ready, t - 1)
                                else:
                                    dve.wait_ge(relu_ready, t)
                                dve.tensor_reduce(S8[:, 0, :], ZR[:, o % 2, :].rearrange("p (h c) -> p h c", c=C), AX, ALU.add)
                                dve.tensor_tensor(S8[:, 1, :], LR[:, o, 0, D:D + H], LR[:, o, 1, D:D + H], ALU.add).then_inc(sums_ready, 1)
                            if now:
                                dve.wait_ge(lin_ready, t + 1)
                                dve.tensor_reduce(LR[:, s, :, D:D + H], LIN.rearrange("p k (h c) -> p k h c", c=C), AX, ALU.add).then_inc(linear, 1)
                                dve.wait_ge(z_ready, t + 1)
                                dve.scalar_tensor_tensor(ZR[:, s % 2, :], ZR[:, s % 2, :], 0.0, VEC[:, 2, :], ALU.max, ALU.mult).then_inc(relu_ready, 1)
                            if prev:
                                dve.wait_ge(sums_ready, t)
                                dve.tensor_tensor(LR[:, o, 1, D + H:RW], S8[:, 0, :], S8[:, 1, :], ALU.add).then_inc(self_ready, 1)
                        lagged(dve, one, 1)

            ctx, sem, ps = stage()
            with ctx:
                expd = [ps(f"expd{k}", [P, G, 512]) for k in range(2)]
                loc_in = [sem(f"loc_in{k}") for k in range(2)]
                gathered = [sem(f"gathered{k}") for k in range(4)]
                spilled = [sem(f"spilled{k}") for k in range(4)]
                hot_ready, exp_ready, idx_ready, z_ready, self_ready, relu_ready, weighted, scored = (
                    sem("hot_ready"), sem("exp_ready"), sem("idx_ready"), sem("z_ready"), sem("self_ready"),
                    sem("relu_ready"), sem("weighted"), sem("scored"))
                turns = NG // 4
                with nc.Block() as block:

                    def quads(eng, body):
                        body(0)
                        with eng.Fori(1, turns) as it:
                            body(it)

                    @block.gpsimd
                    def _(pool):
                        def body(it):
                            for s in range(4):
                                q = 4 * it + s
                                pool.wait_ge(idx_ready, q + 1)
                                pool.nop(nofuse=True)
                                for g in range(G):
                                    pool.indirect_dma_start(GATH[:, s, g, 0:XW], None, tab_d[:, :],
                                                            bass.IndirectOffsetOnAxis(GIDX[:, s, g:g + 1], 0)).then_inc(gathered[s], 16)
                        quads(pool, body)

                    @block.sync
                    def _(sp):
                        def spill(q, s, turn):
                            sp.wait_ge(gathered[s], 64 * (turn + 1))
                            sp.dma_start(spill_d[bass.ds(q, 1), :, :].rearrange("a p w -> (a p) w"), GATH[:, s].rearrange("p g w -> p (g w)")).then_inc(spilled[s], 16)

                        def body(it):
                            for s in range(4):
                                q = 4 * it + s
                                if not (it is 0 and s < 2):
                                    sp.wait_ge(hot_ready, q - 1)
                                sp.dma_start(LBC[:, s % 2, :], loc_d[bass.ds(G * q, G), :].rearrange("g q -> (g q)")
                                             .rearrange("(a n) -> a n", a=1).broadcast_to([P, G * P])).then_inc(loc_in[s % 2], 16)
                                if not (it is 0 and s < 2):
                                    ps_, turn = back(it, s, 2, 4)
                                    spill(q - 2, ps_, turn)
                        quads(sp, body)
                        spill(NG - 2, 2, turns - 1)
                        spill(NG - 1, 3, turns - 1)
                        for s in range(4):
                            sp.wait_ge(spilled[s], 16 * turns)

                    @block.tensor
                    def _(pe):
                        def body(it):
                            for s in range(4):
                                q = 4 * it + s
                                pe.wait_ge(hot_ready, q + 1)
                                if not (it is 0 and s < 2):
                                    pe.wait_ge(z_ready, q - 1)
                                    pe.wait_ge(self_ready, q - 1)
                                for g, j in enumerate(tiles_at(pe, G * q, G, NT - 1)):
                                    for k in range(3):
                                        ins = pe.matmul(expd[s % 2][:, g, 0:RW], OHT[:, s % 2, g * P:(g + 1) * P],
                                                        PARTS[:, k, bass.ds(j, 1), :], start=(k == 0), stop=(k == 2))
                                ins.then_inc(exp_ready, 1)
                        quads(pe, body)

                    @block.vector
                    def _(dve):
                        Zv = Z.rearrange("p s (g w) -> p s g w", g=G)
                        Tv = T.rearrange("p s (g h c) -> p s g h c", g=G, h=H)

                        def hots(q, s2, turn2, first):
                            dve.wait_ge(loc_in[s2], 16 * (turn2 + 1))
                            if not first:
                                dve.wait_ge(exp_ready, q - 1)
                            dve.tensor_scalar(OHT[:, s2, :], LBC[:, s2, :], iota_p[:, 0:1], None, ALU.is_equal).then_inc(hot_ready, 1)

                        def add(q, s4, turn4, first):
                            dve.wait_ge(gathered[s4], 64 * (turn4 + 1))
                            dve.wait_ge(exp_ready, q + 1)
                            if not first:
                                dve.wait_ge(relu_ready, 2 * (q - 1))
                            dve.tensor_tensor(Zv[:, s4 % 2], expd[s4 % 2][:, :, 0:XW], GATH[:, s4, :, 0:XW], ALU.add).then_inc(z_ready, 1)

                        def score(q, s2):
                            dve.wait_ge(relu_ready, 2 * q + 2)
                            TR = Tv[:, s2, :, :, 0:C]
                            dve.tensor_tensor(TR, TR, VEC[:, 2, :].rearrange("p (h c) -> p h c", h=H).unsqueeze(1).broadcast_to([P, G, H, C]),
                                              ALU.mult).then_inc(weighted, 1)
                            dve.wait_ge(weighted, q + 1)
                            dve.tensor_reduce(SC[:, bass.ds(G * H * q, G * H)], T[:, s2, :].rearrange("p (g c) -> p g c", c=C + 1),
                                              AX, ALU.add).then_inc(scored, 1)

                        def body(it):
                            for s in range(4):
                                q = 4 * it + s
                                at0 = it is 0
                                hots(q, s % 2, 2 * it + s // 2, at0 and s < 2)
                                if not (at0 and s < 1):
                                    b, turn = back(it, s, 1, 4)
                                    add(q - 1, b, turn, at0 and s < 3)
                                if not (at0 and s < 2):
                                    score(q - 2, s % 2)
                        quads(dve, body)
                        add(NG - 1, 3, turns - 1, False)
                        score(NG - 2, 0)
                        score(NG - 1, 1)

                    @block.scalar
                    def _(act):
                        Zv = Z.rearrange("p s (g w) -> p s g w", g=G)
                        Tv = T.rearrange("p s (g h c) -> p s g h c", g=G, h=H)

                        def body(it, ahead=True):
                            for s in range(4):
                                q = 4 * it + s
                                act.wait_ge(z_ready, q + 1)
                                if not (it is 0 and s < 2):
                                    act.wait_ge(scored, q - 1)
                                act.activation(SELF[:, bass.ds(G * H * q, G * H)].rearrange("p (g h) -> p g h", g=G),
                                               expd[s % 2][:, :, XW:RW], ACT.Copy).then_inc(self_ready, 1)
                                act.activation(Tv[:, s % 2, :, :, 0:C], Zv[:, s % 2, :, 0:D].rearrange("p g (h c) -> p g h c", h=H),
                                               ACT.Relu).then_inc(relu_ready, 1)
                                act.activation(Tv[:, s % 2, :, :, C], Zv[:, s % 2, :, D:XW], ACT.Copy).then_inc(relu_ready, 1)
                                if ahead:
                                    act.wait_ge(gathered[s], 64 * (it + 1))
                                    act.wait_ge(spilled[s], 16 * (it + 1))
                                    act.activation(GIDX[:, s, :], SRCI[:, bass.ds(G * (q + 4), G)], ACT.Copy).then_inc(idx_ready, 1)
                        for s in range(4):
                            act.activation(GIDX[:, s, :], SRCI[:, G * s:G * (s + 1)], ACT.Copy).then_inc(idx_ready, 1)
                        body(0)
                        with act.Fori(1, turns - 1) as it:
                            body(it)
                        body(turns - 1, ahead=False)

            ctx, sem, ps = stage()
            with ctx:
                psum_f = [ps(f"f{k}", [P, 512]) for k in range(4)]
                BANKS = -(-RUN // 4)
                HALF = BANKS // 2 * 4
                W = NI * H
                SM = ctx.enter_context(nc.sbuf_tensor(f"summary{layer}", [P, 8], FP32))
                CR = ctx.enter_context(nc.sbuf_tensor(f"carries{layer}", [P, 2], FP32))
                KH = ctx.enter_context(nc.sbuf_tensor(f"by_head{layer}", [H, 10, CHUNKS], FP32))
                F2 = gath[:, 0:W]
                masked, to_rows, rows_ev, chain, summary, sum_in, carried, back_ready, to_cols, cols_ev, shifted = (
                    sem("masked"), sem("to_rows"), sem("rows_ev"), sem("chain"), sem("summary"), sem("sum_in"), sem("carried"),
                    sem("back_ready"), sem("to_cols"), sem("cols_ev"), sem("shifted"))
                carry_s, barred = sem("carry_s"), sem("barred")

                def krh(a):
                    return a.rearrange("p (k r h) -> p k r h", k=CHUNKS, r=RUN)

                def krh1(a):
                    return a.rearrange("p (k r) -> p k r", k=CHUNKS)

                def rkh(a):
                    return a.rearrange("p (r k h) -> p k r h", k=CHUNKS, r=RUN)

                with nc.Block() as block:

                    @block.vector
                    def _(dve):
                        link = Chain(dve, chain)
                        for r in (slice(0, HALF), slice(HALF, RUN)):
                            FWr = rkh(FW)[:, :, r]
                            link(dve.tensor_tensor(FWr, krh(SC)[:, :, r], krh(SELF)[:, :, r], ALU.max))
                            dve.tensor_tensor(FWr, FWr, krh1(MASK[:, :])[:, :, r].unsqueeze(3).broadcast_to([P, CHUNKS, FWr.shape[2], H]),
                                              ALU.add).then_inc(masked, 1)
                        dve.tensor_copy(SM[:, 4:5], RST[:, 0:1])
                        link(dve.tensor_reduce(SM[:, 1:2], RST[:, 0:W], AX, ALU.min))
                        link(dve.tensor_reduce(SM[:, 3:4], RST[:, 1:W], AX, ALU.min))
                        link(dve.memset(KH[:, :, :], -BIG))
                        dve.wait_ge(rows_ev, BANKS)
                        link(dve.tensor_tensor_scan(FW, RST[:, 0:W], D1, -BIG, ALU.add, ALU.max))
                        link(dve.tensor_copy(SM[:, 0:1], FW[:, W - 1:W]))
                        link(dve.tensor_tensor_scan(F2[:, ::-1], RST[:, 1:W + 1][:, ::-1], FW[:, ::-1], -BIG, ALU.add, ALU.max))
                        dve.tensor_copy(SM[:, 2:3], F2[:, 0:1]).then_inc(summary, 1)
                        dve.wait_ge(sum_in, 5 * 16)
                        last, low, first, low1, reset = [KH[:, k, :] for k in range(5)]
                        run, left, right, t0, t1 = [KH[:, k, :] for k in range(5, 10)]
                        K1 = CHUNKS - 1
                        link(dve.tensor_tensor_scan(run, low, last, -BIG, ALU.add, ALU.max))
                        link(dve.tensor_copy(left[:, 1:], run[:, 0:K1]))
                        link(dve.tensor_tensor(t0[:, 0:K1], low1[:, 0:K1], reset[:, 1:], ALU.add))
                        link(dve.tensor_tensor_scan(t1[:, ::-1], t0[:, ::-1], first[:, ::-1], -BIG, ALU.add, ALU.max))
                        link(dve.tensor_tensor(right[:, 0:K1], t1[:, 1:], reset[:, 1:], ALU.add))
                        dve.tensor_copy(t0, right).then_inc(carried, 1)
                        dve.wait_ge(back_ready, 2 * 16)
                        link(dve.tensor_tensor_scan(F2, RST[:, 0:W], D1, CR[:, 0:1], ALU.add, ALU.max))
                        dve.tensor_tensor_scan(D1[:, ::-1], RST[:, 1:W + 1][:, ::-1], F2[:, ::-1], CR[:, 1:2], ALU.add, ALU.max).then_inc(masked, 1)
                        dve.wait_ge(cols_ev, BANKS)
                        for k, arr in enumerate((SC, SELF)):
                            dve.wait_ge(barred, k + 1)
                            dve.tensor_tensor(krh(arr), krh(arr), rkh(FW), ALU.subtract).then_inc(shifted, 1)

                    @block.gpsimd
                    def _(pool):
                        pool.memset(ACC, 0.0)
                        pool.wait_ge(masked, 2)
                        for arr, add in ((SC, MASK), (SELF, START)):
                            arr3 = arr.rearrange("p (i h) -> p i h", h=H)
                            pool.tensor_tensor(arr3, arr3, add[:, :].unsqueeze(2).broadcast_to([P, NI, H]), ALU.add).then_inc(barred, 1)

                    @block.tensor
                    def _(pe):
                        for r in range(RUN):
                            b = r // 4
                            if r in (0, HALF):
                                pe.wait_ge(masked, 1 + (r > 0))
                            if b >= 4 and r % 4 == 0:
                                pe.wait_ge(rows_ev, b - 3)
                            ins = pe.transpose(psum_f[b % 4][:, (r % 4) * P:(r % 4 + 1) * P], FW[:, r * P:(r + 1) * P], ident[:, :])
                            if r % 4 == 3 or r == RUN - 1:
                                ins.then_inc(to_rows, 1)
                        pe.wait_ge(masked, 3)
                        pe.wait_ge(rows_ev, BANKS)
                        for r in range(RUN):
                            b = r // 4
                            if b >= 4 and r % 4 == 0:
                                pe.wait_ge(cols_ev, b - 3)
                            ins = pe.transpose(psum_f[b % 4][:, (r % 4) * P:(r % 4 + 1) * P], D1[:, r * P:(r + 1) * P], ident[:, :])
                            if r % 4 == 3 or r == RUN - 1:
                                ins.then_inc(to_cols, 1)

                    @block.scalar
                    def _(act):
                        for dst_buf, full, done in ((D1, to_rows, rows_ev), (FW, to_cols, cols_ev)):
                            for b in range(BANKS):
                                n = min(4, RUN - 4 * b) * P
                                act.wait_ge(full, b + 1)
                                act.activation(dst_buf[:, b * 4 * P:b * 4 * P + n], psum_f[b % 4][:, 0:n], ACT.Copy).then_inc(done, 1)
                        EXv = EX.rearrange("p (i w) -> p i w", w=2 * H)
                        act.wait_ge(shifted, 2)
                        for k, arr in enumerate((SC, SELF)):
                            act.activation(EXv[:, :, k * H:(k + 1) * H], arr.rearrange("p (i h) -> p i h", h=H), ACT.Exp)

                    @block.sync
                    def _(sp):
                        SLOW = dict(allow_slow_non_contiguous=True)
                        sp.wait_ge(summary, 1)
                        sp.dma_start(sum_d[:, :], SM[:, 0:5]).then_inc(carry_s, 16)
                        sp.wait_ge(carry_s, 16)
                        for k in range(5):
                            sp.dma_start(KH[:, k, :], sum_d[:, k].rearrange("(k h) -> h k", h=H), **SLOW).then_inc(sum_in, 16)
                        sp.wait_ge(carried, 1)
                        for k in range(2):
                            sp.dma_start(carry_d[k, :].rearrange("(k h) -> h k", h=H), KH[:, 6 + k, :], **SLOW).then_inc(carry_s, 16)
                        sp.wait_ge(carry_s, 48)
                        for k in range(2):
                            sp.dma_start(CR[:, k:k + 1], carry_d[k, :].rearrange("(p a) -> p a", a=1), **SLOW).then_inc(back_ready, 16)
                        sp.wait_ge(back_ready, 32)

            ctx, sem, ps = stage()
            with ctx:
                sums = [ps(f"sums{k}", [P, 512]) for k in range(4)]
                rows_in = [sem(f"rows_in{k}") for k in range(4)]
                LS = ctx.enter_context(nc.sbuf_tensor(f"dst_local{layer}", [P, 2, G], FP32))
                LD = ctx.enter_context(nc.sbuf_tensor(f"dst_visit{layer}", [P, 4, G], FP32))
                dst_ready = sem("dst_ready")
                loc_ready, hot_ready, sum_ready, added, weighted, appended = (
                    sem("loc_ready"), sem("hot_ready"), sem("sum_ready"), sem("added"), sem("weighted"), sem("appended"))
                turns = VD // 4
                PG = 2
                EXv = EX.rearrange("p (i w) -> p i w", w=2 * H)
                with nc.Block() as block:

                    def quads(eng, body):
                        body(0)
                        with eng.Fori(1, turns) as it:
                            body(it)

                    def visit(eng, v):
                        j = eng.value_load(JROW[0:1, bass.ds(NI + P + v, 1)], min_val=0, max_val=NJ)
                        return j, group_of(v - j, NG - 1)

                    def weigh(eng, s, g0, g1):
                        V = GATH[:, s, g0:g1, 0:D].rearrange("p g (h c) -> p g h c", h=H)
                        return eng.tensor_tensor(V, V, GATH[:, s, g0:g1, D:D + H].unsqueeze(3).broadcast_to([P, g1 - g0, H, C]), ALU.mult)

                    @block.sync
                    def _(sp):
                        def body(it):
                            for s in range(4):
                                v = 4 * it + s
                                j, q = visit(sp, v)
                                if it is not 0:
                                    sp.wait_ge(sum_ready, v - 3)
                                sp.dma_start(GATH[:, s].rearrange("p g w -> p (g w)"), spill_d[bass.ds(q, 1), :, :].rearrange("a p w -> (a p) w")).then_inc(rows_in[s], 16)
                        quads(sp, body)

                    @block.gpsimd
                    def _(pool):
                        def body(it):
                            for s in range(4):
                                pool.wait_ge(appended, 4 * it + s + 1)
                                weigh(pool, s, 0, PG).then_inc(weighted, 1)
                        quads(pool, body)

                    @block.scalar
                    def _(act):
                        def body(it):
                            for s in range(4):
                                v = 4 * it + s
                                j, q = visit(act, v)
                                if it is not 0:
                                    act.wait_ge(loc_ready, v - 3)
                                act.activation(LD[:, s, :], DSTM[:, bass.ds(G * q, G)], ACT.Copy).then_inc(dst_ready, 1)
                                act.wait_ge(rows_in[s], 16 * (it + 1))
                                act.activation(GATH[:, s, :, D:RW], EXv[:, bass.ds(G * q, G), :], ACT.Copy).then_inc(appended, 1)
                        quads(act, body)

                    @block.tensor
                    def _(pe):
                        def body(it):
                            for s in range(4):
                                v = 4 * it + s
                                pe.wait_ge(hot_ready, v + 1)
                                pe.wait_ge(weighted, v + 1)
                                pe.wait_ge(appended, v + 1)
                                if it is not 0:
                                    pe.wait_ge(added, v - 3)
                                for g in range(G):
                                    ins = pe.matmul(sums[s][:, 0:RW], OH[:, s % 2, g, :], GATH[:, s, g, :], start=(g == 0), stop=(g == G - 1))
                                ins.then_inc(sum_ready, 1)
                        quads(pe, body)

                    @block.vector
                    def _(dve):
                        def hots(v, s, it, first):
                            dve.wait_ge(dst_ready, v + 1)
                            if not first:
                                dve.wait_ge(sum_ready, v - 1)
                            dve.tensor_tensor(LS[:, s % 2, :], LD[:, s, :], FIRST[:, 1, bass.ds(v, 1)].broadcast_to([P, G]),
                                              ALU.subtract).then_inc(loc_ready, 1)
                            dve.wait_ge(appended, v + 1)
                            weigh(dve, s, PG, G)
                            dve.wait_ge(loc_ready, v + 1)
                            dve.tensor_tensor(OH[:, s % 2], iota_row[:, :].unsqueeze(1).broadcast_to([P, G, P]),
                                              LS[:, s % 2, :].unsqueeze(2).broadcast_to([P, G, P]), ALU.is_equal).then_inc(hot_ready, 1)

                        def add(v, s, first):
                            j = dve.value_load(JROW[0:1, bass.ds(NI + P + v, 1)], min_val=0, max_val=NJ)
                            dve.wait_ge(sum_ready, v + 1)
                            if not first:
                                dve.wait_ge(added, v)
                            dve.tensor_tensor(ACC[:, bass.ds(j, 1), :], ACC[:, bass.ds(j, 1), :], sums[s][:, 0:RW].unsqueeze(1), ALU.add).then_inc(added, 1)

                        def body(it):
                            for s in range(4):
                                v = 4 * it + s
                                hots(v, s, it, it is 0 and s < 2)
                                if not (it is 0 and s < 2):
                                    add(v - 2, (s - 2) % 4, it is 0 and s < 3)
                        quads(dve, body)
                        for v in (VD - 2, VD - 1):
                            add(v, v % 4, False)

            ctx, sem, ps = stage()
            with ctx:
                XL = EX[:, 0:NT * D].rearrange("p (t d) -> p t d", d=D)
                x1_in = sem("x1_in")
                SW = work[:, 0:NT * H].rearrange("p (t h) -> p t h", h=H)
                DN = work[:, NT * H:2 * NT * H].rearrange("p (t h) -> p t h", h=H)
                rows_in = [sem(f"rows_in{k}") for k in range(PIECES)]
                chain, own_ready, gelu_in, gelu_ready = sem("chain"), sem("own_ready"), sem("gelu_in"), sem("gelu_ready")

                def by_head(a):
                    return a.unsqueeze(3).broadcast_to([P, NT // PIECES, H, C])

                def split(a):
                    return a.rearrange("p t (h c) -> p t h c", h=H)

                with nc.Block() as block:

                    @block.sync
                    def _(sp):
                        for k in range(PIECES):
                            sp.dma_start(XL[:, piece(k)], tab_d[:, 0:D].rearrange("(t p) d -> p t d", p=P)[:, piece(k)]).then_inc(rows_in[k], 16)
                        if layer == len(gat) - 1:
                            sp.dma_start(X1, x1_d[:, :].rearrange("(t p) d -> p t d", p=P)).then_inc(x1_in, 16)
                            sp.wait_ge(x1_in, 16)

                    @block.gpsimd
                    def _(pool):
                        pool.wait_ge(chain, 2)
                        for k in range(PIECES):
                            pool.wait_ge(rows_in[k], 16)
                            pool.tensor_tensor(split(XL[:, piece(k)]), split(XL[:, piece(k)]), by_head(SW[:, piece(k)]), ALU.mult).then_inc(own_ready, 1)
                        for k in range(PIECES):
                            pool.wait_ge(gelu_ready, k + 1)
                            pool.tensor_tensor(Xv[:, piece(k)], Xv[:, piece(k)], XL[:, piece(k)], ALU.add)

                    @block.vector
                    def _(dve):
                        link = Chain(dve, chain)
                        link(dve.tensor_scalar(DN, ACC[:, :, D:D + H], 0.0, None, ALU.is_equal))
                        link(dve.tensor_tensor(SW, ACC[:, :, D + H:RW], DN, ALU.max))
                        link(dve.tensor_tensor(DN, ACC[:, :, D:D + H], SW, ALU.add))
                        link(dve.tensor_scalar(DN, DN, 1e-16, None, ALU.max))
                        link(dve.reciprocal(DN, DN))

                        for k in range(PIECES):
                            Y = XL[:, piece(k)]
                            dve.wait_ge(own_ready, k + 1)
                            link(dve.tensor_tensor(Y, Y, ACC[:, piece(k), 0:D], ALU.add))
                            link(dve.tensor_tensor(split(Y), split(Y), by_head(DN[:, piece(k)]), ALU.mult))
                            dve.tensor_tensor(Y, Y, VEC[:, 0, :].unsqueeze(1).broadcast_to([P, NT // PIECES, D]), ALU.add).then_inc(gelu_in, 1)

                    @block.scalar
                    def _(act):
                        for k in range(PIECES):
                            act.wait_ge(gelu_in, k + 1)
                            act.activation(XL[:, piece(k)], XL[:, piece(k)], ACT.Gelu).then_inc(gelu_ready, 1)

        ctx, sem, ps = stage()
        with ctx:
            summed, chain, moments, rooted, normed, stored = (sem("summed"), sem("chain"), sem("moments"), sem("rooted"), sem("normed"), sem("stored"))
            with nc.Block() as block:

                @block.sync
                def _(sp):
                    for k in range(PIECES):
                        sp.wait_ge(normed, k + 1)
                        t0, t1 = k * (NT // PIECES), min((k + 1) * (NT // PIECES), NT - 1)
                        sp.dma_start(out[t0 * P:t1 * P, :].rearrange("(t p) d -> p t d", p=P), Xv[:, t0:t1, :]).then_inc(stored, 16)
                    sp.dma_start(out[(NT - 1) * P:N, :], Xv[0:TAIL, NT - 1, :]).then_inc(stored, 16)
                    sp.wait_ge(stored, 16 * (PIECES + 1))

                @block.vector
                def _(dve):
                    layernorm(dve, moments, rooted, chain, 0, normed, summed)

                @block.gpsimd
                def _(pool):
                    for k in range(PIECES):
                        pool.tensor_tensor(Xv[:, piece(k)], Xv[:, piece(k)], X1[:, piece(k)], ALU.add).then_inc(summed, 1)

                @block.scalar
                def _(act):
                    act.wait_ge(moments, 1)
                    act.activation(RSTD[:, :, 0], MOM[:, :, 1], ACT.Sqrt).then_inc(rooted, 1)


_INS = ['x', 'src', 'dst', 'edge_weight', 'L0_gnn_W', 'L0_gnn_b', 'L1_gnn_Wl0', 'L1_gnn_Wr0', 'L1_gnn_att0', 'L1_gnn_b0',
        'L1_gnn_Wl1', 'L1_gnn_Wr1', 'L1_gnn_att1', 'L1_gnn_b1']


def kernel(**inputs):
    import numpy as np
    import concourse.bacc as bacc
    from concourse.bass_utils import run_bass_kernel_spmd as run

    nc = bacc.Bacc("TRN2", target_bir_lowering=False, num_devices=1)
    arrays, ins = {}, []
    for name in _INS:
        a = np.ascontiguousarray(inputs[name])
        arrays[f"in_{name}"] = a
        ins.append(nc.dram_tensor(f"in_{name}", a.shape, mybir.dt.from_np(a.dtype), kind="ExternalInput").ap())
    out = nc.dram_tensor("out_0", (N, D), FP32, kind="ExternalOutput").ap()
    gat = [ins[6:10], ins[10:14]]
    build(nc, *ins[:6], gat, out)
    r = run(nc, [arrays], core_ids=[0])
    return r.results[0]["out_0"]
```
